# Optimizing a Trainium2 kernel written in Bass

```python
import numpy as np
import jax
import jax.numpy as jnp

def _softmax(x, axis=-1):
    return jax.nn.softmax(x, axis=axis)

def _gelu(x):
    return jax.nn.gelu(x, approximate=True)

def _silu(x):
    return jax.nn.silu(x)

def _sigmoid(x):
    return jax.nn.sigmoid(x)

def _layernorm(x, axis=-1, eps=1e-05):
    m = jnp.mean(x, axis=axis, keepdims=True)
    v = jnp.var(x, axis=axis, keepdims=True)
    return (x - m) / jnp.sqrt(v + eps)

def _scatter_add(tgt, idx, src, axis=0):
    return tgt.at[idx].add(src)

def _segment_sum(src, seg, n):
    return jax.ops.segment_sum(src, seg, n)
kernel_name = 'mk_vit_tower_cls_d2_tok_img768_r4_e649c5'

def setup_inputs(seed: int=0):
    np.random.seed(seed)
    _w = jnp.asarray

    def _rec_inputs():
        import jax
        import jax.numpy as jnp
        _rk = jax.random.key(seed)
        x = 7.57192e-06 + 1.00007 * jax.random.normal(jax.random.fold_in(_rk, 1), (2, 3, 128, 128), jnp.float32)
        cls_tok = 0.02 * jax.random.normal(jax.random.fold_in(_rk, 5), (1, 1, 192), jnp.float32)
        return (x, cls_tok)
    x, cls_tok = _rec_inputs()

    def _L0_tok_setup():
        import jax, jax.numpy as jnp
        import numpy as np
        QMAX = 127.0

        def fake_quant(v):
            s = jnp.maximum(jnp.max(jnp.abs(v)), 1e-08) / QMAX
            return jnp.round(jnp.clip(v / s, -QMAX, QMAX)) * s
        key = jax.random.key(seed)
        k1, k2, k3 = jax.random.split(key, 3)
        B, C, H, W = (64, 3, 224, 224)
        D, P = (192, 8)
        x = jax.random.normal(k1, (B, C, H, W), dtype=jnp.float32)
        w = jax.random.normal(k2, (D, C, P, P), dtype=jnp.float32) * 0.02
        b = jax.random.normal(k3, (D,), dtype=jnp.float32) * 0.02
        return {'x': x, 'w': w, 'b': b}
    _L0_tok_all = _L0_tok_setup()
    _L0_tok_in = {k: v for k, v in _L0_tok_all.items() if k in ('w', 'b')}
    del _L0_tok_all

    def _L0_attn_setup():
        import jax, jax.numpy as jnp
        import numpy as np
        B, N, DIM = (16, 577, 192)
        HEADS, DIM_HEAD = (12, 64)
        INNER = HEADS * DIM_HEAD
        key = jax.random.key(seed)
        k1, k2, k3, k4 = jax.random.split(key, 4)
        x = jax.random.normal(k1, (B, N, DIM), dtype=jnp.float32)
        w_qkv = jax.random.normal(k2, (DIM, 3 * INNER), dtype=jnp.float32) * 0.02
        scale = jnp.full((HEADS,), DIM_HEAD ** (-0.5), dtype=jnp.float32)
        w_out = jax.random.normal(k3, (INNER, DIM), dtype=jnp.float32) * 0.02
        b_out = jnp.zeros((DIM,), dtype=jnp.float32)
        return {'x': x, 'w_qkv': w_qkv, 'scale': scale, 'w_out': w_out, 'b_out': b_out}
    _L0_attn_all = _L0_attn_setup()
    _L0_attn_in = {k: v for k, v in _L0_attn_all.items() if k in ('w_qkv', 'scale', 'w_out', 'b_out')}
    del _L0_attn_all

    def _L0_ffn_setup():
        import jax, jax.numpy as jnp
        import numpy as np
        D_MODEL = 192
        N_EXPERTS = 16
        TOP_K = 2
        D_FF = 4 * D_MODEL
        B, L = (4, 512)
        key = jax.random.key(seed)
        ks = jax.random.split(key, 6)
        s_in = 1.0 / np.sqrt(D_MODEL)
        s_ff = 1.0 / np.sqrt(D_FF)
        x = jax.random.normal(ks[0], (B, L, D_MODEL), dtype=jnp.float32)
        Wr = jax.random.uniform(ks[1], (N_EXPERTS, D_MODEL), jnp.float32, -s_in, s_in)
        W1 = jax.random.uniform(ks[2], (N_EXPERTS, D_MODEL, D_FF), jnp.float32, -s_in, s_in)
        b1 = jax.random.uniform(ks[3], (N_EXPERTS, D_FF), jnp.float32, -s_in, s_in)
        W2 = jax.random.uniform(ks[4], (N_EXPERTS, D_FF, D_MODEL), jnp.float32, -s_ff, s_ff)
        b2 = jax.random.uniform(ks[5], (N_EXPERTS, D_MODEL), jnp.float32, -s_ff, s_ff)
        return {'x': x, 'Wr': Wr, 'W1': W1, 'b1': b1, 'W2': W2, 'b2': b2}
    _L0_ffn_all = _L0_ffn_setup()
    _L0_ffn_in = {k: v for k, v in _L0_ffn_all.items() if k in ('Wr', 'W1', 'b1', 'W2', 'b2')}
    del _L0_ffn_all

    def _L1_attn_setup():
        import jax, jax.numpy as jnp
        import numpy as np
        DIM = 192
        NUM_HEADS = 12
        HEAD_DIM = DIM // NUM_HEADS
        SCALE = HEAD_DIM ** (-0.5)
        key = jax.random.key(seed)
        k_x, k_qkv, k_proj, k_pb = jax.random.split(key, 4)
        B, N, C = (16, 256, DIM)
        x = jax.random.normal(k_x, (B, N, C), dtype=jnp.float32)
        w_qkv = jax.random.normal(k_qkv, (3 * C, C), dtype=jnp.float32) * C ** (-0.5)
        w_proj = jax.random.normal(k_proj, (C, C), dtype=jnp.float32) * C ** (-0.5)
        b_proj = jax.random.normal(k_pb, (C,), dtype=jnp.float32) * 0.01
        return {'x': x, 'w_qkv': w_qkv, 'w_proj': w_proj, 'b_proj': b_proj}
    _L1_attn_all = _L1_attn_setup()
    _L1_attn_in = {k: v for k, v in _L1_attn_all.items() if k in ('w_qkv', 'w_proj', 'b_proj')}
    del _L1_attn_all

    def _L1_ffn_setup():
        import jax, jax.numpy as jnp
        import numpy as np
        EPS_NORM = 1e-05
        RMS_EPS = 1e-05

        def _l2_normalize(v):
            n = jnp.sqrt(jnp.sum(v * v, axis=-1, keepdims=True))
            return v / jnp.maximum(n, EPS_NORM)

        def _rms_norm(x, weight, eps):
            ms = jnp.mean(x * x, axis=-1, keepdims=True)
            return x * jax.lax.rsqrt(ms + eps) * weight
        key = jax.random.key(seed)
        ks = jax.random.split(key, 6)
        B, T, D = (8, 1024, 192)
        S, F = (64, 768)
        x = jax.random.normal(ks[0], (B, T, D), dtype=jnp.float32)
        slots = 0.02 * jax.random.normal(ks[1], (S, D), dtype=jnp.float32)
        scale = jnp.ones((S,), dtype=jnp.float32)
        fc1_weight = 0.02 * jax.random.normal(ks[2], (S, D, F), dtype=jnp.float32)
        fc1_bias = jnp.zeros((S, F), dtype=jnp.float32)
        fc2_weight = 0.02 * jax.random.normal(ks[3], (S, F, D), dtype=jnp.float32)
        fc2_bias = jnp.zeros((S, D), dtype=jnp.float32)
        norm_weight = jnp.ones((D,), dtype=jnp.float32)
        return {'x': x, 'slots': slots, 'scale': scale, 'fc1_weight': fc1_weight, 'fc1_bias': fc1_bias, 'fc2_weight': fc2_weight, 'fc2_bias': fc2_bias, 'norm_weight': norm_weight}
    _L1_ffn_all = _L1_ffn_setup()
    _L1_ffn_in = {k: v for k, v in _L1_ffn_all.items() if k in ('slots', 'scale', 'fc1_weight', 'fc1_bias', 'fc2_weight', 'fc2_bias', 'norm_weight')}
    del _L1_ffn_all
    return {'x': x, 'cls_tok': cls_tok, 'L0_tok_w': _L0_tok_in['w'], 'L0_tok_b': _L0_tok_in['b'], 'L0_attn_w_qkv': _L0_attn_in['w_qkv'], 'L0_attn_scale': _L0_attn_in['scale'], 'L0_attn_w_out': _L0_attn_in['w_out'], 'L0_attn_b_out': _L0_attn_in['b_out'], 'L0_ffn_Wr': _L0_ffn_in['Wr'], 'L0_ffn_W1': _L0_ffn_in['W1'], 'L0_ffn_b1': _L0_ffn_in['b1'], 'L0_ffn_W2': _L0_ffn_in['W2'], 'L0_ffn_b2': _L0_ffn_in['b2'], 'L1_attn_w_qkv': _L1_attn_in['w_qkv'], 'L1_attn_w_proj': _L1_attn_in['w_proj'], 'L1_attn_b_proj': _L1_attn_in['b_proj'], 'L1_ffn_slots': _L1_ffn_in['slots'], 'L1_ffn_scale': _L1_ffn_in['scale'], 'L1_ffn_fc1_weight': _L1_ffn_in['fc1_weight'], 'L1_ffn_fc1_bias': _L1_ffn_in['fc1_bias'], 'L1_ffn_fc2_weight': _L1_ffn_in['fc2_weight'], 'L1_ffn_fc2_bias': _L1_ffn_in['fc2_bias'], 'L1_ffn_norm_weight': _L1_ffn_in['norm_weight']}

def reference(x, cls_tok, L0_tok_w, L0_tok_b, L0_attn_w_qkv, L0_attn_scale, L0_attn_w_out, L0_attn_b_out, L0_ffn_Wr, L0_ffn_W1, L0_ffn_b1, L0_ffn_W2, L0_ffn_b2, L1_attn_w_qkv, L1_attn_w_proj, L1_attn_b_proj, L1_ffn_slots, L1_ffn_scale, L1_ffn_fc1_weight, L1_ffn_fc1_bias, L1_ffn_fc2_weight, L1_ffn_fc2_bias, L1_ffn_norm_weight):
    import jax
    import jax.numpy as jnp

    def _L0_tok_ref(x, w, b):
        import jax, jax.numpy as jnp
        import numpy as np
        QMAX = 127.0

        def fake_quant(v):
            s = jnp.maximum(jnp.max(jnp.abs(v)), 1e-08) / QMAX
            return jnp.round(jnp.clip(v / s, -QMAX, QMAX)) * s
        B, C, H, W = x.shape
        D, _, P, _ = w.shape
        gh, gw = (H // P, W // P)
        xq = fake_quant(x)
        wq = fake_quant(w)
        xp = xq.reshape(B, C, gh, P, gw, P)
        out = jnp.einsum('bchpwq,dchq->bhwd', xp.transpose(0, 1, 2, 3, 4, 5), wq, optimize=True) if False else jnp.einsum('bcxpyq,dcpq->bxyd', xp, wq)
        out = out + b
        out = out.reshape(B, gh * gw, D)
        return out

    def _L0_attn_ref(x, w_qkv, scale, w_out, b_out):
        import jax, jax.numpy as jnp
        import numpy as np
        B, N, DIM = (16, 577, 192)
        HEADS, DIM_HEAD = (12, 64)
        INNER = HEADS * DIM_HEAD
        b, n, _ = x.shape
        h = scale.shape[0]
        dh = w_qkv.shape[1] // (3 * h)
        qkv = x @ w_qkv
        q, k, v = jnp.split(qkv, 3, axis=-1)
        to_heads = lambda t: t.reshape(b, n, h, dh).transpose(0, 2, 1, 3)
        q, k, v = (to_heads(q), to_heads(k), to_heads(v))
        dots = jnp.einsum('bhid,bhjd->bhij', q, k) * scale[None, :, None, None]
        se = dots.mean(axis=1, keepdims=True)
        diag = jnp.eye(n, dtype=bool)
        neg_inf = jnp.array(-jnp.inf, dots.dtype)
        dots = jnp.where(diag, neg_inf, dots)
        top_k = int(n * 0.75)
        _, idx = jax.lax.top_k(dots, top_k)
        bi = jnp.arange(b)[:, None, None, None]
        hi = jnp.arange(h)[None, :, None, None]
        ii = jnp.arange(n)[None, None, :, None]
        keep = jnp.zeros((b, h, n, n), dtype=bool).at[bi, hi, ii, idx].set(True)
        dots = jnp.where(keep, dots, neg_inf) + se
        attn = jax.nn.softmax(dots, axis=-1)
        out = jnp.einsum('bhij,bhjd->bhid', attn, v)
        out = out.transpose(0, 2, 1, 3).reshape(b, n, h * dh)
        return out @ w_out + b_out

    def _L0_ffn_ref(x, Wr, W1, b1, W2, b2):
        import jax, jax.numpy as jnp
        import numpy as np
        D_MODEL = 192
        N_EXPERTS = 16
        TOP_K = 2
        D_FF = 4 * D_MODEL
        B, L = (4, 512)
        logits = jnp.einsum('bld,ed->ble', x, Wr)
        probs = jax.nn.softmax(logits, axis=-1)
        top_p, top_idx = jax.lax.top_k(probs, TOP_K)
        gating = jnp.sum(jax.nn.one_hot(top_idx, N_EXPERTS, dtype=probs.dtype) * top_p[..., None], axis=-2)
        gate_e = jnp.moveaxis(gating, -1, 0)

        def step(y, params):
            W1e, b1e, W2e, b2e, ge = params
            h = jax.nn.gelu(jnp.einsum('bld,df->blf', x, W1e) + b1e, approximate=False)
            out = jnp.einsum('blf,fd->bld', h, W2e) + b2e
            return (y + ge[..., None] * out, None)
        y0 = jnp.zeros_like(x)
        y, _ = jax.lax.scan(step, y0, (W1, b1, W2, b2, gate_e))
        return x + y

    def _L1_attn_ref(x, w_qkv, w_proj, b_proj):
        import jax, jax.numpy as jnp
        import numpy as np
        DIM = 192
        NUM_HEADS = 12
        HEAD_DIM = DIM // NUM_HEADS
        SCALE = HEAD_DIM ** (-0.5)
        B, N, C = x.shape
        H, D = (NUM_HEADS, HEAD_DIM)
        qkv = jnp.einsum('bnc,ec->bne', x, w_qkv)
        qkv = qkv.reshape(B, N, 3, H, D).transpose(2, 0, 3, 1, 4)
        q, k, v = (qkv[0], qkv[1], qkv[2])
        attn = jnp.einsum('bhqd,bhkd->bhqk', q, k) * SCALE
        attn = jax.nn.softmax(attn, axis=-1)
        out = jnp.einsum('bhqk,bhkd->bhqd', attn, v)
        out = out.transpose(0, 2, 1, 3).reshape(B, N, C)
        out = jnp.einsum('bnc,oc->bno', out, w_proj) + b_proj
        return out

    def _L1_ffn_ref(x, slots, scale, fc1_weight, fc1_bias, fc2_weight, fc2_bias, norm_weight):
        import jax, jax.numpy as jnp
        import numpy as np
        EPS_NORM = 1e-05
        RMS_EPS = 1e-05

        def _l2_normalize(v):
            n = jnp.sqrt(jnp.sum(v * v, axis=-1, keepdims=True))
            return v / jnp.maximum(n, EPS_NORM)

        def _rms_norm(x, weight, eps):
            ms = jnp.mean(x * x, axis=-1, keepdims=True)
            return x * jax.lax.rsqrt(ms + eps) * weight
        xn = _rms_norm(x, norm_weight, RMS_EPS)
        tok = _l2_normalize(xn)
        sl = _l2_normalize(slots) * scale[:, None]
        logits = jnp.einsum('sd,btd->bst', sl, tok)
        dispatch_w = jax.nn.softmax(logits, axis=-1)
        combine_w = jax.nn.softmax(logits, axis=-2)
        y = jnp.einsum('btd,bst->bsd', xn, dispatch_w)
        y = jnp.einsum('sio,bsi->bso', fc1_weight, y) + fc1_bias
        y = jax.nn.gelu(y, approximate=False)
        y = jnp.einsum('sio,bsi->bso', fc2_weight, y) + fc2_bias
        out = jnp.einsum('bsd,bst->btd', y, combine_w)
        return out
    h = _L0_tok_ref(x, L0_tok_w, L0_tok_b)
    h = jnp.concatenate([jnp.broadcast_to(cls_tok, (h.shape[0], 1, h.shape[2])), h], axis=1)
    h = h + _L0_attn_ref(_layernorm(h, axis=-1), L0_attn_w_qkv, L0_attn_scale, L0_attn_w_out, L0_attn_b_out)
    h = h + _L0_ffn_ref(_layernorm(h, axis=-1), L0_ffn_Wr, L0_ffn_W1, L0_ffn_b1, L0_ffn_W2, L0_ffn_b2)
    h = h + _L1_attn_ref(_layernorm(h, axis=-1), L1_attn_w_qkv, L1_attn_w_proj, L1_attn_b_proj)
    h = h + _L1_ffn_ref(_layernorm(h, axis=-1), L1_ffn_slots, L1_ffn_scale, L1_ffn_fc1_weight, L1_ffn_fc1_bias, L1_ffn_fc2_weight, L1_ffn_fc2_bias, L1_ffn_norm_weight)
    return h

_drawn_inputs = setup_inputs


def setup_inputs(seed=0):
    import zlib

    import numpy as np

    out = dict(_drawn_inputs(seed))
    spreads = {'L0_attn_scale': (0.125, 0.6),
     'L0_attn_b_out': (0.0, 0.1),
     'L1_ffn_scale': (1.0, 0.6),
     'L1_ffn_fc1_bias': (0.0, 0.8),
     'L1_ffn_fc2_bias': (0.0, 0.8),
     'L1_ffn_norm_weight': (1.0, 0.6)}
    factors = {'cls_tok': 4.485,
     'L0_ffn_b1': 26.147,
     'L0_ffn_b2': 8.0,
     'L1_attn_b_proj': 8.0,
     'L1_ffn_slots': 8.0,
     'L1_ffn_fc1_weight': 8.0,
     'L1_ffn_fc2_weight': 8.0}
    for name, (base, spread) in spreads.items():
        noise = np.random.default_rng([zlib.crc32(name.encode()), seed]).standard_normal(out[name].shape)
        drawn = base * np.exp(spread * noise) if base else spread * noise
        out[name] = jnp.asarray(drawn.astype(out[name].dtype))
    for name, factor in factors.items():
        out[name] = (out[name] * factor).astype(out[name].dtype)
    return out
```

```python
import concourse.bass as bass
from concourse import mybir
from contextlib import ExitStack
import numpy as np

F32 = mybir.dt.float32
BF16 = mybir.dt.bfloat16
U32 = mybir.dt.uint32
ALU = mybir.AluOpType
ACT = mybir.ActivationFunctionType
AX = mybir.AxisListType
RMAX = bass.bass_isa.ReduceOp.max
ds = bass.ds

P = 128
B = 2
GRID = 16
NP = GRID * GRID
NT = NP + 1
D = 192
KP = 96
KD = D // KP
H = 12
HD0, HD1 = 64, 16
IN0 = H * HD0
C0 = IN0 // P
HPC = KP // HD1
NR = B * H
DROP = NT - int(NT * 0.75) - 1
ROUNDS = DROP // 8
E, FF = 16, 768
MF = FF // P
S = 64
PAIRS = S // 2
TILES = 5
BIG = 2.0 ** 126
THR = 1e30
MAGIC = 12582912.0
QMAX = 127.0
EPS = 1e-5
RING = 8
SLOT = 3 * FF

CST = {}
_at = 0
for _name, _w in (("ident", P), ("mq0", C0 * B * H * B), ("mo0", C0 * H), ("mz1", HPC), ("mq1", KD * B * NR),
                  ("mo1", KD * H), ("nb", NR), ("iota", E), ("eye2", B)):
    CST[_name] = (_at, _at + _w)
    _at += _w
CST_W = _at
CSTB = {"identb": (0, P), "bigd": (P, P + NP + P + 1), "bigc": (2 * P + NP + 1, 2 * P + NP + 1 + NT)}
CSTB_W = 2 * P + NP + 1 + NT


def rows(t):
    return P if t < TILES - 1 else B


def cols(t):
    if t == TILES - 1:
        return slice(NP, B * NT, NT)
    a = (t // 2) * NT + (t % 2) * P
    return slice(a, a + P)


def vit_tower(nc, a):
    out = a["out"]
    with ExitStack() as ctx:
        def sb(name, shape, dt=F32):
            return ctx.enter_context(nc.sbuf_tensor(name, shape, dt))

        def sem(name):
            return ctx.enter_context(nc.semaphore(name))

        cst = sb("cst", [P, CST_W])
        cstb = sb("cstb", [P, CSTB_W], BF16)

        def const(name, p=P):
            lo, hi = CST[name]
            return cst[0:p, lo:hi]

        ident = const("ident")
        identb = cstb[:, 0:P]
        bigd = cstb[:, CSTB["bigd"][0]:CSTB["bigd"][1]]
        bigc = cstb[0:NR, CSTB["bigc"][0]:CSTB["bigc"][1]]

        h = sb("h", [P, TILES, D])
        hb = sb("hb", [P, TILES, D])
        xn = sb("xn", [P, TILES, D])
        xT = sb("xT", [KP, KD, B * NT])
        rowsb = sb("rowsb", [P, 4, D])
        stats = sb("stats", [P, TILES, 6])
        mv = sb("mv", [P, TILES, 2])
        sm = sb("sm", [P, 16, TILES])
        NEGB = RING * SLOT
        arena = sb("arena", [P, NEGB])

        class Cut:
            at = 0

        def take(p, *shape):
            n = 1
            for s_ in shape:
                n *= s_
            v = arena[0:p, Cut.at:Cut.at + n]
            Cut.at += n
            assert Cut.at <= NEGB
            if len(shape) == 1:
                return v
            names = "abc"[:len(shape)]
            return v.rearrange("p (%s) -> p %s" % (" ".join(names), " ".join(names)),
                               **{k: s_ for k, s_ in zip(names, shape)})

        wq0 = sb("wq0", [KP, KD, 3 * IN0])
        kT0 = take(P, C0, B * NT)
        qz0 = take(P, H, P)
        qf0 = take(P, C0, P)
        W = take(P, NT)
        X = take(P, 2, NT)
        PR = take(P, 2, NT)
        PT = take(P, 2, P)
        PTr = take(1, P)
        O0 = take(P, IN0)
        seb = take(P, NT)
        negC = take(NR, NT)
        Oc = take(P, B * C0, H)
        L = sb("L", [P, H, NT])
        neg = sb("neg", [P, H, NT])
        OT0 = sb("OT0", [P, C0, B * NT])
        v0 = sb("v0", [P, 4, IN0])
        vc0 = sb("vc0", [1, B, IN0])
        wo0 = sb("wo0", [P, C0, D])
        QM0 = sb("QM0", [P, C0, B * NR])
        PCT = sb("PCT", [P, 2, NR])
        PCr = sb("PCr", [1, NR])
        m8 = sb("m8", [P, 8])
        tick = sb("tick", [P, 8])
        nmx = sb("nmx", [P, 2])
        rs = sb("rs", [P, H])
        rr = sb("rr", [P, H])
        scb = sb("scb", [KP, H])
        junk = sb("junk", [S, D])

        wr = sb("wr", [KP, KD, E])
        lg = sb("lg", [P, TILES, E])
        gate = sb("gate", [P, TILES, E])
        gate2 = sb("gate2", [P, TILES, E])
        top = sb("top", [P, TILES, 8])
        topi = sb("topi", [P, TILES, 8], U32)
        topf = sb("topf", [P, TILES, 8])
        gT = sb("gT", [E, TILES, P])
        b2e = sb("b2e", [E, D])
        b1e = sb("b1e", [P, MF, E])
        b1c = sb("b1c", [P, 2, MF])
        gcol = sb("gcol", [P, 2, TILES])
        w1e = [v0[0:KP, :, :].rearrange("p a b -> p (a b)")[:, n * KD * FF:(n + 1) * KD * FF].rearrange(
            "p (k f) -> p k f", k=KD) for n in range(2)]
        w2e = [sb(f"w2e{n}", [P, MF, D]) for n in range(2)]
        hT = OT0

        wq0f = wq0[:, :, :].rearrange("p a b -> p (a b)")
        wq1 = wq0f[:, 0:KD * 3 * D].rearrange("p (k n) -> p k n", k=KD)
        wp1 = wq0f[:, 1152:1152 + KD * D].rearrange("p (k n) -> p k n", k=KD)
        kT1 = wq0f[:, 1536:1536 + KD * B * NT].rearrange("p (k n) -> p k n", k=KD)
        OT1 = wq0f[:, 2564:2564 + KD * B * NT].rearrange("p (k n) -> p k n", k=KD)
        v1 = sb("v1", [P, 4, D])
        vc1 = sb("vc1", [1, B, D])
        QM1 = sb("QM1", [KP, KD, B * NR])
        qz1 = L[0:KP, :, 0:P]
        PR1 = neg[:, 0:2, :]
        PT1 = neg[:, 2:4, 0:2 * P].rearrange("p a (k n) -> p a k n", k=2)
        PTr1 = neg[0:1, 4:6, 0:P]
        O1 = neg[:, 6, 0:D]
        Oc1 = neg[0:KP, 7, 0:B * KD * H]
        PC1 = neg[0:NR, 8, :]

        def carve(buf):
            flat, at = buf[:, :, :].rearrange("p a b -> p (a b)"), [0]

            def cut(p, *shape):
                n = int(np.prod(shape))
                v = flat[0:p, at[0]:at[0] + n]
                at[0] += n
                assert at[0] <= flat.shape[1]
                names = "abc"[:len(shape)]
                if len(shape) == 1:
                    return v
                return v.rearrange("p (%s) -> p %s" % (" ".join(names), " ".join(names)), **dict(zip(names, shape)))
            return cut

        cut = carve(neg)
        xr = cut(P, TILES, D)
        YM = cut(P, PAIRS, 3, 4)
        DT = cut(P, 4, S)
        DTc = cut(B, B, S)
        Dm = cut(S, B, NT)
        cut = carve(L)
        hs = cut(P, MF, B * S)
        y2T = cut(KP, KD, B * S)
        y2 = cut(S, B, D)
        lgc = cut(P, TILES, S)
        CT = cut(S, 4, P)
        CTc = cut(S, B, B)
        slT = cut(KP, KD, S)
        cut = carve(OT0)
        slots = cut(S, D)
        slscale = cut(S, 1)
        b1T = cut(P, MF, S)
        b2T = cut(KP, KD, S)

        s_cst = sem("constants_landed")
        s_x = sem("patches_landed")
        s_wq0 = sem("attn0_weights_landed")
        s_wo0 = sem("attn0_out_weights_landed")
        s_hz = sem("residual_cleared")
        s_cls = sem("class_rows_landed")
        s_dve = sem("vector_chain")
        s_pool = sem("pool_chain")
        s_amax = sem("absmax_of_partitions")
        s_gmax = sem("absmax_of_all")
        s_xq = sem("quantized")
        s_tokps = sem("tokens_in_psum")
        s_var = sem("variances_ready")
        s_std = sem("deviations_ready")
        s_xn = sem("normalised_tiles")
        s_xtps = sem("transposed_tiles_in_psum")
        s_xt = sem("transposed_tiles")
        s_out = sem("stored")
        s_final = sem("result_ready")
        s_amz = sem("absmax_cleared")
        s_qzz = sem("spread_queries_cleared")

        xp = wq0[:, 0, 0:KD * B * NP].rearrange("p (k n) -> p k n", k=KD)
        wt = wq0[:, 1, 0:KD * D].rearrange("p (k n) -> p k n", k=KD)
        xqb = OT0[0:KP, 0:2, 0:NP].bitcast(BF16)
        wqb = OT0[0:KP, 2:4, 0:D // 2].bitcast(BF16)
        am = sb("am", [P, 2])
        gm = sb("gm", [P, 8])

        bank = ctx.enter_context(nc.psum_tensor("bank", [P, 8, 512], F32))

        block = ctx.enter_context(nc.Block())

        s_kps, s_kev = sem("keys0_in_psum"), sem("keys0_ready")
        s_vps, s_vev = sem("values0_in_psum"), sem("values0_ready")
        s_wqs = sem("query_weights_scaled")
        s_qcps, s_qm = sem("class_queries_in_psum"), sem("class_queries_spread")
        s_ncps, s_nc = sem("class_scores_in_psum"), sem("class_scores_ready")
        s_lc = sem("class_logits_in_psum")
        s_xc, s_pc, s_pcn = sem("class_masked"), sem("class_exp"), sem("class_probs")
        s_pctps, s_pct = sem("class_probsT_in_psum"), sem("class_probsT")
        s_ocps, s_oc = sem("class_out_in_psum"), sem("class_out_copied")
        s_qps, s_qev = sem("queries_in_psum"), sem("queries_ready")
        s_seps, s_se = sem("mean_scores_in_psum"), sem("mean_scores_ready")
        s_dps, s_neg = sem("scores_in_psum"), sem("scores_ready")
        s_L = sem("logits_ready")
        s_step = sem("topk_step")
        s_xm = sem("masked_logits_ready")
        s_exp = sem("exp_done_plus_two")
        s_rr = sem("row_reciprocals")
        s_ptps, s_pt = sem("probsT_in_psum"), sem("probsT_ready")
        s_av = sem("head_out_in_psum")
        s_o = sem("tile_out_ready")
        s_otps, s_ot = sem("tile_outT_in_psum"), sem("tile_outT_ready")
        s_otc = sem("class_outT_ready")
        s_prps = sem("projection0_in_psum")
        s_mw = sem("router_weights_landed")
        s_rps, s_lg = sem("router_logits_in_psum"), sem("router_logits_ready")
        s_rsub, s_rexp = sem("router_logits_shifted"), sem("router_exp_ready")
        s_gate = sem("gates_ready")
        s_gtps, s_gt = sem("gatesT_in_psum"), sem("gatesT_ready")
        s_gbps = sem("gated_bias_in_psum")
        s_ew = [sem(f"expert_weights_landed_{n}") for n in range(2)]
        s_ewf = [sem(f"expert_weights_free_{n}") for n in range(2)]
        s_h1ps, s_h1 = sem("hidden_in_psum"), sem("hidden_ready_plus_two")
        s_yps, s_y = sem("expert_out_in_psum"), sem("expert_out_added")
        s_gc = sem("gate_columns_ready")
        s_b1c = sem("expert_bias_ready")
        s_aw = sem("attn1_weights_landed")
        s1_kps, s1_kev = sem("keys1_in_psum"), sem("keys1_ready")
        s1_vps, s1_vev = sem("values1_in_psum"), sem("values1_ready")
        s1_qcps, s1_qm = sem("class_queries1_in_psum"), sem("class_queries1_spread")
        s1_csc, s1_cmx, s1_cexp = sem("class_scores1_in_psum"), sem("class_max1"), sem("class_exp1")
        s1_cp, s1_ctps, s1_ct = sem("class_probs1"), sem("class_probsT1_in_psum"), sem("class_probsT1")
        s1_ocps = sem("class_out1_in_psum")
        s1_qps, s1_qz = sem("queries1_in_psum"), sem("queries1_spread")
        s1_dps, s1_mx, s1_exp = sem("scores1_in_psum"), sem("max1_ready"), sem("exp1_done")
        s1_ptps, s1_pt, s1_ptr = sem("probsT1_in_psum"), sem("probsT1_ready"), sem("probsT1_row_ready")
        s1_ops, s1_o = sem("out1_in_psum"), sem("out1_normalised")
        s1_otps, s1_ot, s1_otc = sem("outT1_in_psum"), sem("outT1_ready"), sem("class_outT1_ready")
        s1_prps = sem("projection1_in_psum")
        s_sl = sem("slots_landed")
        s_slot = [sem(f"ring_landed_{n}") for n in range(RING)]
        s_free = [sem(f"ring_free_{n}") for n in range(RING)]
        s2_u, s2_sq, s2_ms, s2_rms = sem("layernorm_done"), sem("squares_summed"), sem("mean_squares"), sem("rms_ready")
        s2_xr, s2_nrm = sem("rmsnorm_done"), sem("norms_ready")
        s2_sln, s2_sl, s2_slps, s2_slT = sem("slot_norms_ready"), sem("slots_ready"), sem("slotsT_in_psum"), sem("slotsT_ready")
        s2_lps, s2_mx, s2_exp, s2_d = sem("logits2_in_psum"), sem("logits2_max"), sem("logits2_exp"), sem("dispatch_ready")
        s2_dps, s2_dt = sem("dispatchT_in_psum"), sem("dispatchT_ready")
        s2_yps, s2_ym = sem("slot_inputs_in_psum"), sem("slot_inputs_ready")
        s2_cps, s2_csub, s2_cexp, s2_c = sem("combine_in_psum"), sem("combine_shifted"), sem("combine_exp"), sem("combine_ready")
        s2_ctps, s2_ct = sem("combineT_in_psum"), sem("combineT_ready")
        s2_h1, s2_hb, s2_hs = sem("fc1_in_psum"), sem("fc1_biased"), sem("hidden2_ready")
        s2_f2, s2_y2b, s2_y2ps, s2_y2 = sem("fc2_in_psum"), sem("fc2_biased"), sem("slot_outT_in_psum"), sem("slot_out_ready")
        s2_ops = sem("combined_in_psum")

        @block.sync
        def _(sp):
            sp.dma_start(xp, a["xp"]).then_inc(s_x, 16)
            sp.dma_start(wt, a["wt"]).then_inc(s_x, 16)
            sp.dma_start(cst[:, :], a["cst"]).then_inc(s_cst, 16)
            sp.dma_start(cstb[:, :], a["cstb"]).then_inc(s_cst, 16)
            for n, name in enumerate(("tok_b", "b_out", "b_proj", "norm_w")):
                sp.dma_start(rowsb[:, n, :], a[name].partition_broadcast(P)).then_inc(s_cst, 16)
            sp.dma_start(scb[:, :], a["scale0"].partition_broadcast(KP)).then_inc(s_cst, 16)
            sp.wait_ge(s_hz, 1)
            sp.dma_start(h[0:B, TILES - 1, :], a["cls"].partition_broadcast(B)).then_inc(s_cls, 16)
            sp.dma_start(wo0[:, :, :], a["wo0"].rearrange("(c p) n -> p c n", p=P)).then_inc(s_wo0, 16)
            sp.wait_ge(s_xq, 2)
            sp.dma_start(wq0[:, :, :], a["wqkv0"].rearrange("(k p) n -> p k n", p=KP)).then_inc(s_wq0, 16)
            sp.wait_ge(s_av, 4 * H)
            sp.dma_start(wq1, a["wqkv1"]).then_inc(s_aw, 16)
            sp.dma_start(wp1, a["wp1"]).then_inc(s_aw, 16)
            sp.dma_start(wr[:, :, :], a["wr"]).then_inc(s_mw, 16)
            sp.dma_start(b2e[:, :], a["b2e"]).then_inc(s_mw, 16)
            sp.dma_start(b1e[:, :, :], a["b1e"]).then_inc(s_mw, 16)
            w1d = a["w1e"].rearrange("e (k p) f -> e p k f", p=KP)
            w2d = a["w2e"].rearrange("e (c p) d -> e p c d", p=P)
            sp.wait_ge(s_av, 4 * H)
            for n in range(2):
                sp.dma_start(w1e[n], w1d[n]).then_inc(s_ew[n], 16)
                sp.dma_start(w2e[n][:, :, :], w2d[n]).then_inc(s_ew[n], 16)
            f1 = a["fc1"].rearrange("(g s) (p j) f -> g s p (j f)", s=2, j=3)
            f2 = a["fc2"].rearrange("s (c p) d -> s p c d", p=P)
            sp.wait_ge(s_prps, TILES)
            for n in range(RING):
                sp.dma_start(arena[:, n * SLOT:(n + 1) * SLOT], f1[n].rearrange("s p f -> (s p) f")).then_inc(s_slot[n], 16)
            with sp.Fori(1, E // 2) as i:
                for n in range(2):
                    sp.wait_ge(s_ewf[n], i)
                    sp.dma_start(w1e[n], w1d[ds(2 * i + n, 1)].rearrange("e p k f -> p (e k) f")).then_inc(s_ew[n], 16)
                    sp.dma_start(w2e[n][:, :, :], w2d[ds(2 * i + n, 1)].rearrange("e p c d -> p (e c) d")).then_inc(s_ew[n], 16)
            sp.wait_ge(s_y, E + 1)
            sp.dma_start(slots, a["slots"]).then_inc(s_sl, 16)
            sp.dma_start(slscale, a["slot_scale"]).then_inc(s_sl, 16)
            sp.dma_start(b1T, a["b1T"]).then_inc(s_sl, 16)
            sp.dma_start(b2T, a["b2T"]).then_inc(s_sl, 16)
            with sp.Fori(1, PAIRS // RING) as i:
                for n in range(RING):
                    sp.wait_ge(s_free[n], i)
                    sp.dma_start(arena[:, n * SLOT:(n + 1) * SLOT],
                                 f1[ds(RING * i + n, 1)].rearrange("g s p f -> (g s p) f")).then_inc(s_slot[n], 16)
            with sp.Fori(0, PAIRS // RING) as i:
                for n in range(RING):
                    sp.wait_ge(s_free[n], i + PAIRS // RING)
                    sp.dma_start(arena[:, n * SLOT:(n + 1) * SLOT].rearrange("p (s c d) -> p s c d", s=2, c=MF),
                                 f2[ds(2 * (RING * i + n), 2)].rearrange("s p c d -> p s c d")).then_inc(s_slot[n], 16)
            sp.wait_ge(s_final, TILES)
            sp.dma_start(out[0:4 * P, :].rearrange("(t p) d -> p t d", p=P), h[:, 0:4, :]).then_inc(s_out, 16)
            sp.dma_start(out[4 * P:4 * P + B, :], h[0:B, 4, :]).then_inc(s_out, 16)
            sp.wait_ge(s_out, 32)

        @block.gpsimd
        def _(pool):
            nc.gpsimd.memset(h[:, TILES - 1, :], 0.0).then_inc(s_hz, 1)
            nc.gpsimd.memset(am[:, :], 0.0).then_inc(s_amz, 1)
            nc.gpsimd.memset(qz0[:, :, :], 0.0).then_inc(s_qzz, 1)
            pool.wait_ge(s_amax, 2)
            nc.gpsimd.partition_all_reduce(gm[:, 0:2], am[:, 0:2], P, RMAX).then_inc(s_gmax, 1)
            with pool.Fori(0, 4) as t:
                for hd in range(H):
                    n = t * H + hd
                    if hd == 0:
                        pool.wait_ge(s_se, t + 1)
                    pool.wait_ge(s_neg, n + 1)
                    nc.gpsimd.tensor_tensor(L[:, hd, :], seb, neg[:, hd, :], ALU.subtract).then_inc(s_L, 1)

        @block.tensor
        def _(pe):
            def mm(o, l, r, start=True, stop=True, **kw):
                return nc.tensor.matmul(o, l, r, start=start, stop=stop, **kw)

            def transpose_tiles(s_):
                for t in range(TILES):
                    pe.wait_ge(s_xn, s_ * TILES + t + 1)
                    for k in range(KD):
                        i = nc.tensor.transpose(bank[0:KP, t, k * P:k * P + rows(t)],
                                                xn[0:rows(t), t, k * KP:(k + 1) * KP], ident[0:rows(t), 0:rows(t)])
                    i.then_inc(s_xtps, 1)

            pe.wait_ge(s_cst, 16 * 7)
            pe.wait_ge(s_xq, 2)
            for t in range(4):
                b, q = t // 2, t % 2
                for k in range(KD):
                    i = mm(bank[:, t, 0:D], xqb[:, k, t * P:(t + 1) * P], wqb[:, k, :], k == 0, k == KD - 1)
                i.then_inc(s_tokps, 1)
            transpose_tiles(0)

            pe.wait_ge(s_wq0, 16)
            pe.wait_ge(s_xt, TILES)

            def keys(c):
                if c >= 2:
                    pe.wait_ge(s_kev, c - 1)
                for b in range(B):
                    for k in range(KD):
                        i = mm(bank[:, 2 * (c % 2) + b, 0:NT], wq0[:, k, IN0 + c * P:IN0 + (c + 1) * P],
                               xT[:, k, b * NT:(b + 1) * NT], k == 0, k == KD - 1)
                i.then_inc(s_kps, 1)

            def values(v):
                if v >= 2:
                    pe.wait_ge(s_vev, v - 1)
                m = P if v < 4 else 1
                cs = cols(v) if v < 4 else slice((v - 4) * NT + NP, (v - 3) * NT)
                for half in range(2):
                    for k in range(KD):
                        i = mm(bank[0:m, 4 + 2 * (v % 2) + half, 0:IN0 // 2], xT[:, k, cs],
                               wq0[:, k, 2 * IN0 + half * 384:2 * IN0 + half * 384 + 384], k == 0, k == KD - 1)
                i.then_inc(s_vps, 1)

            for c in range(6):
                keys(c)
                values(c)

            pe.wait_ge(s_wqs, 1)
            pe.wait_ge(s_kev, 6)
            for c in range(C0):
                for k in range(KD):
                    i = mm(bank[:, 0, c * B:(c + 1) * B], wq0[:, k, c * P:(c + 1) * P], xT[:, k, cols(4)],
                           k == 0, k == KD - 1)
            i.then_inc(s_qcps, 1)
            pe.wait_ge(s_qm, 1)
            for b in range(B):
                for c in range(C0):
                    mm(bank[0:NR, 1, 0:NT], QM0[:, c, b * NR:(b + 1) * NR], kT0[:, c, b * NT:(b + 1) * NT],
                       b == 0 and c == 0, False)
            mm(bank[0:NR, 1, 0:NT], identb[0:NR, 0:NR], bigc, False, True).then_inc(s_ncps, 1)
            pe.wait_ge(s_nc, 1)
            mm(bank[0:NR, 3, 0:NT], const("nb", NR), negC).then_inc(s_lc, 1)

            def prepare(t):
                b = t // 2
                col = t * P + b
                for c in range(C0):
                    for k in range(KD):
                        i = mm(bank[:, 4 + c // 3, (c % 3) * P:(c % 3 + 1) * P], wq0[:, k, c * P:(c + 1) * P],
                               xT[:, k, ds(col, P)], k == 0, k == KD - 1)
                i.then_inc(s_qps, 1)
                pe.wait_ge(s_qev, t + 1)
                for c in range(C0):
                    i = mm(bank[:, 2, 0:NT], qf0[:, c, :], kT0[:, c, ds(b * NT, NT)], c == 0, c == C0 - 1)
                i.then_inc(s_seps, 1)

            def scores(t, hd):
                b = t // 2
                mm(bank[:, hd % 2, 0:NT], qz0[:, hd, :], kT0[:, hd // 2, ds(b * NT, NT)], True, False)
                mm(bank[:, hd % 2, 0:NT], identb, bigd[:, ds((1 - t % 2) * P, NT)], False, True).then_inc(s_dps, 1)

            def attend(t, hd):
                b = t // 2
                pe.wait_ge(s_exp, t * H + hd + 3)
                for k in range(2):
                    nc.tensor.transpose(bank[:, 3, k * P:(k + 1) * P], PR[:, hd % 2, k * P:(k + 1) * P], ident)
                nc.tensor.transpose(bank[0:1, 3, 2 * P:3 * P], PR[:, hd % 2, NP:NT], ident).then_inc(s_ptps, 1)
                pe.wait_ge(s_pt, t * H + hd + 1)
                o = bank[:, 6 + hd % 2, 0:HD0]
                hs = slice(hd * HD0, (hd + 1) * HD0)
                for k in range(2):
                    mm(o, PT[:, k, :], v0[:, ds(2 * b + k, 1), hs], k == 0, False)
                mm(o, PTr, vc0[0:1, ds(b, 1), hs], False, True).then_inc(s_av, 1)

            def finish(t):
                pe.wait_ge(s_o, t + 1)
                for c in range(C0):
                    i = nc.tensor.transpose(bank[:, 4 + c // 3, (c % 3) * P:(c % 3 + 1) * P],
                                            O0[:, c * P:(c + 1) * P], ident)
                i.then_inc(s_otps, 1)
                pe.wait_ge(s_ot, t + 1)

            prepare(0)
            for hd in range(H):
                if hd >= 2:
                    pe.wait_ge(s_neg, hd - 1)
                scores(0, hd)
            pe.wait_ge(s_pcn, 1)
            for k in range(2):
                nc.tensor.transpose(bank[:, 3, k * NR:(k + 1) * NR], PR[0:NR, 0, k * P:(k + 1) * P], ident[0:NR, 0:NR])
            nc.tensor.transpose(bank[0:1, 3, 2 * NR:3 * NR], PR[0:NR, 0, NP:NT], ident[0:NR, 0:NR]).then_inc(s_pctps, 1)
            pe.wait_ge(s_pct, 1)
            for b in range(B):
                for c in range(C0):
                    o = bank[:, 6, (b * C0 + c) * H:(b * C0 + c + 1) * H]
                    for k in range(2):
                        mm(o, v0[:, 2 * b + k, c * P:(c + 1) * P], PCT[:, k, b * H:(b + 1) * H], k == 0, False)
                    i = mm(o, vc0[0:1, b, c * P:(c + 1) * P], PCr[0:1, b * H:(b + 1) * H], False, True)
            i.then_inc(s_ocps, 1)
            pe.wait_ge(s_oc, 1)

            with pe.Fori(0, 3) as t:
                prepare(t + 1)
                for hd in range(H):
                    attend(t, hd)
                    pe.wait_ge(s_neg, (t + 1) * H + hd - 1)
                    scores(t + 1, hd)
                finish(t)
            for hd in range(H):
                attend(3, hd)
            finish(3)

            pe.wait_ge(s_wo0, 16)
            for t in range(TILES):
                if t == TILES - 1:
                    pe.wait_ge(s_otc, 1)
                for c in range(C0):
                    i = mm(bank[0:rows(t), t, 0:D], OT0[:, c, cols(t)], wo0[:, c, :], c == 0, c == C0 - 1)
                i.then_inc(s_prps, 1)
            transpose_tiles(1)
            pe.wait_ge(s_xt, 2 * TILES)
            pe.wait_ge(s_mw, 48)
            for t in range(TILES):
                for k in range(KD):
                    i = mm(bank[0:rows(t), 5, t * E:(t + 1) * E], xT[:, k, cols(t)], wr[:, k, :], k == 0, k == KD - 1)
            i.then_inc(s_rps, 1)
            pe.wait_ge(s_gate, 1)
            for t in range(TILES):
                i = nc.tensor.transpose(bank[0:E, 6 + t // 4, (t % 4) * P:(t % 4) * P + rows(t)], gate[0:rows(t), t, :],
                                        ident[0:rows(t), 0:rows(t)])
            i.then_inc(s_gtps, 1)
            pe.wait_ge(s_gt, 1)
            for t in range(TILES):
                i = mm(bank[0:rows(t), t, 0:D], gT[:, t, 0:rows(t)], b2e[:, :])
            i.then_inc(s_gbps, 1)
            pe.wait_ge(s_y, 1)

            with pe.Fori(0, E // 2) as i2:
                for n in range(2):
                    e = 2 * i2 + n
                    pe.wait_ge(s_ew[n], 32 * i2 + 32)
                    for m in range(MF):
                        pe.wait_ge(s_h1, e * MF + m + 1)
                        for b in range(B):
                            for k in range(KD):
                                i = mm(bank[:, 2 * (m % 2) + b, 0:NT], w1e[n][:, k, m * P:(m + 1) * P],
                                       xT[:, k, b * NT:(b + 1) * NT], k == 0, k == KD - 1)
                        i.then_inc(s_h1ps, 1)
                    pe.wait_ge(s_y, e + 1)
                    for m in range(MF):
                        pe.wait_ge(s_h1, e * MF + m + 3)
                        for t in range(4):
                            mm(bank[:, 4 + t, 0:D], hT[:, m, cols(t)], w2e[n][:, m, :], m == 0, m == MF - 1)
                    for m in range(MF):
                        i = mm(bank[0:B, 7, 256:256 + D], hT[:, m, cols(4)], w2e[n][:, m, :], m == 0, m == MF - 1)
                    i.then_inc(s_yps, 1)
                    pe.wait_ge(s_yps, e + 1)
                    pe.sem_inc(s_ewf[n], 1)
            transpose_tiles(2)
            pe.wait_ge(s_aw, 32)
            pe.wait_ge(s_xt, 3 * TILES)
            for c in range(KD):
                for b in range(B):
                    for k in range(KD):
                        i = mm(bank[0:KP, 2 * c + b, 0:NT], wq1[:, k, D + c * KP:D + (c + 1) * KP],
                               xT[:, k, b * NT:(b + 1) * NT], k == 0, k == KD - 1)
                i.then_inc(s1_kps, 1)
            for v in range(6):
                if v >= 2:
                    pe.wait_ge(s1_vev, v - 1)
                cs = cols(v) if v < 4 else slice((v - 4) * NT + NP, (v - 3) * NT)
                for k in range(KD):
                    i = mm(bank[0:P if v < 4 else 1, 4 + v % 2, 0:D], xT[:, k, cs], wq1[:, k, 2 * D:3 * D],
                           k == 0, k == KD - 1)
                i.then_inc(s1_vps, 1)
            for c in range(KD):
                for k in range(KD):
                    i = mm(bank[0:KP, 6, c * B:(c + 1) * B], wq1[:, k, c * KP:(c + 1) * KP], xT[:, k, cols(4)],
                           k == 0, k == KD - 1)
            i.then_inc(s1_qcps, 1)
            pe.wait_ge(s1_qm, 1)
            pe.wait_ge(s1_kev, 2)
            for b in range(B):
                for c in range(KD):
                    i = mm(bank[0:NR, 7, 0:NT], QM1[:, c, b * NR:(b + 1) * NR], kT1[:, c, b * NT:(b + 1) * NT],
                           b == 0 and c == 0, b == 1 and c == KD - 1)
            i.then_inc(s1_csc, 1)
            pe.wait_ge(s1_cp, 1)
            for k in range(2):
                nc.tensor.transpose(bank[:, 3, k * NR:(k + 1) * NR], PC1[:, k * P:(k + 1) * P], ident[0:NR, 0:NR])
            nc.tensor.transpose(bank[0:1, 3, 2 * NR:3 * NR], PC1[:, NP:NT], ident[0:NR, 0:NR]).then_inc(s1_ctps, 1)
            pe.wait_ge(s1_ct, 1)
            pe.wait_ge(s1_vev, 6)
            for b in range(B):
                for c in range(KD):
                    o = bank[0:KP, 6, (b * KD + c) * H:(b * KD + c + 1) * H]
                    for k in range(2):
                        mm(o, v1[:, 2 * b + k, c * KP:(c + 1) * KP], PCT[:, k, b * H:(b + 1) * H], k == 0, False)
                    i = mm(o, vc1[0:1, b, c * KP:(c + 1) * KP], PCr[0:1, b * H:(b + 1) * H], False, True)
            i.then_inc(s1_ocps, 1)
            pe.wait_ge(s1_otc, 1)
            with pe.Fori(0, 4) as t:
                b = t // 2
                for c in range(KD):
                    for k in range(KD):
                        i = mm(bank[0:KP, 4, c * P:(c + 1) * P], wq1[:, k, c * KP:(c + 1) * KP],
                               xT[:, k, ds(t * P + b, P)], k == 0, k == KD - 1)
                i.then_inc(s1_qps, 1)
                pe.wait_ge(s1_qz, t + 1)

                def scores(hd):
                    if hd >= 2:
                        pe.wait_ge(s1_exp, t * H + hd - 1)
                    mm(bank[:, hd % 2, 0:NT], qz1[:, hd, :], kT1[:, hd // HPC, ds(b * NT, NT)]).then_inc(s1_dps, 1)

                def attend(hd):
                    pe.wait_ge(s1_pt, t * H + hd + 1)
                    pe.wait_ge(s1_ptr, t * H + hd + 1)
                    o, hs = bank[:, 6, hd * HD1:(hd + 1) * HD1], slice(hd * HD1, (hd + 1) * HD1)
                    for k in range(2):
                        mm(o, PT1[:, hd % 2, k, :], v1[:, ds(2 * b + k, 1), hs], k == 0, False)
                    return mm(o, PTr1[:, hd % 2, :], vc1[0:1, ds(b, 1), hs], False, True)

                scores(0)
                for hd in range(H):
                    if hd < H - 1:
                        scores(hd + 1)
                    pe.wait_ge(s1_exp, t * H + hd + 1)
                    o = bank[:, 2 + hd % 2, :]
                    for k in range(2):
                        nc.tensor.transpose(o[:, k * P:(k + 1) * P], PR1[:, hd % 2, k * P:(k + 1) * P], ident)
                    nc.tensor.transpose(bank[0:1, 4 + hd % 2, 0:P], PR1[:, hd % 2, NP:NT], ident).then_inc(s1_ptps, 1)
                    if hd:
                        attend(hd - 1)
                attend(H - 1).then_inc(s1_ops, 1)
                pe.wait_ge(s1_o, t + 1)
                for c in range(KD):
                    i = nc.tensor.transpose(bank[0:KP, 7, c * P:(c + 1) * P], O1[:, c * KP:(c + 1) * KP], ident)
                i.then_inc(s1_otps, 1)
            pe.wait_ge(s1_ot, 4)
            for t in range(TILES):
                for k in range(KD):
                    i = mm(bank[0:rows(t), t, 0:D], OT1[:, k, cols(t)], wp1[:, k, :], k == 0, k == KD - 1)
                i.then_inc(s1_prps, 1)
            pe.wait_ge(s2_sl, 1)
            for k in range(KD):
                i = nc.tensor.transpose(bank[0:KP, 5, k * S:(k + 1) * S], slots[:, k * KP:(k + 1) * KP], ident[0:S, 0:S])
            i.then_inc(s2_slps, 1)
            transpose_tiles(3)
            pe.wait_ge(s2_slT, 1)
            pe.wait_ge(s_xt, 4 * TILES)
            for b in range(B):
                for k in range(KD):
                    i = mm(bank[0:S, 6 + b, 0:NT], slT[:, k, :], xT[:, k, b * NT:(b + 1) * NT], k == 0, k == KD - 1)
            i.then_inc(s2_lps, 1)
            for t in range(TILES):
                for k in range(KD):
                    i = mm(bank[0:rows(t), 4, t * S:(t + 1) * S], xT[:, k, cols(t)], slT[:, k, :], k == 0, k == KD - 1)
            i.then_inc(s2_cps, 1)
            pe.wait_ge(s2_d, 1)
            for t in range(4):
                nc.tensor.transpose(bank[:, 5, t * S:(t + 1) * S], Dm[:, t // 2, (t % 2) * P:(t % 2 + 1) * P], ident[0:S, 0:S])
            nc.tensor.transpose(bank[0:B, 5, 4 * S:5 * S], Dm[:, :, NP], ident[0:S, 0:S]).then_inc(s2_dps, 1)
            pe.wait_ge(s2_dt, 1)
            for par in range(2):
                for j in range(3):
                    for b in range(B):
                        o = bank[64 * par:64 * par + 64, 6, (j * B + b) * PAIRS:(j * B + b + 1) * PAIRS]
                        for q in range(2):
                            mm(o, xr[:, 2 * b + q, j:D:3], DT[:, 2 * b + q, par:S:2], q == 0, False)
                        i = mm(o, xr[0:B, 4, j:D:3], DTc[:, b, par:S:2], False, True)
            i.then_inc(s2_yps, 1)
            pe.wait_ge(s2_ym, 1)
            with pe.Fori(0, PAIRS // RING) as g:
                for n in range(RING):
                    pe.wait_ge(s_slot[n], 16 * g + 16)
                    w = arena[:, n * SLOT:(n + 1) * SLOT].rearrange("p (j f) -> p j f", j=3)
                    for m in range(MF):
                        for j in range(3):
                            i = mm(bank[:, m // 3, ds((m % 3) * P + (RING * g + n) * 4, 4)], w[:, j, m * P:(m + 1) * P],
                                   YM[:, ds(RING * g + n, 1), j, :], j == 0, j == 2)
                    i.then_inc(s_free[n], 1)
            pe.wait_ge(s_free[RING - 1], PAIRS // RING)
            pe.sem_inc(s2_h1, 1)
            pe.wait_ge(s2_c, 1)
            for t in range(4):
                nc.tensor.transpose(bank[0:S, 4, t * P:(t + 1) * P], lgc[:, t, :], ident)
            nc.tensor.transpose(bank[0:S, 5, 0:B], lgc[0:B, 4, :], ident[0:B, 0:B]).then_inc(s2_ctps, 1)
            pe.wait_ge(s2_hs, 2)
            with pe.Fori(0, PAIRS // RING) as g:
                for n in range(RING):
                    pe.wait_ge(s_slot[n], 16 * g + 16 * (PAIRS // RING + 1))
                    w = arena[:, n * SLOT:(n + 1) * SLOT].rearrange("p (s c d) -> p s c d", s=2, c=MF)
                    for q in range(2):
                        for m in range(KD):
                            for k in range(MF):
                                i = mm(bank[0:KP, 2, ds(m * B * S + (RING * g + n) * 4 + 2 * q, 2)],
                                       w[:, q, k, m * KP:(m + 1) * KP],
                                       hs[:, k, ds((RING * g + n) * 4 + 2 * q, 2)], k == 0, k == MF - 1)
                    i.then_inc(s_free[n], 1)
            pe.wait_ge(s_free[RING - 1], 2 * PAIRS // RING)
            pe.sem_inc(s2_f2, 1)
            pe.wait_ge(s2_y2b, 1)
            for b in range(B):
                for k in range(KD):
                    i = nc.tensor.transpose(bank[0:S, 3, b * D + k * KP:b * D + (k + 1) * KP], y2T[:, k, b:B * S:B],
                                            ident[0:KP, 0:KP])
            i.then_inc(s2_y2ps, 1)
            pe.wait_ge(s2_y2, 1)
            pe.wait_ge(s2_ct, 1)
            for t in range(4):
                mm(bank[:, t, 0:D], CT[:, t, :], y2[:, t // 2, :]).then_inc(s2_ops, 1)
            for b in range(B):
                i = mm(bank[0:B, 4, 0:D], CTc[:, b, :], y2[:, b, :], b == 0, b == 1)
            i.then_inc(s2_ops, 1)

        @block.scalar
        def _(act):
            def copy(o, i, scale=1.0):
                return nc.scalar.activation(o, i, ACT.Copy, scale=scale)

            def deviations(s_):
                act.wait_ge(s_var, s_ + 1)
                nc.scalar.activation(sm[:, 1, :], sm[:, 0, :], ACT.Sqrt).then_inc(s_std, 1)

            def copy_tiles(s_):
                for t in range(TILES):
                    act.wait_ge(s_xtps, s_ * TILES + t + 1)
                    copy(xT[:, :, cols(t)],
                         bank[0:KP, t, 0:KD * P].rearrange("p (k n) -> p k n", k=KD)[:, :, 0:rows(t)]).then_inc(s_xt, 1)

            deviations(0)
            copy_tiles(0)
            for c in range(C0):
                act.wait_ge(s_kps, c + 1)
                copy(kT0[:, c, :].rearrange("p (b n) -> p b n", b=B), bank[:, 2 * (c % 2):2 * (c % 2) + 2, 0:NT]).then_inc(s_kev, 1)
            act.wait_ge(s_ncps, 1)
            copy(negC, bank[0:NR, 1, 0:NT]).then_inc(s_nc, 1)

            def prepare(t, first):
                qb = bank[:, 4:6, 0:3 * P].rearrange("p a (c n) -> p a c n", c=3)
                act.wait_ge(s_qps, t + 1)
                for par in range(2):
                    r = slice(64 * par, 64 * par + 64)
                    for half in range(2):
                        copy(qz0[r, 6 * half + par:6 * half + 6:2, :], bank[r, 4 + half, 0:3 * P].rearrange(
                            "p (c n) -> p c n", c=3))
                for half in range(2):
                    i = copy(qf0[:, 3 * half:3 * half + 3, :],
                             bank[:, 4 + half, 0:3 * P].rearrange("p (c n) -> p c n", c=3), -1.0 / H)
                i.then_inc(s_qev, 1)
                act.wait_ge(s_seps, t + 1)
                if not first:
                    act.wait_ge(s_L, t * H)
                copy(seb, bank[:, 2, 0:NT]).then_inc(s_se, 1)

            def keep(t, hd):
                act.wait_ge(s_dps, t * H + hd + 1)
                copy(neg[:, hd, :], bank[:, hd % 2, 0:NT]).then_inc(s_neg, 1)

            def attend(t, hd):
                n = t * H + hd
                act.wait_ge(s_xm, n + 1)
                nc.scalar.activation(PR[:, hd % 2, :], X[:, hd % 2, :], ACT.Exp, bias=nmx[:, hd % 2:hd % 2 + 1],
                                     accum_out=rs[:, hd:hd + 1]).then_inc(s_exp, 1)
                act.wait_ge(s_ptps, n + 1)
                copy(PT, bank[:, 3, 0:2 * P].rearrange("p (k n) -> p k n", k=2))
                copy(PTr, bank[0:1, 3, 2 * P:3 * P]).then_inc(s_pt, 1)
                act.wait_ge(s_av, n + 1)
                act.wait_ge(s_rr, n + 2)
                i = nc.scalar.activation(O0[:, hd * HD0:(hd + 1) * HD0], bank[:, 6 + hd % 2, 0:HD0], ACT.Copy,
                                         scale=rr[:, hd:hd + 1])
                if hd == H - 1:
                    i.then_inc(s_o, 1)

            def finish(t):
                act.wait_ge(s_otps, t + 1)
                for half in range(2):
                    i = copy(OT0[:, 3 * half:3 * half + 3, ds(t * P + t // 2, P)],
                             bank[:, 4 + half, 0:3 * P].rearrange("p (c n) -> p c n", c=3))
                i.then_inc(s_ot, 1)

            act.wait_ge(s_qzz, 1)
            prepare(0, True)
            for hd in range(H):
                keep(0, hd)
            act.wait_ge(s_xc, 1)
            nc.scalar.activation(PR[0:NR, 0, :], X[0:NR, 0, :], ACT.Exp, bias=nmx[0:NR, 0:1],
                                 accum_out=gm[0:NR, 6:7]).then_inc(s_pc, 1)
            act.wait_ge(s_pctps, 1)
            copy(PCT[:, :, :], bank[:, 3, 0:2 * NR].rearrange("p (k n) -> p k n", k=2))
            copy(PCr[:, :], bank[0:1, 3, 2 * NR:3 * NR]).then_inc(s_pct, 1)
            act.wait_ge(s_ocps, 1)
            copy(Oc.rearrange("p a b -> p (a b)"), bank[:, 6, 0:B * C0 * H]).then_inc(s_oc, 1)
            act.sem_inc(s_exp, 2)
            with act.Fori(0, 3) as t:
                prepare(t + 1, False)
                for hd in range(H):
                    attend(t, hd)
                    keep(t + 1, hd)
                finish(t)
            for hd in range(H):
                attend(3, hd)
            finish(3)
            deviations(1)
            copy_tiles(1)
            act.wait_ge(s_rsub, 1)
            nc.scalar.activation(lg[:, :, :], lg[:, :, :], ACT.Exp).then_inc(s_rexp, 1)
            act.wait_ge(s_gtps, 1)
            copy(gT[:, 0:4, :].rearrange("p a b -> p (a b)"), bank[0:E, 6, :])
            copy(gT[:, 4, 0:B], bank[0:E, 7, 0:B]).then_inc(s_gt, 1)
            act.wait_ge(s_mw, 48)
            act.sem_inc(s_h1, 2)
            with act.Fori(0, E // 2) as i2:
                for n in range(2):
                    e = 2 * i2 + n
                    copy(b1c[:, n, :], b1e[:, :, ds(e, 1)]).then_inc(s_b1c, 1)
                    for m in range(MF):
                        act.wait_ge(s_h1ps, e * MF + m + 1)
                        if m == 0:
                            act.wait_ge(s_b1c, e + 1)
                        nc.scalar.activation(hT[:, m, :].rearrange("p (b n) -> p b n", b=B),
                                             bank[:, 2 * (m % 2):2 * (m % 2) + 2, 0:NT], ACT.Gelu,
                                             bias=b1c[:, n, m:m + 1]).then_inc(s_h1, 1)
            deviations(2)
            copy_tiles(2)
            for c in range(KD):
                act.wait_ge(s1_kps, c + 1)
                copy(kT1[:, c, :].rearrange("p (b n) -> p b n", b=B), bank[0:KP, 2 * c:2 * c + 2, 0:NT]).then_inc(s1_kev, 1)
            act.wait_ge(s1_cmx, 1)
            nc.scalar.activation(PC1, bank[0:NR, 7, 0:NT], ACT.Exp, bias=nmx[0:NR, 0:1],
                                 accum_out=gm[0:NR, 6:7]).then_inc(s1_cexp, 1)
            act.wait_ge(s1_ctps, 1)
            copy(PCT[:, :, :], bank[:, 3, 0:2 * NR].rearrange("p (k n) -> p k n", k=2))
            copy(PCr[:, :], bank[0:1, 3, 2 * NR:3 * NR]).then_inc(s1_ct, 1)
            with act.Fori(0, 4) as t:
                def exponentials(hd):
                    act.wait_ge(s1_mx, t * H + hd + 1)
                    nc.scalar.activation(PR1[:, hd % 2, :], bank[:, hd % 2, 0:NT], ACT.Exp, bias=nmx[:, hd % 2:hd % 2 + 1],
                                         accum_out=rs[:, hd:hd + 1]).then_inc(s1_exp, 1)
                exponentials(0)
                for hd in range(H):
                    if hd < H - 1:
                        exponentials(hd + 1)
                    act.wait_ge(s1_ptps, t * H + hd + 1)
                    copy(PTr1[:, hd % 2, :], bank[0:1, 4 + hd % 2, 0:P]).then_inc(s1_ptr, 1)
                act.wait_ge(s1_otps, t + 1)
                copy(OT1[:, :, ds(t * P + t // 2, P)],
                     bank[0:KP, 7, 0:KD * P].rearrange("p (k n) -> p k n", k=KD)).then_inc(s1_ot, 1)
            def sum_squares(src, dst, squares):
                return nc.scalar.activation(squares, src, ACT.Square, accum_out=dst)

            act.wait_ge(s_sl, 64)
            sum_squares(slots, sm[0:S, 12, 0:1], junk[:, :]).then_inc(s2_sln, 1)
            act.wait_ge(s2_sln, 1)
            nc.scalar.activation(sm[0:S, 12, 1:2], sm[0:S, 12, 0:1], ACT.Sqrt).then_inc(s2_sln, 1)
            act.wait_ge(s2_slps, 1)
            copy(slT, bank[0:KP, 5, 0:KD * S].rearrange("p (k n) -> p k n", k=KD)).then_inc(s2_slT, 1)
            deviations(3)
            act.wait_ge(s2_u, 1)
            for t in range(TILES):
                i = sum_squares(xn[:, t, :], sm[:, 6, t:t + 1], xr[:, t, :])
            i.then_inc(s2_sq, 1)
            act.wait_ge(s2_ms, 1)
            nc.scalar.activation(sm[:, 7, :], sm[:, 7, :], ACT.Sqrt).then_inc(s2_rms, 1)
            act.wait_ge(s2_xr, 1)
            for t in range(TILES):
                i = sum_squares(xr[:, t, :], sm[:, 9, t:t + 1], hb[:, t, :])
            i.then_inc(s2_nrm, 1)
            act.wait_ge(s2_nrm, 1)
            nc.scalar.activation(sm[:, 10, :], sm[:, 9, :], ACT.Sqrt).then_inc(s2_nrm, 1)
            copy_tiles(3)
            act.wait_ge(s2_mx, 1)
            for b in range(B):
                i = nc.scalar.activation(Dm[:, b, :], bank[0:S, 6 + b, 0:NT], ACT.Exp, bias=nmx[0:S, b:b + 1],
                                         accum_out=rs[0:S, b:b + 1])
            i.then_inc(s2_exp, 1)
            act.wait_ge(s2_csub, 1)
            nc.scalar.activation(lgc, lgc, ACT.Exp).then_inc(s2_cexp, 1)
            for half in range(2):
                act.wait_ge(s2_hb, half + 1)
                nc.scalar.activation(hs[:, 3 * half:3 * half + 3, :], hs[:, 3 * half:3 * half + 3, :],
                                     ACT.Gelu).then_inc(s2_hs, 1)
            act.wait_ge(s2_y2ps, 1)
            copy(y2.rearrange("p b d -> p (b d)"), bank[0:S, 3, 0:B * D]).then_inc(s2_y2, 1)

        @block.vector
        def _(dve):
            ts, tt, stt = nc.vector.tensor_scalar, nc.vector.tensor_tensor, nc.vector.scalar_tensor_tensor
            chain = [0]

            def link(ins):
                chain[0] += 1
                ins.then_inc(s_dve, 1)
                dve.wait_ge(s_dve, chain[0])

            def normalise(s_, done=None):
                for t in range(TILES):
                    i = nc.vector.bn_stats(stats[:, t, :], h[:, t, :])
                link(i)
                for t in range(TILES):
                    i = nc.vector.bn_aggr(mv[:, t, :], stats[:, t, :])
                link(i)
                ts(sm[:, 0, :], mv[:, :, 1], EPS, None, ALU.add).then_inc(s_var, 1)
                dve.wait_ge(s_std, s_ + 1)
                link(nc.vector.reciprocal(sm[:, 2, :], sm[:, 1, :]))
                for t in range(TILES):
                    i = ts(xn[:, t, :], h[:, t, :], mv[:, t, 0:1], sm[:, 2, t:t + 1], ALU.subtract, ALU.mult)
                    if not done:
                        i.then_inc(s_xn, 1)
                if done:
                    i.then_inc(done, 1)
                    dve.wait_ge(done, 1)
                else:
                    dve.wait_ge(s_xn, (s_ + 1) * TILES)

            dve.wait_ge(s_amz, 1)
            dve.wait_ge(s_x, 32)
            nc.vector.tensor_reduce(am[0:KP, 0:1], xp.rearrange("p k n -> p (k n)"), AX.X, ALU.max,
                                    apply_absolute_value=True).then_inc(s_amax, 1)
            nc.vector.tensor_reduce(am[0:KP, 1:2], wt.rearrange("p k n -> p (k n)"), AX.X, ALU.max,
                                    apply_absolute_value=True).then_inc(s_amax, 1)
            dve.wait_ge(s_gmax, 1)
            link(ts(gm[:, 2:4], gm[:, 0:2], 1e-8, 1.0 / QMAX, ALU.max, ALU.mult))
            link(nc.vector.reciprocal(gm[:, 4:6], gm[:, 2:4]))
            link(tt(gm[:, 6:7], gm[:, 2:3], gm[:, 3:4], ALU.mult))
            for n, (src, tmp, dst) in enumerate((
                    (xp.rearrange("p k (a n) -> p k a n", a=2), neg[0:KP, 0:4, 0:NP].rearrange("p (k a) n -> p k a n", a=2),
                     xqb.rearrange("p k (a n) -> p k a n", a=2)),
                    (wt, neg[0:KP, 4:6, 0:D], wqb))):
                link(ts(tmp, src, gm[0:KP, 4 + n:5 + n], QMAX, ALU.mult, ALU.min))
                link(ts(tmp, tmp, -QMAX, MAGIC, ALU.max, ALU.add))
                ts(dst, tmp, MAGIC, None, ALU.subtract).then_inc(s_xq, 1)
            dve.wait_ge(s_cst, 16 * 7)
            for t in range(4):
                dve.wait_ge(s_tokps, t + 1)
                i = stt(h[:, t, :], bank[:, t, 0:D], gm[:, 6:7], rowsb[:, 0, :], ALU.mult, ALU.add)
            dve.wait_ge(s_cls, 16)
            link(i)
            normalise(0)

            dve.wait_ge(s_wq0, 16)
            for k in range(KD):
                i = stt(wq0[:, k, 0:IN0].rearrange("p (h e) -> p h e", h=H),
                        wq0[:, k, 0:IN0].rearrange("p (h e) -> p h e", h=H), -1.0,
                        scb[:, :].unsqueeze(2).to_broadcast([KP, H, HD0]), ALU.mult, ALU.mult)
            i.then_inc(s_wqs, 1)
            for v in range(6):
                dve.wait_ge(s_vps, v + 1)
                src = bank[:, 4 + 2 * (v % 2):6 + 2 * (v % 2), 0:384]
                dst = v0[:, v, :] if v < 4 else vc0[0:1, v - 4, :]
                nc.vector.tensor_copy(dst.rearrange("p (a n) -> p a n", a=2), src if v < 4 else src[0:1]).then_inc(s_vev, 1)
            dve.wait_ge(s_qcps, 1)
            for b in range(B):
                i = tt(QM0[:, :, b * NR:(b + 1) * NR],
                       const("mq0").rearrange("p (c b r) -> p c b r", c=C0, b=B)[:, :, b, :],
                       bank[:, 0, b:C0 * B:B].unsqueeze(2).to_broadcast([P, C0, NR]), ALU.mult)
            i.then_inc(s_qm, 1)

            def drop(p, src, early):
                step = 0
                now = src
                for r in range(ROUNDS):
                    if step:
                        dve.wait_ge(s_step, step)
                    nc.vector.max(m8[0:p, :], now).then_inc(s_step, 1)
                    step += 1
                    dve.wait_ge(s_step, step)
                    nc.vector.match_replace(W[0:p], m8[0:p, :], now, -BIG).then_inc(s_step, 1)
                    step += 1
                    now = W[0:p]
                    if r == 1 and early:
                        early()
                dve.wait_ge(s_step, step)
                return step

            def mask(p, slot, logits, step, done):
                stt(X[0:p, slot, :], W[0:p], THR, logits, ALU.add, ALU.min).then_inc(s_step, 1)
                dve.wait_ge(s_step, step + 1)
                dve.sem_clear(s_step)
                nc.vector.tensor_reduce(nmx[0:p, slot:slot + 1], X[0:p, slot, :], AX.X, ALU.max,
                                        negate=True).then_inc(done, 1)

            dve.wait_ge(s_nc, 1)
            step = drop(NR, negC, None)
            dve.wait_ge(s_lc, 1)
            mask(NR, 0, bank[0:NR, 3, 0:NT], step, s_xc)
            dve.wait_ge(s_pc, 1)
            link(nc.vector.reciprocal(gm[0:NR, 7:8], gm[0:NR, 6:7]))
            ts(PR[0:NR, 0, :], PR[0:NR, 0, :], gm[0:NR, 7:8], None, ALU.mult).then_inc(s_pcn, 1)
            link(nc.vector.memset(rs[:, H - 1:H], 1.0))

            with dve.Fori(0, 4) as t:
                for hd in range(H):
                    n = t * H + hd
                    dve.wait_ge(s_L, n + 1)
                    nc.vector.memset(tick[:, 0:1], 0.0)

                    def reciprocal_before():
                        dve.wait_ge(s_exp, n + 2)
                        g = (hd - 1) % H
                        nc.vector.reciprocal(rr[:, g:g + 1], rs[:, g:g + 1]).then_inc(s_rr, 1)

                    step = drop(P, neg[:, hd, :], reciprocal_before)
                    mask(P, hd % 2, L[:, hd, :], step, s_xm)
            dve.wait_ge(s_exp, 4 * H + 2)
            nc.vector.reciprocal(rr[:, H - 1:H], rs[:, H - 1:H]).then_inc(s_rr, 1)
            dve.wait_ge(s_oc, 1)
            link(tt(Oc.rearrange("p (b c) r -> p b c r", b=B)[:, 0], Oc.rearrange("p (b c) r -> p b c r", b=B)[:, 0],
                    const("mo0").rearrange("p (c r) -> p c r", c=C0), ALU.mult))
            link(tt(Oc.rearrange("p (b c) r -> p b c r", b=B)[:, 1], Oc.rearrange("p (b c) r -> p b c r", b=B)[:, 1],
                    const("mo0").rearrange("p (c r) -> p c r", c=C0), ALU.mult))
            for b in range(B):
                i = nc.vector.tensor_reduce(OT0[:, :, b * NT + NP:b * NT + NP + 1],
                                            Oc.rearrange("p (b c) r -> p b c r", b=B)[:, b], AX.X, ALU.add)
            i.then_inc(s_otc, 1)
            for t in range(TILES):
                i = tt(hb[:, t, :], h[:, t, :], rowsb[:, 1, :], ALU.add)
            link(i)
            for t in range(TILES):
                dve.wait_ge(s_prps, t + 1)
                i = tt(h[0:rows(t), t, :], bank[0:rows(t), t, 0:D], hb[0:rows(t), t, :], ALU.add)
            link(i)
            normalise(1)
            link(nc.vector.memset(lg[:, TILES - 1, :], 0.0))
            dve.wait_ge(s_rps, 1)
            nc.vector.tensor_copy(lg[:, 0:4, :], bank[:, 5, 0:4 * E].rearrange("p (t e) -> p t e", e=E))
            link(nc.vector.tensor_copy(lg[0:B, 4, :], bank[0:B, 5, 4 * E:5 * E]))
            link(nc.vector.tensor_reduce(sm[:, 3, :], lg[:, :, :], AX.X, ALU.max))
            tt(lg[:, :, :], lg[:, :, :], sm[:, 3, :].unsqueeze(2).to_broadcast([P, TILES, E]),
               ALU.subtract).then_inc(s_rsub, 1)
            dve.wait_ge(s_rexp, 1)
            link(nc.vector.tensor_reduce(sm[:, 4, :], lg[:, :, :], AX.X, ALU.add))
            link(nc.vector.reciprocal(sm[:, 5, :], sm[:, 4, :]))
            link(tt(lg[:, :, :], lg[:, :, :], sm[:, 5, :].unsqueeze(2).to_broadcast([P, TILES, E]), ALU.mult))
            for t in range(TILES):
                i = nc.vector.max(top[:, t, :], lg[:, t, :])
            link(i)
            for t in range(TILES):
                i = nc.vector.max_index(topi[:, t, :], top[:, t, :], lg[:, t, :])
            link(i)
            link(nc.vector.tensor_copy(topf[:, :, :], topi[:, :, :]))
            for t in range(TILES):
                ts(gate[:, t, :], const("iota"), topf[:, t, 0:1], top[:, t, 0:1], ALU.is_equal, ALU.mult)
                i = ts(gate2[:, t, :], const("iota"), topf[:, t, 1:2], top[:, t, 1:2], ALU.is_equal, ALU.mult)
            link(i)
            tt(gate[:, :, :], gate[:, :, :], gate2[:, :, :], ALU.add).then_inc(s_gate, 1)
            link(tt(h[:, :, :], h[:, :, :], xn[:, :, :], ALU.add))
            dve.wait_ge(s_gbps, 1)
            for t in range(TILES):
                i = tt(h[0:rows(t), t, :], bank[0:rows(t), t, 0:D], h[0:rows(t), t, :], ALU.add)
            i.then_inc(s_y, 1)
            dve.wait_ge(s_y, 1)
            with dve.Fori(0, E // 2) as i2:
                for n in range(2):
                    e = 2 * i2 + n
                    nc.vector.tensor_copy(gcol[:, n, :], gate[:, :, ds(e, 1)]).then_inc(s_gc, 1)
                    dve.wait_ge(s_gc, e + 1)
                    dve.wait_ge(s_yps, e + 1)
                    for t in range(TILES):
                        src = bank[:, 4 + t, 0:D] if t < 4 else bank[0:B, 7, 256:256 + D]
                        i = stt(h[0:rows(t), t, :], src, gcol[0:rows(t), n, t:t + 1], h[0:rows(t), t, :],
                                ALU.mult, ALU.add)
                    i.then_inc(s_y, 1)
                    dve.wait_ge(s_y, e + 2)
            normalise(2)
            for v in range(6):
                dve.wait_ge(s1_vps, v + 1)
                dst = v1[:, v, :] if v < 4 else vc1[0:1, v - 4, :]
                nc.vector.tensor_copy(dst, bank[0:P if v < 4 else 1, 4 + v % 2, 0:D]).then_inc(s1_vev, 1)
            dve.wait_ge(s1_qcps, 1)
            for b in range(B):
                i = tt(QM1[:, :, b * NR:(b + 1) * NR],
                       const("mq1", KP).rearrange("p (c b r) -> p c b r", c=KD, b=B)[:, :, b, :],
                       bank[0:KP, 6, b:KD * B:B].unsqueeze(2).to_broadcast([KP, KD, NR]), ALU.mult)
            i.then_inc(s1_qm, 1)
            dve.wait_ge(s1_csc, 1)
            nc.vector.tensor_reduce(nmx[0:NR, 0:1], bank[0:NR, 7, 0:NT], AX.X, ALU.max, negate=True).then_inc(s1_cmx, 1)
            dve.wait_ge(s1_cexp, 1)
            link(nc.vector.reciprocal(gm[0:NR, 7:8], gm[0:NR, 6:7]))
            ts(PC1, PC1, gm[0:NR, 7:8], None, ALU.mult).then_inc(s1_cp, 1)
            dve.wait_ge(s1_ocps, 1)
            for b in range(B):
                i = tt(Oc1[:, b * KD * H:(b + 1) * KD * H], bank[0:KP, 6, b * KD * H:(b + 1) * KD * H],
                       const("mo1", KP), ALU.mult)
            link(i)
            for b in range(B):
                i = nc.vector.tensor_reduce(OT1[:, :, b * NT + NP:b * NT + NP + 1],
                                            Oc1[:, b * KD * H:(b + 1) * KD * H].rearrange("p (c r) -> p c r", c=KD),
                                            AX.X, ALU.add)
            i.then_inc(s1_otc, 1)
            with dve.Fori(0, 4) as t:
                dve.wait_ge(s1_qps, t + 1)
                for c in range(KD):
                    i = tt(qz1[:, c * HPC:(c + 1) * HPC, :],
                           bank[0:KP, 4, c * P:(c + 1) * P].unsqueeze(1).to_broadcast([KP, HPC, P]),
                           const("mz1", KP).unsqueeze(2).to_broadcast([KP, HPC, P]), ALU.mult)
                i.then_inc(s1_qz, 1)

                def maximum(hd):
                    dve.wait_ge(s1_dps, t * H + hd + 1)
                    nc.vector.tensor_reduce(nmx[:, hd % 2:hd % 2 + 1], bank[:, hd % 2, 0:NT], AX.X, ALU.max,
                                            negate=True).then_inc(s1_mx, 1)
                maximum(0)
                for hd in range(H):
                    if hd < H - 1:
                        maximum(hd + 1)
                    dve.wait_ge(s1_ptps, t * H + hd + 1)
                    nc.vector.tensor_copy(PT1[:, hd % 2], bank[:, 2 + hd % 2, 0:2 * P].rearrange(
                        "p (k n) -> p k n", k=2)).then_inc(s1_pt, 1)
                dve.wait_ge(s1_ops, t + 1)
                nc.vector.reciprocal(rr[:, :], rs[:, :]).then_inc(s_rr, 1)
                dve.wait_ge(s_rr, t + 1 + 4 * H + 1)
                tt(O1.rearrange("p (h e) -> p h e", h=H), bank[:, 6, 0:D].rearrange("p (h e) -> p h e", h=H),
                   rr[:, :].unsqueeze(2).to_broadcast([P, H, HD1]), ALU.mult).then_inc(s1_o, 1)
            for t in range(TILES):
                i = tt(hb[:, t, :], h[:, t, :], rowsb[:, 2, :], ALU.add)
            link(i)
            for t in range(TILES):
                dve.wait_ge(s1_prps, t + 1)
                i = tt(h[0:rows(t), t, :], bank[0:rows(t), t, 0:D], hb[0:rows(t), t, :], ALU.add)
            link(i)
            dve.wait_ge(s2_sln, 2)
            link(ts(sm[0:S, 12, 2:3], sm[0:S, 12, 1:2], EPS, None, ALU.max))
            link(nc.vector.reciprocal(sm[0:S, 12, 3:4], sm[0:S, 12, 2:3]))
            ts(slots, slots, sm[0:S, 12, 3:4], slscale, ALU.mult, ALU.mult).then_inc(s2_sl, 1)
            normalise(3, s2_u)
            dve.wait_ge(s2_sq, 1)
            ts(sm[:, 7, :], sm[:, 6, :], 1.0 / D, EPS, ALU.mult, ALU.add).then_inc(s2_ms, 1)
            dve.wait_ge(s2_rms, 1)
            link(nc.vector.reciprocal(sm[:, 8, :], sm[:, 7, :]))
            for t in range(TILES):
                i = stt(xr[:, t, :], xn[:, t, :], sm[:, 8, t:t + 1], rowsb[:, 3, :], ALU.mult, ALU.mult)
            i.then_inc(s2_xr, 1)
            dve.wait_ge(s2_xr, 1)
            dve.wait_ge(s2_nrm, 2)
            link(ts(sm[:, 10, :], sm[:, 10, :], EPS, None, ALU.max))
            link(nc.vector.reciprocal(sm[:, 11, :], sm[:, 10, :]))
            for t in range(TILES):
                ts(xn[:, t, :], xr[:, t, :], sm[:, 11, t:t + 1], None, ALU.mult).then_inc(s_xn, 1)
            link(nc.vector.memset(YM, 0.0))
            link(nc.vector.memset(lgc[:, TILES - 1, :], 0.0))
            link(nc.vector.memset(CTc, 0.0))
            dve.wait_ge(s2_lps, 1)
            nc.vector.tensor_reduce(nmx[0:S, 0:B], bank[0:S, 6:8, 0:NT], AX.X, ALU.max, negate=True).then_inc(s2_mx, 1)
            dve.wait_ge(s2_exp, 1)
            link(nc.vector.reciprocal(rr[0:S, 0:B], rs[0:S, 0:B]))
            for b in range(B):
                i = ts(Dm[:, b, :], Dm[:, b, :], rr[0:S, b:b + 1], None, ALU.mult)
            i.then_inc(s2_d, 1)
            dve.wait_ge(s2_dps, 1)
            nc.vector.tensor_copy(DT.rearrange("p a b -> p (a b)"), bank[:, 5, 0:4 * S])
            for b in range(B):
                i = ts(DTc[:, b, :], bank[0:B, 5, 4 * S:5 * S], cst[0:B, CST["eye2"][0] + b:CST["eye2"][0] + b + 1],
                       None, ALU.mult)
            i.then_inc(s2_dt, 1)
            dve.wait_ge(s2_yps, 1)
            for par in range(2):
                r = slice(64 * par, 64 * par + 64)
                for b in range(B):
                    i = nc.vector.tensor_copy(YM[r, :, :, 2 * par + b],
                                              bank[r, 6, 0:3 * B * PAIRS].rearrange("p (j b s) -> p s j b", j=3, b=B)[:, :, :, b])
            i.then_inc(s2_ym, 1)
            dve.wait_ge(s2_cps, 1)
            nc.vector.tensor_copy(lgc[:, 0:4, :], bank[:, 4, 0:4 * S].rearrange("p (t s) -> p t s", t=4))
            link(nc.vector.tensor_copy(lgc[0:B, 4, :], bank[0:B, 4, 4 * S:5 * S]))
            link(nc.vector.tensor_reduce(sm[:, 13, :], lgc, AX.X, ALU.max))
            tt(lgc, lgc, sm[:, 13, :].unsqueeze(2).to_broadcast([P, TILES, S]), ALU.subtract).then_inc(s2_csub, 1)
            dve.wait_ge(s2_cexp, 1)
            link(nc.vector.tensor_reduce(sm[:, 14, :], lgc, AX.X, ALU.add))
            link(nc.vector.reciprocal(sm[:, 15, :], sm[:, 14, :]))
            tt(lgc, lgc, sm[:, 15, :].unsqueeze(2).to_broadcast([P, TILES, S]), ALU.mult).then_inc(s2_c, 1)
            dve.wait_ge(s2_h1, 1)
            for half in range(2):
                for b in range(B):
                    i = tt(hs[:, 3 * half:3 * half + 3, b:B * S:B],
                           bank[:, half, 0:3 * P].rearrange("p (m n) -> p m n", m=3)[:, :, b:B * S:B],
                           b1T[:, 3 * half:3 * half + 3, :], ALU.add)
                i.then_inc(s2_hb, 1)
            dve.wait_ge(s2_ctps, 1)
            nc.vector.tensor_copy(CT.rearrange("p a b -> p (a b)"), bank[0:S, 4, :])
            for b in range(B):
                i = nc.vector.tensor_copy(CTc[:, b, b:b + 1], bank[0:S, 5, b:b + 1])
            i.then_inc(s2_ct, 1)
            dve.wait_ge(s2_f2, 1)
            for b in range(B):
                i = tt(y2T[:, :, b:B * S:B], bank[0:KP, 2, 0:KD * B * S].rearrange("p (k n) -> p k n", k=KD)[:, :, b:B * S:B],
                       b2T, ALU.add)
            i.then_inc(s2_y2b, 1)
            for t in range(TILES):
                dve.wait_ge(s2_ops, t + 1)
                tt(h[0:rows(t), t, :], bank[0:rows(t), t, 0:D], h[0:rows(t), t, :], ALU.add).then_inc(s_final, 1)


def kernel(**inputs):
    import concourse.bacc as bacc
    from concourse.bass_utils import run_bass_kernel_spmd

    x = {k: np.asarray(v) for k, v in inputs.items()}
    patch = D // 3
    side = int(patch ** 0.5)
    xp = x["x"].reshape(B, 3, GRID, side, GRID, side).transpose(1, 3, 5, 0, 2, 4).reshape(D, B, NP)[:, :, ::-1]
    chunk = lambda m: m.reshape(KD, KP, -1).transpose(1, 0, 2)
    cst = np.zeros((P, CST_W), np.float32)

    def put(name, v):
        lo, hi = CST[name]
        cst[:v.shape[0], lo:hi] = v.reshape(v.shape[0], -1)

    p, p1 = np.arange(P), np.arange(KP)
    put("ident", np.eye(P))
    m = np.zeros((P, C0, B, NR))
    mo = np.zeros((P, C0, H))
    for c in range(C0):
        for b in range(B):
            m[p, c, b, b * H + 2 * c + p // HD0] = 1
        mo[p, c, 2 * c + p // HD0] = 1
    put("mq0", m)
    put("mo0", mo)
    m = np.zeros((KP, KD, B, NR))
    mo = np.zeros((KP, KD, H))
    for c in range(KD):
        for b in range(B):
            m[p1, c, b, b * H + HPC * c + p1 // HD1] = HD1 ** -0.5
        mo[p1, c, HPC * c + p1 // HD1] = 1
    put("mq1", m)
    put("mo1", mo)
    m = np.zeros((KP, HPC))
    m[p1, p1 // HD1] = HD1 ** -0.5
    put("mz1", m)
    put("nb", -(np.eye(NR) + np.kron(np.eye(B), np.ones((H, H))) / H))
    put("iota", np.tile(np.arange(E), (P, 1)))
    put("eye2", np.eye(B))
    bf = mybir.dt.np(BF16)
    cstb = np.zeros((P, CSTB_W), np.float32)
    cstb[:, 0:P] = np.eye(P)
    cstb[p, CSTB["bigd"][0] + P + p] = -BIG
    cstb[:, CSTB["bigc"][0] + NP] = -BIG
    arrays = {
        "xp": chunk(xp.reshape(D, B * NP)), "wt": chunk(x["L0_tok_w"].reshape(D, D).T),
        "cst": cst, "cstb": cstb.astype(bf),
        "tok_b": x["L0_tok_b"], "b_out": x["L0_attn_b_out"], "b_proj": x["L1_attn_b_proj"],
        "norm_w": x["L1_ffn_norm_weight"], "scale0": x["L0_attn_scale"],
        "cls": x["cls_tok"].reshape(D), "wqkv0": x["L0_attn_w_qkv"], "wo0": x["L0_attn_w_out"],
        "wqkv1": chunk(x["L1_attn_w_qkv"].T), "wp1": chunk(x["L1_attn_w_proj"].T),
        "slots": x["L1_ffn_slots"], "slot_scale": x["L1_ffn_scale"].reshape(S, 1),
        "fc1": x["L1_ffn_fc1_weight"], "fc2": x["L1_ffn_fc2_weight"],
        "b1T": x["L1_ffn_fc1_bias"].reshape(S, MF, P).transpose(2, 1, 0),
        "b2T": x["L1_ffn_fc2_bias"].reshape(S, KD, KP).transpose(2, 1, 0),
        "wr": chunk(x["L0_ffn_Wr"].T), "w1e": x["L0_ffn_W1"], "w2e": x["L0_ffn_W2"], "b2e": x["L0_ffn_b2"],
        "b1e": x["L0_ffn_b1"].reshape(E, MF, P).transpose(2, 1, 0),
    }
    nc = bacc.Bacc("TRN2", target_bir_lowering=False, num_devices=1)
    arrays = {k: np.ascontiguousarray(v) for k, v in arrays.items()}
    aps = {k: nc.dram_tensor(f"in_{k}", v.shape, mybir.dt.from_np(v.dtype), kind="ExternalInput").ap()
           for k, v in arrays.items()}
    aps["out"] = nc.dram_tensor("out", (B * NT, D), F32, kind="ExternalOutput").ap()
    vit_tower(nc, aps)
    r = run_bass_kernel_spmd(nc, [{f"in_{k}": v for k, v in arrays.items()}], core_ids=[0])
    got = r.results[0]["out"]
    patches = got[:B * NP].reshape(B, NP, D)[:, ::-1]
    return np.ascontiguousarray(np.concatenate([got[B * NP:].reshape(B, 1, D), patches], axis=1))
```

```python
import concourse.bass as bass
from concourse import mybir
from contextlib import ExitStack
import numpy as np

F32 = mybir.dt.float32
BF16 = mybir.dt.bfloat16
U32 = mybir.dt.uint32
ALU = mybir.AluOpType
ACT = mybir.ActivationFunctionType
AX = mybir.AxisListType
RMAX = bass.bass_isa.ReduceOp.max
ds = bass.ds

P = 128
B = 2
GRID = 16
NP = GRID * GRID
NT = NP + 1
D = 192
KP = 96
KD = D // KP
H = 12
HD0, HD1 = 64, 16
IN0 = H * HD0
C0 = IN0 // P
HPC = KP // HD1
NR = B * H
DROP = NT - int(NT * 0.75) - 1
ROUNDS = DROP // 8
E, FF = 16, 768
MF = FF // P
S = 64
PAIRS = S // 2
TILES = 5
BIG = 2.0 ** 126
THR = 1e30
MAGIC = 12582912.0
QMAX = 127.0
EPS = 1e-5
RING = 8
SLOT = 3 * FF

CST = {}
_at = 0
for _name, _w in (("ident", P), ("mq0", C0 * B * H * B), ("mo0", C0 * H), ("mz1", HPC), ("mq1", KD * B * NR),
                  ("mo1", KD * H), ("nb", NR), ("iota", E), ("eye2", B), ("m16", 16)):
    CST[_name] = (_at, _at + _w)
    _at += _w
CST_W = _at
CSTB = {"identb": (0, P), "bigd": (P, P + NP + P + 1), "bigc": (2 * P + NP + 1, 2 * P + NP + 1 + NT)}
CSTB_W = 2 * P + NP + 1 + NT


def rows(t):
    return P if t < TILES - 1 else B


def cols(t):
    if t == TILES - 1:
        return slice(NP, B * NT, NT)
    a = (t // 2) * NT + (t % 2) * P
    return slice(a, a + P)


def vit_tower(nc, a):
    out = a["out"]
    with ExitStack() as ctx:
        def sb(name, shape, dt=F32):
            return ctx.enter_context(nc.sbuf_tensor(name, shape, dt))

        def sem(name):
            return ctx.enter_context(nc.semaphore(name))

        cst = sb("cst", [P, CST_W])
        cstb = sb("cstb", [P, CSTB_W], BF16)

        def const(name, p=P):
            lo, hi = CST[name]
            return cst[0:p, lo:hi]

        ident = const("ident")
        identb = cstb[:, 0:P]
        bigd = cstb[:, CSTB["bigd"][0]:CSTB["bigd"][1]]
        bigc = cstb[0:NR, CSTB["bigc"][0]:CSTB["bigc"][1]]

        h = sb("h", [P, TILES, D])
        hb = sb("hb", [P, TILES, D])
        xn = sb("xn", [P, TILES, D])
        xT = sb("xT", [KP, KD, B * NT])
        rowsb = sb("rowsb", [P, 4, D])
        stats = sb("stats", [P, TILES, 6])
        mv = sb("mv", [P, TILES, 2])
        sm = sb("sm", [P, 16, TILES])
        NEGB = RING * SLOT
        arena = sb("arena", [P, NEGB])

        class Cut:
            at = 0

        def take(p, *shape):
            n = 1
            for s_ in shape:
                n *= s_
            v = arena[0:p, Cut.at:Cut.at + n]
            Cut.at += n
            assert Cut.at <= NEGB
            if len(shape) == 1:
                return v
            names = "abc"[:len(shape)]
            return v.rearrange("p (%s) -> p %s" % (" ".join(names), " ".join(names)),
                               **{k: s_ for k, s_ in zip(names, shape)})

        wq0 = sb("wq0", [KP, KD, 3 * IN0])
        kT0 = take(P, C0, B * NT)
        qz0 = take(P, H, P)
        qf0 = take(P, C0, P)
        W = take(P, 2, NT)
        X = take(P, 2, NT)
        PR = take(P, 2, NT)
        PT = take(P, 2, P)
        PTr = take(1, P)
        O0 = take(P, IN0)
        seb = take(P, NT)
        negC = take(NR, NT)
        Oc = take(P, B * C0, H)
        L = sb("L", [P, H, NT])
        neg = sb("neg", [P, H, NT])
        OT0 = sb("OT0", [P, C0, B * NT])
        v0 = sb("v0", [P, 4, IN0])
        vc0 = sb("vc0", [1, B, IN0])
        wo0 = sb("wo0", [P, C0, D])
        QM0 = sb("QM0", [P, C0, B * NR])
        PCT = sb("PCT", [P, 2, NR])
        PCr = sb("PCr", [1, NR])
        m8 = sb("m8", [P, 2, 8])
        tick = sb("tick", [P, 8])
        nmx = sb("nmx", [P, 2])
        rs = sb("rs", [P, H])
        rr = sb("rr", [P, H])
        scb = sb("scb", [KP, H])
        junk = sb("junk", [S, D])

        wr = sb("wr", [KP, KD, E])
        lg = sb("lg", [P, TILES, E])
        gate = sb("gate", [P, TILES, E])
        gate2 = sb("gate2", [P, TILES, E])
        top = sb("top", [P, TILES, 8])
        topi = sb("topi", [P, TILES, 8], U32)
        topf = sb("topf", [P, TILES, 8])
        gT = sb("gT", [E, TILES, P])
        b2e = sb("b2e", [E, D])
        b1e = sb("b1e", [P, MF, E])
        b1c = sb("b1c", [P, 2, MF])
        gcol = sb("gcol", [P, 2, TILES])
        w1e = [v0[0:KP, :, :].rearrange("p a b -> p (a b)")[:, n * KD * FF:(n + 1) * KD * FF].rearrange(
            "p (k f) -> p k f", k=KD) for n in range(2)]
        w2e = [sb(f"w2e{n}", [P, MF, D]) for n in range(2)]
        hT = OT0

        wq0f = wq0[:, :, :].rearrange("p a b -> p (a b)")
        wq1 = wq0f[:, 0:KD * 3 * D].rearrange("p (k n) -> p k n", k=KD)
        wp1 = wq0f[:, 1152:1152 + KD * D].rearrange("p (k n) -> p k n", k=KD)
        kT1 = wq0f[:, 1536:1536 + KD * B * NT].rearrange("p (k n) -> p k n", k=KD)
        OT1 = wq0f[:, 2564:2564 + KD * B * NT].rearrange("p (k n) -> p k n", k=KD)
        v1 = sb("v1", [P, 4, D])
        vc1 = sb("vc1", [1, B, D])
        QM1 = sb("QM1", [KP, KD, B * NR])
        qz1 = L[0:KP, :, 0:P]
        PR1 = neg[:, 0:2, :]
        PT1 = neg[:, 2:4, 0:2 * P].rearrange("p a (k n) -> p a k n", k=2)
        PTr1 = neg[0:1, 4:6, 0:P]
        O1 = neg[:, 6, 0:D]
        Oc1 = neg[0:KP, 7, 0:B * KD * H]
        PC1 = neg[0:NR, 8, :]
        kTc = neg[0:KP, 9:11, :]
        vcc = neg[0:1, 11, 0:D]
        vC = w2e[0][:, 0:2, :]

        def carve(buf):
            flat, at = buf[:, :, :].rearrange("p a b -> p (a b)"), [0]

            def cut(p, *shape):
                n = int(np.prod(shape))
                v = flat[0:p, at[0]:at[0] + n]
                at[0] += n
                assert at[0] <= flat.shape[1]
                names = "abc"[:len(shape)]
                if len(shape) == 1:
                    return v
                return v.rearrange("p (%s) -> p %s" % (" ".join(names), " ".join(names)), **dict(zip(names, shape)))
            return cut

        cut = carve(neg)
        YM = cut(P, PAIRS, 3, 32)
        cut = carve(L)
        hrow = cut(P, FF)
        hT2 = cut(P, MF, P)
        lgc = cut(P, TILES, S)
        lgx = cut(P, TILES, P)
        Y2 = cut(P, D)
        cut = carve(OT0)
        slots = cut(S, D)
        slscale = cut(S, 1)
        b1R = cut(P, FF)
        b2R = cut(P, D)
        xr = cut(P, TILES, D)
        DT = cut(P, 4, S)
        DTc = cut(B, B, S)
        Dm = cut(S, B, NT)
        cut = carve(v0)
        CT = cut(P, TILES, P)
        slT = cut(KP, KD, S)
        YMg = cut(P, RING, 3, 32)
        mcol = cut(P, 4)
        zero = cut(P, 32)

        s_cst = sem("constants_landed")
        s_x = sem("patches_landed")
        s_wq0 = sem("attn0_weights_landed")
        s_wo0 = sem("attn0_out_weights_landed")
        s_hz = sem("residual_cleared")
        s_cls = sem("class_rows_landed")
        s_dve = sem("vector_chain")
        s_pool = sem("pool_chain")
        s_amax = sem("absmax_of_partitions")
        s_gmax = sem("absmax_of_all")
        s_xq = sem("quantized")
        s_tokps = sem("tokens_in_psum")
        s_var = sem("variances_ready")
        s_std = sem("deviations_ready")
        s_xn = sem("normalised_tiles")
        s_xtps = sem("transposed_tiles_in_psum")
        s_xt = sem("transposed_tiles")
        s_out = sem("stored")
        s_final = sem("result_ready")
        s_amz = sem("absmax_cleared")
        s_qzz = sem("spread_queries_cleared")

        xp = wq0[:, 0, 0:KD * B * NP].rearrange("p (k n) -> p k n", k=KD)
        wt = wq0[:, 1, 0:KD * D].rearrange("p (k n) -> p k n", k=KD)
        xqb = OT0[0:KP, 0:2, 0:NP].bitcast(BF16)
        wqb = OT0[0:KP, 2:4, 0:D // 2].bitcast(BF16)
        am = sb("am", [P, 2])
        gm = sb("gm", [P, 8])

        bank = ctx.enter_context(nc.psum_tensor("bank", [P, 8, 512], F32))

        block = ctx.enter_context(nc.Block())

        s_kps, s_kev = sem("keys0_in_psum"), sem("keys0_ready")
        s_vps, s_vev = sem("values0_in_psum"), sem("values0_ready")
        s_wqs = sem("query_weights_scaled")
        s_qcps, s_qm = sem("class_queries_in_psum"), sem("class_queries_spread")
        s_ncps, s_nc = sem("class_scores_in_psum"), sem("class_scores_ready")
        s_lc = sem("class_logits_in_psum")
        s_xc, s_pc, s_pcn = sem("class_masked"), sem("class_exp"), sem("class_probs")
        s_pctps, s_pct = sem("class_probsT_in_psum"), sem("class_probsT")
        s_ocps, s_oc = sem("class_out_in_psum"), sem("class_out_copied")
        s_qps, s_qev = sem("queries_in_psum"), sem("queries_ready")
        s_seps, s_se = sem("mean_scores_in_psum"), sem("mean_scores_ready")
        s_dps, s_neg = sem("scores_in_psum"), sem("scores_ready")
        s_L = sem("logits_ready")
        s_step = sem("topk_step")
        s_xm = sem("masked_logits_ready")
        s_exp = sem("exp_done_plus_two")
        s_rr = sem("row_reciprocals")
        s_ptps, s_pt = sem("probsT_in_psum"), sem("probsT_ready")
        s_av = sem("head_out_in_psum")
        s_o = sem("tile_out_ready")
        s_otps, s_ot = sem("tile_outT_in_psum"), sem("tile_outT_ready")
        s_otc = sem("class_outT_ready")
        s_prps = sem("projection0_in_psum")
        s_mw = sem("router_weights_landed")
        s_rps, s_lg = sem("router_logits_in_psum"), sem("router_logits_ready")
        s_rsub, s_rexp = sem("router_logits_shifted"), sem("router_exp_ready")
        s_gate = sem("gates_ready")
        s_gtps, s_gt = sem("gatesT_in_psum"), sem("gatesT_ready")
        s_gbps = sem("gated_bias_in_psum")
        s_ew = [sem(f"expert_weights_landed_{n}") for n in range(2)]
        s_ewf = [sem(f"expert_weights_free_{n}") for n in range(2)]
        s_h1ps, s_h1 = sem("hidden_in_psum"), sem("hidden_ready_plus_two")
        s_yps, s_y = sem("expert_out_in_psum"), sem("expert_out_added")
        s_gc = sem("gate_columns_ready")
        s_b1c = sem("expert_bias_ready")
        s_aw = sem("attn1_weights_landed")
        s1_kps, s1_kev = sem("keys1_in_psum"), sem("keys1_ready")
        s1_vps, s1_vev = sem("values1_in_psum"), sem("values1_ready")
        s1_qcps, s1_qm = sem("class_queries1_in_psum"), sem("class_queries1_spread")
        s1_csc, s1_cmx, s1_cexp = sem("class_scores1_in_psum"), sem("class_max1"), sem("class_exp1")
        s1_cp, s1_ctps, s1_ct = sem("class_probs1"), sem("class_probsT1_in_psum"), sem("class_probsT1")
        s1_ocps = sem("class_out1_in_psum")
        s1_qps, s1_qz = sem("queries1_in_psum"), sem("queries1_spread")
        s1_dps, s1_mx, s1_exp = sem("scores1_in_psum"), sem("max1_ready"), sem("exp1_done")
        s1_ptps, s1_pt, s1_ptr = sem("probsT1_in_psum"), sem("probsT1_ready"), sem("probsT1_row_ready")
        s1_ops, s1_o = sem("out1_in_psum"), sem("out1_normalised")
        s1_otps, s1_ot, s1_otc = sem("outT1_in_psum"), sem("outT1_ready"), sem("class_outT1_ready")
        s1_prps = sem("projection1_in_psum")
        s_sl = sem("slots_landed")
        s_slot = [sem(f"ring_landed_{n}") for n in range(RING)]
        s_free = [sem(f"ring_free_{n}") for n in range(RING)]
        s2_u, s2_sq, s2_ms, s2_rms = sem("layernorm_done"), sem("squares_summed"), sem("mean_squares"), sem("rms_ready")
        s2_xr, s2_nrm = sem("rmsnorm_done"), sem("norms_ready")
        s2_sln, s2_sl, s2_slps, s2_slT = sem("slot_norms_ready"), sem("slots_ready"), sem("slotsT_in_psum"), sem("slotsT_ready")
        s2_lps, s2_mx, s2_exp, s2_d = sem("logits2_in_psum"), sem("logits2_max"), sem("logits2_exp"), sem("dispatch_ready")
        s2_dps, s2_dt = sem("dispatchT_in_psum"), sem("dispatchT_ready")
        s2_yps = sem("slot_inputs_in_psum")
        s2_cps, s2_csub, s2_cexp, s2_c = sem("combine_in_psum"), sem("combine_shifted"), sem("combine_exp"), sem("combine_ready")
        s2_ctps, s2_ct = sem("combineT_in_psum"), sem("combineT_ready")
        s2_hb, s2_ge, s2_htps, s2_hs = sem("fc1_biased"), sem("gelu2_done"), sem("hiddenT_in_psum"), sem("hiddenT_ready")
        s2_z, s2_yg, s2_mg, s2_f2, s2_y2 = sem("zeros_ready"), sem("group_inputs_ready"), sem("group_masks_ready"), sem("fc2_even_in_psum"), sem("slot_out_added")
        s2_ops = sem("combined_in_psum")

        @block.sync
        def _(sp):
            sp.dma_start(xp, a["xp"]).then_inc(s_x, 16)
            sp.dma_start(wt, a["wt"]).then_inc(s_x, 16)
            sp.dma_start(cst[:, :], a["cst"]).then_inc(s_cst, 16)
            sp.dma_start(cstb[:, :], a["cstb"]).then_inc(s_cst, 16)
            for n, name in enumerate(("tok_b", "b_out", "b_proj", "norm_w")):
                sp.dma_start(rowsb[:, n, :], a[name].partition_broadcast(P)).then_inc(s_cst, 16)
            sp.dma_start(scb[:, :], a["scale0"].partition_broadcast(KP)).then_inc(s_cst, 16)
            sp.wait_ge(s_hz, 1)
            sp.dma_start(h[0:B, TILES - 1, :], a["cls"].partition_broadcast(B)).then_inc(s_cls, 16)
            sp.dma_start(wo0[:, :, :], a["wo0"].rearrange("(c p) n -> p c n", p=P)).then_inc(s_wo0, 16)
            sp.wait_ge(s_xq, 2)
            sp.dma_start(wq0[:, :, :], a["wqkv0"].rearrange("(k p) n -> p k n", p=KP)).then_inc(s_wq0, 16)
            sp.wait_ge(s_av, 4 * H)
            sp.dma_start(wq1, a["wqkv1"]).then_inc(s_aw, 16)
            sp.dma_start(wp1, a["wp1"]).then_inc(s_aw, 16)
            sp.dma_start(wr[:, :, :], a["wr"]).then_inc(s_mw, 16)
            sp.dma_start(b2e[:, :], a["b2e"]).then_inc(s_mw, 16)
            sp.dma_start(b1e[:, :, :], a["b1e"]).then_inc(s_mw, 16)
            w1d = a["w1e"].rearrange("e (k p) f -> e p k f", p=KP)
            w2d = a["w2e"].rearrange("e (c p) d -> e p c d", p=P)
            sp.wait_ge(s_av, 4 * H)
            for n in range(2):
                sp.dma_start(w1e[n], w1d[n]).then_inc(s_ew[n], 16)
                sp.dma_start(w2e[n][:, :, :], w2d[n]).then_inc(s_ew[n], 16)
            f1 = a["fc1"].rearrange("(g s) (p j) f -> g s p (j f)", s=2, j=3)
            f2 = a["fc2"].rearrange("s (c p) d -> s p c d", p=P)
            sp.wait_ge(s_prps, TILES)
            for n in range(RING):
                sp.dma_start(arena[:, n * SLOT:(n + 1) * SLOT], f1[n].rearrange("s p f -> (s p) f")).then_inc(s_slot[n], 16)
            with sp.Fori(1, E // 2) as i:
                for n in range(2):
                    sp.wait_ge(s_ewf[n], i)
                    sp.dma_start(w1e[n], w1d[ds(2 * i + n, 1)].rearrange("e p k f -> p (e k) f")).then_inc(s_ew[n], 16)
                    sp.dma_start(w2e[n][:, :, :], w2d[ds(2 * i + n, 1)].rearrange("e p c d -> p (e c) d")).then_inc(s_ew[n], 16)
            sp.wait_ge(s_y, E + 1)
            sp.dma_start(slots, a["slots"]).then_inc(s_sl, 16)
            sp.dma_start(slscale, a["slot_scale"]).then_inc(s_sl, 16)
            sp.dma_start(b1R, a["b1R"]).then_inc(s_sl, 16)
            sp.dma_start(b2R, a["b2R"]).then_inc(s_sl, 16)
            with sp.Fori(1, PAIRS // RING) as i:
                for n in range(RING):
                    sp.wait_ge(s_free[n], i)
                    sp.dma_start(arena[:, n * SLOT:(n + 1) * SLOT],
                                 f1[ds(RING * i + n, 1)].rearrange("g s p f -> (g s p) f")).then_inc(s_slot[n], 16)
            with sp.Fori(0, PAIRS // RING) as i:
                for n in range(RING):
                    sp.wait_ge(s_free[n], i + PAIRS // RING)
                    sp.dma_start(arena[:, n * SLOT:(n + 1) * SLOT].rearrange("p (s c d) -> p s c d", s=2, c=MF),
                                 f2[ds(2 * (RING * i + n), 2)].rearrange("s p c d -> p s c d")).then_inc(s_slot[n], 16)
            sp.wait_ge(s_final, TILES)
            sp.dma_start(out[0:4 * P, :].rearrange("(t p) d -> p t d", p=P), h[:, 0:4, :]).then_inc(s_out, 16)
            sp.dma_start(out[4 * P:4 * P + B, :], h[0:B, 4, :]).then_inc(s_out, 16)
            sp.wait_ge(s_out, 32)

        @block.gpsimd
        def _(pool):
            nc.gpsimd.memset(h[:, TILES - 1, :], 0.0).then_inc(s_hz, 1)
            nc.gpsimd.memset(am[:, :], 0.0).then_inc(s_amz, 1)
            nc.gpsimd.memset(qz0[:, :, :], 0.0).then_inc(s_qzz, 1)
            pool.wait_ge(s_amax, 2)
            nc.gpsimd.partition_all_reduce(gm[:, 0:2], am[:, 0:2], P, RMAX).then_inc(s_gmax, 1)
            with pool.Fori(0, 4) as t:
                for hd in range(H):
                    n = t * H + hd
                    if hd == 0:
                        pool.wait_ge(s_se, t + 1)
                    pool.wait_ge(s_neg, n + 1)
                    nc.gpsimd.tensor_tensor(L[:, hd, :], seb, neg[:, hd, :], ALU.subtract).then_inc(s_L, 1)

        @block.tensor
        def _(pe):
            def mm(o, l, r, start=True, stop=True, **kw):
                return nc.tensor.matmul(o, l, r, start=start, stop=stop, **kw)

            def transpose_tiles(s_):
                for t in range(TILES):
                    pe.wait_ge(s_xn, s_ * TILES + t + 1)
                    for k in range(KD):
                        i = nc.tensor.transpose(bank[0:KP, t, k * P:k * P + rows(t)],
                                                xn[0:rows(t), t, k * KP:(k + 1) * KP], ident[0:rows(t), 0:rows(t)])
                    i.then_inc(s_xtps, 1)

            pe.wait_ge(s_cst, 16 * 7)
            pe.wait_ge(s_xq, 2)
            for t in range(4):
                b, q = t // 2, t % 2
                for k in range(KD):
                    i = mm(bank[:, t, 0:D], xqb[:, k, t * P:(t + 1) * P], wqb[:, k, :], k == 0, k == KD - 1)
                i.then_inc(s_tokps, 1)
            transpose_tiles(0)

            pe.wait_ge(s_wq0, 16)
            pe.wait_ge(s_xt, TILES)

            def keys(c):
                if c >= 2:
                    pe.wait_ge(s_kev, c - 1)
                for b in range(B):
                    for k in range(KD):
                        i = mm(bank[:, 2 * (c % 2) + b, 0:NT], wq0[:, k, IN0 + c * P:IN0 + (c + 1) * P],
                               xT[:, k, b * NT:(b + 1) * NT], k == 0, k == KD - 1)
                i.then_inc(s_kps, 1)

            def values(v):
                if v >= 2:
                    pe.wait_ge(s_vev, v - 1)
                m = P if v < 4 else 1
                cs = cols(v) if v < 4 else slice((v - 4) * NT + NP, (v - 3) * NT)
                for half in range(2):
                    for k in range(KD):
                        i = mm(bank[0:m, 4 + 2 * (v % 2) + half, 0:IN0 // 2], xT[:, k, cs],
                               wq0[:, k, 2 * IN0 + half * 384:2 * IN0 + half * 384 + 384], k == 0, k == KD - 1)
                i.then_inc(s_vps, 1)

            for c in range(6):
                keys(c)
                values(c)

            pe.wait_ge(s_wqs, 1)
            pe.wait_ge(s_kev, 6)
            for c in range(C0):
                for k in range(KD):
                    i = mm(bank[:, 0, c * B:(c + 1) * B], wq0[:, k, c * P:(c + 1) * P], xT[:, k, cols(4)],
                           k == 0, k == KD - 1)
            i.then_inc(s_qcps, 1)
            pe.wait_ge(s_qm, 1)
            for b in range(B):
                for c in range(C0):
                    mm(bank[0:NR, 1, 0:NT], QM0[:, c, b * NR:(b + 1) * NR], kT0[:, c, b * NT:(b + 1) * NT],
                       b == 0 and c == 0, False)
            mm(bank[0:NR, 1, 0:NT], identb[0:NR, 0:NR], bigc, False, True).then_inc(s_ncps, 1)
            pe.wait_ge(s_nc, 1)
            mm(bank[0:NR, 3, 0:NT], const("nb", NR), negC).then_inc(s_lc, 1)

            def prepare(t):
                b = t // 2
                col = t * P + b
                for c in range(C0):
                    for k in range(KD):
                        i = mm(bank[:, 4 + c // 3, (c % 3) * P:(c % 3 + 1) * P], wq0[:, k, c * P:(c + 1) * P],
                               xT[:, k, ds(col, P)], k == 0, k == KD - 1)
                i.then_inc(s_qps, 1)
                pe.wait_ge(s_qev, t + 1)
                for c in range(C0):
                    i = mm(bank[:, 2, 0:NT], qf0[:, c, :], kT0[:, c, ds(b * NT, NT)], c == 0, c == C0 - 1)
                i.then_inc(s_seps, 1)

            def scores(t, hd):
                b = t // 2
                mm(bank[:, hd % 2, 0:NT], qz0[:, hd, :], kT0[:, hd // 2, ds(b * NT, NT)], True, False)
                mm(bank[:, hd % 2, 0:NT], identb, bigd[:, ds((1 - t % 2) * P, NT)], False, True).then_inc(s_dps, 1)

            def attend(t, hd):
                b = t // 2
                pe.wait_ge(s_exp, t * H + hd + 3)
                for k in range(2):
                    nc.tensor.transpose(bank[:, 3, k * P:(k + 1) * P], PR[:, hd % 2, k * P:(k + 1) * P], ident)
                nc.tensor.transpose(bank[0:1, 3, 2 * P:3 * P], PR[:, hd % 2, NP:NT], ident).then_inc(s_ptps, 1)
                pe.wait_ge(s_pt, t * H + hd + 1)
                o = bank[:, 6 + hd % 2, 0:HD0]
                hs = slice(hd * HD0, (hd + 1) * HD0)
                for k in range(2):
                    mm(o, PT[:, k, :], v0[:, ds(2 * b + k, 1), hs], k == 0, False)
                mm(o, PTr, vc0[0:1, ds(b, 1), hs], False, True).then_inc(s_av, 1)

            def finish(t):
                pe.wait_ge(s_o, t + 1)
                for c in range(C0):
                    i = nc.tensor.transpose(bank[:, 4 + c // 3, (c % 3) * P:(c % 3 + 1) * P],
                                            O0[:, c * P:(c + 1) * P], ident)
                i.then_inc(s_otps, 1)
                pe.wait_ge(s_ot, t + 1)

            prepare(0)
            for hd in range(H):
                if hd >= 2:
                    pe.wait_ge(s_neg, hd - 1)
                scores(0, hd)
            pe.wait_ge(s_pcn, 1)
            for k in range(2):
                nc.tensor.transpose(bank[:, 3, k * NR:(k + 1) * NR], PR[0:NR, 0, k * P:(k + 1) * P], ident[0:NR, 0:NR])
            nc.tensor.transpose(bank[0:1, 3, 2 * NR:3 * NR], PR[0:NR, 0, NP:NT], ident[0:NR, 0:NR]).then_inc(s_pctps, 1)
            pe.wait_ge(s_pct, 1)
            for b in range(B):
                for c in range(C0):
                    o = bank[:, 6, (b * C0 + c) * H:(b * C0 + c + 1) * H]
                    for k in range(2):
                        mm(o, v0[:, 2 * b + k, c * P:(c + 1) * P], PCT[:, k, b * H:(b + 1) * H], k == 0, False)
                    i = mm(o, vc0[0:1, b, c * P:(c + 1) * P], PCr[0:1, b * H:(b + 1) * H], False, True)
            i.then_inc(s_ocps, 1)
            pe.wait_ge(s_oc, 1)

            with pe.Fori(0, 3) as t:
                for hd in range(H):
                    if hd == H // 2:
                        prepare(t + 1)
                    attend(t, hd)
                    if hd % 2 and hd >= H // 2:
                        for g in range(2 * hd - H - 2, 2 * hd - H + 2):
                            pe.wait_ge(s_neg, (t + 1) * H + g - 1)
                            scores(t + 1, g)
                finish(t)
            for hd in range(H):
                attend(3, hd)
            finish(3)

            pe.wait_ge(s_wo0, 16)
            for t in range(TILES):
                if t == TILES - 1:
                    pe.wait_ge(s_otc, 1)
                for c in range(C0):
                    i = mm(bank[0:rows(t), t, 0:D], OT0[:, c, cols(t)], wo0[:, c, :], c == 0, c == C0 - 1)
                i.then_inc(s_prps, 1)
            transpose_tiles(1)
            pe.wait_ge(s_xt, 2 * TILES)
            pe.wait_ge(s_mw, 48)
            for t in range(TILES):
                for k in range(KD):
                    i = mm(bank[0:rows(t), 5, t * E:(t + 1) * E], xT[:, k, cols(t)], wr[:, k, :], k == 0, k == KD - 1)
            i.then_inc(s_rps, 1)
            pe.wait_ge(s_gate, 1)
            for t in range(TILES):
                i = nc.tensor.transpose(bank[0:E, 6 + t // 4, (t % 4) * P:(t % 4) * P + rows(t)], gate[0:rows(t), t, :],
                                        ident[0:rows(t), 0:rows(t)])
            i.then_inc(s_gtps, 1)
            pe.wait_ge(s_gt, 1)
            for t in range(TILES):
                i = mm(bank[0:rows(t), t, 0:D], gT[:, t, 0:rows(t)], b2e[:, :])
            i.then_inc(s_gbps, 1)
            pe.wait_ge(s_y, 1)

            with pe.Fori(0, E // 2) as i2:
                for n in range(2):
                    e = 2 * i2 + n
                    pe.wait_ge(s_ew[n], 32 * i2 + 32)
                    for m in range(MF):
                        pe.wait_ge(s_h1, e * MF + m + 1)
                        for b in range(B):
                            for k in range(KD):
                                i = mm(bank[:, 2 * (m % 2) + b, 0:NT], w1e[n][:, k, m * P:(m + 1) * P],
                                       xT[:, k, b * NT:(b + 1) * NT], k == 0, k == KD - 1)
                        i.then_inc(s_h1ps, 1)
                    pe.wait_ge(s_y, e + 1)
                    for m in range(MF):
                        pe.wait_ge(s_h1, e * MF + m + 3)
                        for t in range(4):
                            mm(bank[:, 4 + t, 0:D], hT[:, m, cols(t)], w2e[n][:, m, :], m == 0, m == MF - 1)
                    for m in range(MF):
                        i = mm(bank[0:B, 7, 256:256 + D], hT[:, m, cols(4)], w2e[n][:, m, :], m == 0, m == MF - 1)
                    i.then_inc(s_yps, 1)
                    pe.wait_ge(s_yps, e + 1)
                    pe.sem_inc(s_ewf[n], 1)
            transpose_tiles(2)
            pe.wait_ge(s_aw, 32)
            pe.wait_ge(s_xt, 3 * TILES)
            for c in range(KD):
                for b in range(B):
                    for k in range(KD):
                        i = mm(bank[0:KP, 2 * c + b, 0:NT], wq1[:, k, D + c * KP:D + (c + 1) * KP],
                               xT[:, k, b * NT:(b + 1) * NT], k == 0, k == KD - 1)
                i.then_inc(s1_kps, 1)
            for v in range(6):
                if v >= 2:
                    pe.wait_ge(s1_vev, v - 1)
                cs = cols(v) if v < 4 else slice((v - 4) * NT + NP, (v - 3) * NT)
                for k in range(KD):
                    i = mm(bank[0:P if v < 4 else 1, 4 + v % 2, 0:D], xT[:, k, cs], wq1[:, k, 2 * D:3 * D],
                           k == 0, k == KD - 1)
                i.then_inc(s1_vps, 1)
            for c in range(KD):
                for k in range(KD):
                    i = mm(bank[0:KP, 6, c * B:(c + 1) * B], wq1[:, k, c * KP:(c + 1) * KP], xT[:, k, cols(4)],
                           k == 0, k == KD - 1)
            i.then_inc(s1_qcps, 1)
            pe.wait_ge(s1_qm, 1)
            pe.wait_ge(s1_kev, 2)
            for b in range(B):
                for c in range(KD):
                    i = mm(bank[0:NR, 7, 0:NT], QM1[:, c, b * NR:(b + 1) * NR], kT1[:, c, b * NT:(b + 1) * NT],
                           b == 0 and c == 0, b == 1 and c == KD - 1)
            i.then_inc(s1_csc, 1)
            pe.wait_ge(s1_cp, 1)
            for k in range(2):
                nc.tensor.transpose(bank[:, 3, k * NR:(k + 1) * NR], PC1[:, k * P:(k + 1) * P], ident[0:NR, 0:NR])
            nc.tensor.transpose(bank[0:1, 3, 2 * NR:3 * NR], PC1[:, NP:NT], ident[0:NR, 0:NR]).then_inc(s1_ctps, 1)
            pe.wait_ge(s1_ct, 1)
            pe.wait_ge(s1_vev, 6)
            for b in range(B):
                for c in range(KD):
                    o = bank[0:KP, 6, (b * KD + c) * H:(b * KD + c + 1) * H]
                    for k in range(2):
                        mm(o, v1[:, 2 * b + k, c * KP:(c + 1) * KP], PCT[:, k, b * H:(b + 1) * H], k == 0, False)
                    i = mm(o, vc1[0:1, b, c * KP:(c + 1) * KP], PCr[0:1, b * H:(b + 1) * H], False, True)
            i.then_inc(s1_ocps, 1)
            pe.wait_ge(s1_otc, 1)
            with pe.Fori(0, 4) as t:
                b = t // 2
                for c in range(KD):
                    for k in range(KD):
                        i = mm(bank[0:KP, 4, c * P:(c + 1) * P], wq1[:, k, c * KP:(c + 1) * KP],
                               xT[:, k, ds(t * P + b, P)], k == 0, k == KD - 1)
                i.then_inc(s1_qps, 1)
                pe.wait_ge(s1_qz, t + 1)

                def scores(hd):
                    if hd >= 2:
                        pe.wait_ge(s1_exp, t * H + hd - 1)
                    mm(bank[:, hd % 2, 0:NT], qz1[:, hd, :], kTc[:, hd // HPC, :]).then_inc(s1_dps, 1)

                def attend(hd):
                    pe.wait_ge(s1_pt, t * H + hd + 1)
                    pe.wait_ge(s1_ptr, t * H + hd + 1)
                    o, hs = bank[:, 6, hd * HD1:(hd + 1) * HD1], slice(hd * HD1, (hd + 1) * HD1)
                    for k in range(2):
                        mm(o, PT1[:, hd % 2, k, :], vC[:, k, hs], k == 0, False)
                    return mm(o, PTr1[:, hd % 2, :], vcc[0:1, hs], False, True)

                scores(0)
                for hd in range(H):
                    if hd < H - 1:
                        scores(hd + 1)
                    pe.wait_ge(s1_exp, t * H + hd + 1)
                    o = bank[:, 2 + hd % 2, :]
                    for k in range(2):
                        nc.tensor.transpose(o[:, k * P:(k + 1) * P], PR1[:, hd % 2, k * P:(k + 1) * P], ident)
                    nc.tensor.transpose(bank[0:1, 4 + hd % 2, 0:P], PR1[:, hd % 2, NP:NT], ident).then_inc(s1_ptps, 1)
                    if hd:
                        attend(hd - 1)
                attend(H - 1).then_inc(s1_ops, 1)
                pe.wait_ge(s1_o, t + 1)
                for c in range(KD):
                    i = nc.tensor.transpose(bank[0:KP, 7, c * P:(c + 1) * P], O1[:, c * KP:(c + 1) * KP], ident)
                i.then_inc(s1_otps, 1)
            pe.wait_ge(s1_ot, 4)
            for t in range(TILES):
                for k in range(KD):
                    i = mm(bank[0:rows(t), t, 0:D], OT1[:, k, cols(t)], wp1[:, k, :], k == 0, k == KD - 1)
                i.then_inc(s1_prps, 1)
            pe.wait_ge(s2_sl, 1)
            for k in range(KD):
                i = nc.tensor.transpose(bank[0:KP, 5, k * S:(k + 1) * S], slots[:, k * KP:(k + 1) * KP], ident[0:S, 0:S])
            i.then_inc(s2_slps, 1)
            transpose_tiles(3)
            pe.wait_ge(s2_slT, 1)
            pe.wait_ge(s_xt, 4 * TILES)
            for b in range(B):
                for k in range(KD):
                    i = mm(bank[0:S, 6 + b, 0:NT], slT[:, k, :], xT[:, k, b * NT:(b + 1) * NT], k == 0, k == KD - 1)
            i.then_inc(s2_lps, 1)
            for t in range(TILES):
                for k in range(KD):
                    i = mm(bank[0:rows(t), 4, t * S:(t + 1) * S], xT[:, k, cols(t)], slT[:, k, :], k == 0, k == KD - 1)
            i.then_inc(s2_cps, 1)
            pe.wait_ge(s2_d, 1)
            for t in range(4):
                nc.tensor.transpose(bank[:, 5, t * S:(t + 1) * S], Dm[:, t // 2, (t % 2) * P:(t % 2 + 1) * P], ident[0:S, 0:S])
            nc.tensor.transpose(bank[0:B, 5, 4 * S:5 * S], Dm[:, :, NP], ident[0:S, 0:S]).then_inc(s2_dps, 1)
            pe.wait_ge(s2_dt, 1)
            for par in range(2):
                for j in range(3):
                    for b in range(B):
                        o = bank[64 * par:64 * par + 64, 6, (j * B + b) * PAIRS:(j * B + b + 1) * PAIRS]
                        for q in range(2):
                            mm(o, xr[:, 2 * b + q, j:D:3], DT[:, 2 * b + q, par:S:2], q == 0, False)
                        i = mm(o, xr[0:B, 4, j:D:3], DTc[:, b, par:S:2], False, True)
            i.then_inc(s2_yps, 1)
            pe.wait_ge(s2_z, 1)
            for half in range(2):
                for c in range(4):
                    mm(bank[32 * c:32 * c + 32, half, 0:FF // 2], zero, cst[:, 0:FF // 2], True, False, skip_group_check=True)
            with pe.Fori(0, PAIRS // RING) as g:
                pe.wait_ge(s2_yg, g + 1)
                for quad in range(RING // 4):
                    for c in range(4):
                        pe.wait_ge(s_slot[4 * quad + c], 16 * g + 16)
                    for j in range(3):
                        for half in range(2):
                            for c in range(4):
                                n = 4 * quad + c
                                i = mm(bank[32 * c:32 * c + 32, half, 0:FF // 2], YMg[:, n, j, :],
                                       arena[:, n * SLOT + j * FF + half * 384:n * SLOT + j * FF + half * 384 + 384],
                                       False, False, skip_group_check=True)
                                if j == 2 and half == 1:
                                    i.then_inc(s_free[n], 1)
            pe.wait_ge(s2_c, 1)
            for t in range(TILES):
                i = nc.tensor.transpose(bank[:, 4 + t // 4, (t % 4) * P:(t % 4) * P + rows(t)], lgx[0:rows(t), t, :],
                                        ident[0:rows(t), 0:rows(t)])
            i.then_inc(s2_ctps, 1)
            pe.wait_ge(s2_ge, 1)
            for k in range(MF):
                i = nc.tensor.transpose(bank[:, 6 + k // 3, (k % 3) * P:(k % 3 + 1) * P], hrow[:, k * P:(k + 1) * P], ident)
            i.then_inc(s2_htps, 1)
            pe.wait_ge(s2_hs, 1)
            pe.wait_ge(s2_ct, 1)
            with pe.Fori(0, PAIRS // RING) as g:
                pe.wait_ge(s2_mg, g + 1)
                for quad in range(RING // 4):
                    for c in range(4):
                        pe.wait_ge(s_slot[4 * quad + c], 16 * g + 16 * (PAIRS // RING + 1))
                    for odd in range(2):
                        for k in range(MF):
                            for c in range(4):
                                n = 4 * quad + c
                                at = n * SLOT + (odd * MF + k) * D
                                i = mm(bank[32 * c:32 * c + 32, 2 + 2 * quad + odd, 0:D], hT2[:, k, 32 * c:32 * c + 32],
                                       arena[:, at:at + D], k == 0, k == MF - 1)
                                if k == MF - 1 and odd:
                                    i.then_inc(s_free[n], 1)
                        if not odd:
                            i.then_inc(s2_f2, 1)
            pe.wait_ge(s2_y2, 4 * (PAIRS // RING) + 1)
            for t in range(TILES):
                mm(bank[0:rows(t), t if t else 6, 0:D], CT[:, t, 0:rows(t)], Y2).then_inc(s2_ops, 1)

        @block.scalar
        def _(act):
            def copy(o, i, scale=1.0):
                return nc.scalar.activation(o, i, ACT.Copy, scale=scale)

            def deviations(s_):
                act.wait_ge(s_var, s_ + 1)
                nc.scalar.activation(sm[:, 1, :], sm[:, 0, :], ACT.Sqrt).then_inc(s_std, 1)

            def copy_tiles(s_):
                for t in range(TILES):
                    act.wait_ge(s_xtps, s_ * TILES + t + 1)
                    copy(xT[:, :, cols(t)],
                         bank[0:KP, t, 0:KD * P].rearrange("p (k n) -> p k n", k=KD)[:, :, 0:rows(t)]).then_inc(s_xt, 1)

            deviations(0)
            copy_tiles(0)
            for c in range(C0):
                act.wait_ge(s_kps, c + 1)
                copy(kT0[:, c, :].rearrange("p (b n) -> p b n", b=B), bank[:, 2 * (c % 2):2 * (c % 2) + 2, 0:NT]).then_inc(s_kev, 1)
            act.wait_ge(s_ncps, 1)
            copy(negC, bank[0:NR, 1, 0:NT]).then_inc(s_nc, 1)

            def prepare(t, first):
                qb = bank[:, 4:6, 0:3 * P].rearrange("p a (c n) -> p a c n", c=3)
                act.wait_ge(s_qps, t + 1)
                for par in range(2):
                    r = slice(64 * par, 64 * par + 64)
                    for half in range(2):
                        copy(qz0[r, 6 * half + par:6 * half + 6:2, :], bank[r, 4 + half, 0:3 * P].rearrange(
                            "p (c n) -> p c n", c=3))
                for half in range(2):
                    i = copy(qf0[:, 3 * half:3 * half + 3, :],
                             bank[:, 4 + half, 0:3 * P].rearrange("p (c n) -> p c n", c=3), -1.0 / H)
                i.then_inc(s_qev, 1)
                act.wait_ge(s_seps, t + 1)
                if not first:
                    act.wait_ge(s_L, t * H)
                copy(seb, bank[:, 2, 0:NT]).then_inc(s_se, 1)

            def keep(t, hd):
                act.wait_ge(s_dps, t * H + hd + 1)
                copy(neg[:, hd, :], bank[:, hd % 2, 0:NT]).then_inc(s_neg, 1)

            def attend(t, hd):
                n = t * H + hd
                for g in range(2):
                    act.wait_ge(s_xm, n + g + 1)
                    nc.scalar.activation(PR[:, g, :], X[:, g, :], ACT.Exp, bias=nmx[:, g:g + 1],
                                         accum_out=rs[:, hd + g:hd + g + 1]).then_inc(s_exp, 1)
                for g in range(2):
                    act.wait_ge(s_ptps, n + g + 1)
                    if g:
                        act.wait_ge(s_av, n + 1)
                    copy(PT, bank[:, 3, 0:2 * P].rearrange("p (k n) -> p k n", k=2))
                    copy(PTr, bank[0:1, 3, 2 * P:3 * P]).then_inc(s_pt, 1)
                act.wait_ge(s_av, n + 2)
                act.wait_ge(s_rr, t * (H // 2) + hd // 2 + 2)
                for g in range(2):
                    i = nc.scalar.activation(O0[:, (hd + g) * HD0:(hd + g + 1) * HD0], bank[:, 6 + g, 0:HD0], ACT.Copy,
                                             scale=rr[:, hd + g:hd + g + 1])
                if hd == H - 2:
                    i.then_inc(s_o, 1)

            def finish(t):
                act.wait_ge(s_otps, t + 1)
                for half in range(2):
                    i = copy(OT0[:, 3 * half:3 * half + 3, ds(t * P + t // 2, P)],
                             bank[:, 4 + half, 0:3 * P].rearrange("p (c n) -> p c n", c=3))
                i.then_inc(s_ot, 1)

            act.wait_ge(s_qzz, 1)
            prepare(0, True)
            for hd in range(H):
                keep(0, hd)
            act.wait_ge(s_xc, 1)
            nc.scalar.activation(PR[0:NR, 0, :], X[0:NR, 0, :], ACT.Exp, bias=nmx[0:NR, 0:1],
                                 accum_out=gm[0:NR, 6:7]).then_inc(s_pc, 1)
            act.wait_ge(s_pctps, 1)
            copy(PCT[:, :, :], bank[:, 3, 0:2 * NR].rearrange("p (k n) -> p k n", k=2))
            copy(PCr[:, :], bank[0:1, 3, 2 * NR:3 * NR]).then_inc(s_pct, 1)
            act.wait_ge(s_ocps, 1)
            copy(Oc.rearrange("p a b -> p (a b)"), bank[:, 6, 0:B * C0 * H]).then_inc(s_oc, 1)
            act.sem_inc(s_exp, 2)
            with act.Fori(0, 3) as t:
                for hd in range(0, H, 2):
                    if hd == H // 2:
                        prepare(t + 1, False)
                    attend(t, hd)
                    if hd >= H // 2:
                        for g in range(2 * hd - H, 2 * hd - H + 4):
                            keep(t + 1, g)
                finish(t)
            for hd in range(0, H, 2):
                attend(3, hd)
            finish(3)
            deviations(1)
            copy_tiles(1)
            act.wait_ge(s_rsub, 1)
            nc.scalar.activation(lg[:, :, :], lg[:, :, :], ACT.Exp).then_inc(s_rexp, 1)
            act.wait_ge(s_gtps, 1)
            copy(gT[:, 0:4, :].rearrange("p a b -> p (a b)"), bank[0:E, 6, :])
            copy(gT[:, 4, 0:B], bank[0:E, 7, 0:B]).then_inc(s_gt, 1)
            act.wait_ge(s_mw, 48)
            act.sem_inc(s_h1, 2)
            with act.Fori(0, E // 2) as i2:
                for n in range(2):
                    e = 2 * i2 + n
                    copy(b1c[:, n, :], b1e[:, :, ds(e, 1)]).then_inc(s_b1c, 1)
                    for m in range(MF):
                        act.wait_ge(s_h1ps, e * MF + m + 1)
                        if m == 0:
                            act.wait_ge(s_b1c, e + 1)
                        nc.scalar.activation(hT[:, m, :].rearrange("p (b n) -> p b n", b=B),
                                             bank[:, 2 * (m % 2):2 * (m % 2) + 2, 0:NT], ACT.Gelu,
                                             bias=b1c[:, n, m:m + 1]).then_inc(s_h1, 1)
            deviations(2)
            copy_tiles(2)
            for c in range(KD):
                act.wait_ge(s1_kps, c + 1)
                copy(kT1[:, c, :].rearrange("p (b n) -> p b n", b=B), bank[0:KP, 2 * c:2 * c + 2, 0:NT]).then_inc(s1_kev, 1)
            act.wait_ge(s1_cmx, 1)
            nc.scalar.activation(PC1, bank[0:NR, 7, 0:NT], ACT.Exp, bias=nmx[0:NR, 0:1],
                                 accum_out=gm[0:NR, 6:7]).then_inc(s1_cexp, 1)
            act.wait_ge(s1_ctps, 1)
            copy(PCT[:, :, :], bank[:, 3, 0:2 * NR].rearrange("p (k n) -> p k n", k=2))
            copy(PCr[:, :], bank[0:1, 3, 2 * NR:3 * NR]).then_inc(s1_ct, 1)
            with act.Fori(0, 4) as t:
                def exponentials(hd):
                    act.wait_ge(s1_mx, t * H + hd + 1)
                    nc.scalar.activation(PR1[:, hd % 2, :], bank[:, hd % 2, 0:NT], ACT.Exp, bias=nmx[:, hd % 2:hd % 2 + 1],
                                         accum_out=rs[:, hd:hd + 1]).then_inc(s1_exp, 1)
                exponentials(0)
                for hd in range(H):
                    if hd < H - 1:
                        exponentials(hd + 1)
                    act.wait_ge(s1_ptps, t * H + hd + 1)
                    copy(PTr1[:, hd % 2, :], bank[0:1, 4 + hd % 2, 0:P]).then_inc(s1_ptr, 1)
                act.wait_ge(s1_otps, t + 1)
                copy(OT1[:, :, ds(t * P + t // 2, P)],
                     bank[0:KP, 7, 0:KD * P].rearrange("p (k n) -> p k n", k=KD)).then_inc(s1_ot, 1)
            def sum_squares(src, dst, squares):
                return nc.scalar.activation(squares, src, ACT.Square, accum_out=dst)

            act.wait_ge(s_sl, 64)
            sum_squares(slots, sm[0:S, 12, 0:1], junk[:, :]).then_inc(s2_sln, 1)
            act.wait_ge(s2_sln, 1)
            nc.scalar.activation(sm[0:S, 12, 1:2], sm[0:S, 12, 0:1], ACT.Sqrt).then_inc(s2_sln, 1)
            act.wait_ge(s2_slps, 1)
            copy(slT, bank[0:KP, 5, 0:KD * S].rearrange("p (k n) -> p k n", k=KD)).then_inc(s2_slT, 1)
            deviations(3)
            act.wait_ge(s2_u, 1)
            for t in range(TILES):
                i = sum_squares(xn[:, t, :], sm[:, 6, t:t + 1], xr[:, t, :])
            i.then_inc(s2_sq, 1)
            act.wait_ge(s2_ms, 1)
            nc.scalar.activation(sm[:, 7, :], sm[:, 7, :], ACT.Sqrt).then_inc(s2_rms, 1)
            act.wait_ge(s2_xr, 1)
            for t in range(TILES):
                i = sum_squares(xr[:, t, :], sm[:, 9, t:t + 1], hb[:, t, :])
            i.then_inc(s2_nrm, 1)
            act.wait_ge(s2_nrm, 1)
            nc.scalar.activation(sm[:, 10, :], sm[:, 9, :], ACT.Sqrt).then_inc(s2_nrm, 1)
            copy_tiles(3)
            act.wait_ge(s2_mx, 1)
            for b in range(B):
                i = nc.scalar.activation(Dm[:, b, :], bank[0:S, 6 + b, 0:NT], ACT.Exp, bias=nmx[0:S, b:b + 1],
                                         accum_out=rs[0:S, b:b + 1])
            i.then_inc(s2_exp, 1)
            act.wait_ge(s2_csub, 1)
            nc.scalar.activation(lgc, lgc, ACT.Exp).then_inc(s2_cexp, 1)
            act.wait_ge(s2_hb, 1)
            nc.scalar.activation(hrow, hrow, ACT.Gelu).then_inc(s2_ge, 1)
            act.wait_ge(s2_htps, 1)
            copy(hT2.rearrange("p (a c) n -> p a (c n)", a=2), bank[:, 6:8, 0:3 * P]).then_inc(s2_hs, 1)

        @block.vector
        def _(dve):
            ts, tt, stt = nc.vector.tensor_scalar, nc.vector.tensor_tensor, nc.vector.scalar_tensor_tensor
            chain = [0]

            def link(ins):
                chain[0] += 1
                ins.then_inc(s_dve, 1)
                dve.wait_ge(s_dve, chain[0])

            def normalise(s_, done=None):
                for t in range(TILES):
                    i = nc.vector.bn_stats(stats[:, t, :], h[:, t, :])
                link(i)
                for t in range(TILES):
                    i = nc.vector.bn_aggr(mv[:, t, :], stats[:, t, :])
                link(i)
                ts(sm[:, 0, :], mv[:, :, 1], EPS, None, ALU.add).then_inc(s_var, 1)
                dve.wait_ge(s_std, s_ + 1)
                link(nc.vector.reciprocal(sm[:, 2, :], sm[:, 1, :]))
                for t in range(TILES):
                    i = ts(xn[:, t, :], h[:, t, :], mv[:, t, 0:1], sm[:, 2, t:t + 1], ALU.subtract, ALU.mult)
                    if not done:
                        i.then_inc(s_xn, 1)
                if done:
                    i.then_inc(done, 1)
                    dve.wait_ge(done, 1)
                else:
                    dve.wait_ge(s_xn, (s_ + 1) * TILES)

            dve.wait_ge(s_amz, 1)
            dve.wait_ge(s_x, 32)
            nc.vector.tensor_reduce(am[0:KP, 0:1], xp.rearrange("p k n -> p (k n)"), AX.X, ALU.max,
                                    apply_absolute_value=True).then_inc(s_amax, 1)
            nc.vector.tensor_reduce(am[0:KP, 1:2], wt.rearrange("p k n -> p (k n)"), AX.X, ALU.max,
                                    apply_absolute_value=True).then_inc(s_amax, 1)
            dve.wait_ge(s_gmax, 1)
            link(ts(gm[:, 2:4], gm[:, 0:2], 1e-8, 1.0 / QMAX, ALU.max, ALU.mult))
            link(nc.vector.reciprocal(gm[:, 4:6], gm[:, 2:4]))
            link(tt(gm[:, 6:7], gm[:, 2:3], gm[:, 3:4], ALU.mult))
            for n, (src, tmp, dst) in enumerate((
                    (xp.rearrange("p k (a n) -> p k a n", a=2), neg[0:KP, 0:4, 0:NP].rearrange("p (k a) n -> p k a n", a=2),
                     xqb.rearrange("p k (a n) -> p k a n", a=2)),
                    (wt, neg[0:KP, 4:6, 0:D], wqb))):
                link(ts(tmp, src, gm[0:KP, 4 + n:5 + n], QMAX, ALU.mult, ALU.min))
                link(ts(tmp, tmp, -QMAX, MAGIC, ALU.max, ALU.add))
                ts(dst, tmp, MAGIC, None, ALU.subtract).then_inc(s_xq, 1)
            dve.wait_ge(s_cst, 16 * 7)
            for t in range(4):
                dve.wait_ge(s_tokps, t + 1)
                i = stt(h[:, t, :], bank[:, t, 0:D], gm[:, 6:7], rowsb[:, 0, :], ALU.mult, ALU.add)
            dve.wait_ge(s_cls, 16)
            link(i)
            normalise(0)

            dve.wait_ge(s_wq0, 16)
            for k in range(KD):
                i = stt(wq0[:, k, 0:IN0].rearrange("p (h e) -> p h e", h=H),
                        wq0[:, k, 0:IN0].rearrange("p (h e) -> p h e", h=H), -1.0,
                        scb[:, :].unsqueeze(2).to_broadcast([KP, H, HD0]), ALU.mult, ALU.mult)
            i.then_inc(s_wqs, 1)
            for v in range(6):
                dve.wait_ge(s_vps, v + 1)
                src = bank[:, 4 + 2 * (v % 2):6 + 2 * (v % 2), 0:384]
                dst = v0[:, v, :] if v < 4 else vc0[0:1, v - 4, :]
                nc.vector.tensor_copy(dst.rearrange("p (a n) -> p a n", a=2), src if v < 4 else src[0:1]).then_inc(s_vev, 1)
            dve.wait_ge(s_qcps, 1)
            for b in range(B):
                i = tt(QM0[:, :, b * NR:(b + 1) * NR],
                       const("mq0").rearrange("p (c b r) -> p c b r", c=C0, b=B)[:, :, b, :],
                       bank[:, 0, b:C0 * B:B].unsqueeze(2).to_broadcast([P, C0, NR]), ALU.mult)
            i.then_inc(s_qm, 1)

            def drop(p, srcs, early):
                step, lag = 0, len(srcs) - 1
                now = list(srcs)
                for r in range(ROUNDS):
                    for n in range(len(srcs)):
                        if step > lag:
                            dve.wait_ge(s_step, step - lag)
                        nc.vector.max(m8[0:p, n, :], now[n]).then_inc(s_step, 1)
                        step += 1
                    for n in range(len(srcs)):
                        dve.wait_ge(s_step, step - lag)
                        nc.vector.match_replace(W[0:p, n, :], m8[0:p, n, :], now[n], -BIG).then_inc(s_step, 1)
                        now[n] = W[0:p, n, :]
                        step += 1
                    if r == 1 and early:
                        early()
                return step

            def mask(p, logits, step, done):
                lag = len(logits) - 1
                for n, lgt in enumerate(logits):
                    dve.wait_ge(s_step, step - lag)
                    stt(X[0:p, n, :], W[0:p, n, :], THR, lgt, ALU.add, ALU.min).then_inc(s_step, 1)
                    step += 1
                dve.wait_ge(s_step, step)
                dve.sem_clear(s_step)
                for n in range(len(logits)):
                    nc.vector.tensor_reduce(nmx[0:p, n:n + 1], X[0:p, n, :], AX.X, ALU.max,
                                            negate=True).then_inc(done, 1)

            dve.wait_ge(s_nc, 1)
            step = drop(NR, [negC], None)
            dve.wait_ge(s_lc, 1)
            mask(NR, [bank[0:NR, 3, 0:NT]], step, s_xc)
            dve.wait_ge(s_pc, 1)
            link(nc.vector.reciprocal(gm[0:NR, 7:8], gm[0:NR, 6:7]))
            ts(PR[0:NR, 0, :], PR[0:NR, 0, :], gm[0:NR, 7:8], None, ALU.mult).then_inc(s_pcn, 1)
            link(nc.vector.memset(rs[:, H - 2:H], 1.0))

            with dve.Fori(0, 4) as t:
                for hd in range(0, H, 2):
                    n = t * H + hd
                    dve.wait_ge(s_L, n + 2)
                    nc.vector.memset(tick[:, 0:1], 0.0)

                    def reciprocals_before():
                        dve.wait_ge(s_exp, n + 2)
                        g = (hd - 2) % H
                        nc.vector.reciprocal(rr[:, g:g + 2], rs[:, g:g + 2]).then_inc(s_rr, 1)

                    step = drop(P, [neg[:, hd, :], neg[:, hd + 1, :]], reciprocals_before)
                    mask(P, [L[:, hd, :], L[:, hd + 1, :]], step, s_xm)
            dve.wait_ge(s_exp, 4 * H + 2)
            nc.vector.reciprocal(rr[:, H - 2:H], rs[:, H - 2:H]).then_inc(s_rr, 1)
            dve.wait_ge(s_oc, 1)
            link(tt(Oc.rearrange("p (b c) r -> p b c r", b=B)[:, 0], Oc.rearrange("p (b c) r -> p b c r", b=B)[:, 0],
                    const("mo0").rearrange("p (c r) -> p c r", c=C0), ALU.mult))
            link(tt(Oc.rearrange("p (b c) r -> p b c r", b=B)[:, 1], Oc.rearrange("p (b c) r -> p b c r", b=B)[:, 1],
                    const("mo0").rearrange("p (c r) -> p c r", c=C0), ALU.mult))
            for b in range(B):
                i = nc.vector.tensor_reduce(OT0[:, :, b * NT + NP:b * NT + NP + 1],
                                            Oc.rearrange("p (b c) r -> p b c r", b=B)[:, b], AX.X, ALU.add)
            i.then_inc(s_otc, 1)
            for t in range(TILES):
                i = tt(hb[:, t, :], h[:, t, :], rowsb[:, 1, :], ALU.add)
            link(i)
            for t in range(TILES):
                dve.wait_ge(s_prps, t + 1)
                i = tt(h[0:rows(t), t, :], bank[0:rows(t), t, 0:D], hb[0:rows(t), t, :], ALU.add)
            link(i)
            normalise(1)
            link(nc.vector.memset(lg[:, TILES - 1, :], 0.0))
            dve.wait_ge(s_rps, 1)
            nc.vector.tensor_copy(lg[:, 0:4, :], bank[:, 5, 0:4 * E].rearrange("p (t e) -> p t e", e=E))
            link(nc.vector.tensor_copy(lg[0:B, 4, :], bank[0:B, 5, 4 * E:5 * E]))
            link(nc.vector.tensor_reduce(sm[:, 3, :], lg[:, :, :], AX.X, ALU.max))
            tt(lg[:, :, :], lg[:, :, :], sm[:, 3, :].unsqueeze(2).to_broadcast([P, TILES, E]),
               ALU.subtract).then_inc(s_rsub, 1)
            dve.wait_ge(s_rexp, 1)
            link(nc.vector.tensor_reduce(sm[:, 4, :], lg[:, :, :], AX.X, ALU.add))
            link(nc.vector.reciprocal(sm[:, 5, :], sm[:, 4, :]))
            link(tt(lg[:, :, :], lg[:, :, :], sm[:, 5, :].unsqueeze(2).to_broadcast([P, TILES, E]), ALU.mult))
            for t in range(TILES):
                i = nc.vector.max(top[:, t, :], lg[:, t, :])
            link(i)
            for t in range(TILES):
                i = nc.vector.max_index(topi[:, t, :], top[:, t, :], lg[:, t, :])
            link(i)
            link(nc.vector.tensor_copy(topf[:, :, :], topi[:, :, :]))
            for t in range(TILES):
                ts(gate[:, t, :], const("iota"), topf[:, t, 0:1], top[:, t, 0:1], ALU.is_equal, ALU.mult)
                i = ts(gate2[:, t, :], const("iota"), topf[:, t, 1:2], top[:, t, 1:2], ALU.is_equal, ALU.mult)
            link(i)
            tt(gate[:, :, :], gate[:, :, :], gate2[:, :, :], ALU.add).then_inc(s_gate, 1)
            link(tt(h[:, :, :], h[:, :, :], xn[:, :, :], ALU.add))
            dve.wait_ge(s_gbps, 1)
            for t in range(TILES):
                i = tt(h[0:rows(t), t, :], bank[0:rows(t), t, 0:D], h[0:rows(t), t, :], ALU.add)
            i.then_inc(s_y, 1)
            dve.wait_ge(s_y, 1)
            with dve.Fori(0, E // 2) as i2:
                for n in range(2):
                    e = 2 * i2 + n
                    nc.vector.tensor_copy(gcol[:, n, :], gate[:, :, ds(e, 1)]).then_inc(s_gc, 1)
                    dve.wait_ge(s_gc, e + 1)
                    dve.wait_ge(s_yps, e + 1)
                    for t in range(TILES):
                        src = bank[:, 4 + t, 0:D] if t < 4 else bank[0:B, 7, 256:256 + D]
                        i = stt(h[0:rows(t), t, :], src, gcol[0:rows(t), n, t:t + 1], h[0:rows(t), t, :],
                                ALU.mult, ALU.add)
                    i.then_inc(s_y, 1)
                    dve.wait_ge(s_y, e + 2)
            normalise(2)
            for v in range(6):
                dve.wait_ge(s1_vps, v + 1)
                dst = v1[:, v, :] if v < 4 else vc1[0:1, v - 4, :]
                nc.vector.tensor_copy(dst, bank[0:P if v < 4 else 1, 4 + v % 2, 0:D]).then_inc(s1_vev, 1)
            dve.wait_ge(s1_qcps, 1)
            for b in range(B):
                i = tt(QM1[:, :, b * NR:(b + 1) * NR],
                       const("mq1", KP).rearrange("p (c b r) -> p c b r", c=KD, b=B)[:, :, b, :],
                       bank[0:KP, 6, b:KD * B:B].unsqueeze(2).to_broadcast([KP, KD, NR]), ALU.mult)
            i.then_inc(s1_qm, 1)
            dve.wait_ge(s1_csc, 1)
            nc.vector.tensor_reduce(nmx[0:NR, 0:1], bank[0:NR, 7, 0:NT], AX.X, ALU.max, negate=True).then_inc(s1_cmx, 1)
            dve.wait_ge(s1_cexp, 1)
            link(nc.vector.reciprocal(gm[0:NR, 7:8], gm[0:NR, 6:7]))
            ts(PC1, PC1, gm[0:NR, 7:8], None, ALU.mult).then_inc(s1_cp, 1)
            dve.wait_ge(s1_ocps, 1)
            for b in range(B):
                i = tt(Oc1[:, b * KD * H:(b + 1) * KD * H], bank[0:KP, 6, b * KD * H:(b + 1) * KD * H],
                       const("mo1", KP), ALU.mult)
            link(i)
            for b in range(B):
                i = nc.vector.tensor_reduce(OT1[:, :, b * NT + NP:b * NT + NP + 1],
                                            Oc1[:, b * KD * H:(b + 1) * KD * H].rearrange("p (c r) -> p c r", c=KD),
                                            AX.X, ALU.add)
            i.then_inc(s1_otc, 1)
            dve.wait_ge(s1_kev, 2)
            with dve.Fori(0, 4) as t:
                dve.wait_ge(s1_qps, t + 1)
                nc.vector.tensor_copy(kTc, kT1[:, :, ds((t // 2) * NT, NT)])
                nc.vector.tensor_copy(vC, v1[:, ds((t // 2) * 2, 2), :])
                nc.vector.tensor_copy(vcc, vc1[0:1, ds(t // 2, 1), :].rearrange("p a n -> p (a n)"))
                for c in range(KD):
                    i = tt(qz1[:, c * HPC:(c + 1) * HPC, :],
                           bank[0:KP, 4, c * P:(c + 1) * P].unsqueeze(1).to_broadcast([KP, HPC, P]),
                           const("mz1", KP).unsqueeze(2).to_broadcast([KP, HPC, P]), ALU.mult)
                i.then_inc(s1_qz, 1)

                def maximum(hd):
                    dve.wait_ge(s1_dps, t * H + hd + 1)
                    nc.vector.tensor_reduce(nmx[:, hd % 2:hd % 2 + 1], bank[:, hd % 2, 0:NT], AX.X, ALU.max,
                                            negate=True).then_inc(s1_mx, 1)
                maximum(0)
                for hd in range(H):
                    if hd < H - 1:
                        maximum(hd + 1)
                    dve.wait_ge(s1_ptps, t * H + hd + 1)
                    nc.vector.tensor_copy(PT1[:, hd % 2], bank[:, 2 + hd % 2, 0:2 * P].rearrange(
                        "p (k n) -> p k n", k=2)).then_inc(s1_pt, 1)
                dve.wait_ge(s1_ops, t + 1)
                nc.vector.reciprocal(rr[:, :], rs[:, :]).then_inc(s_rr, 1)
                dve.wait_ge(s_rr, t + 1 + 2 * H + 1)
                tt(O1.rearrange("p (h e) -> p h e", h=H), bank[:, 6, 0:D].rearrange("p (h e) -> p h e", h=H),
                   rr[:, :].unsqueeze(2).to_broadcast([P, H, HD1]), ALU.mult).then_inc(s1_o, 1)
            for t in range(TILES):
                i = tt(hb[:, t, :], h[:, t, :], rowsb[:, 2, :], ALU.add)
            link(i)
            for t in range(TILES):
                dve.wait_ge(s1_prps, t + 1)
                i = tt(h[0:rows(t), t, :], bank[0:rows(t), t, 0:D], hb[0:rows(t), t, :], ALU.add)
            link(i)
            dve.wait_ge(s2_sln, 2)
            link(ts(sm[0:S, 12, 2:3], sm[0:S, 12, 1:2], EPS, None, ALU.max))
            link(nc.vector.reciprocal(sm[0:S, 12, 3:4], sm[0:S, 12, 2:3]))
            ts(slots, slots, sm[0:S, 12, 3:4], slscale, ALU.mult, ALU.mult).then_inc(s2_sl, 1)
            normalise(3, s2_u)
            dve.wait_ge(s2_sq, 1)
            ts(sm[:, 7, :], sm[:, 6, :], 1.0 / D, EPS, ALU.mult, ALU.add).then_inc(s2_ms, 1)
            dve.wait_ge(s2_rms, 1)
            link(nc.vector.reciprocal(sm[:, 8, :], sm[:, 7, :]))
            for t in range(TILES):
                i = stt(xr[:, t, :], xn[:, t, :], sm[:, 8, t:t + 1], rowsb[:, 3, :], ALU.mult, ALU.mult)
            i.then_inc(s2_xr, 1)
            dve.wait_ge(s2_xr, 1)
            dve.wait_ge(s2_nrm, 2)
            link(ts(sm[:, 10, :], sm[:, 10, :], EPS, None, ALU.max))
            link(nc.vector.reciprocal(sm[:, 11, :], sm[:, 10, :]))
            for t in range(TILES):
                ts(xn[:, t, :], xr[:, t, :], sm[:, 11, t:t + 1], None, ALU.mult).then_inc(s_xn, 1)
            link(nc.vector.memset(YM, 0.0))
            link(nc.vector.memset(lgc[:, TILES - 1, :], 0.0))
            link(nc.vector.memset(lgx, 0.0))
            nc.vector.memset(zero, 0.0).then_inc(s2_z, 1)
            dve.wait_ge(s2_lps, 1)
            nc.vector.tensor_reduce(nmx[0:S, 0:B], bank[0:S, 6:8, 0:NT], AX.X, ALU.max, negate=True).then_inc(s2_mx, 1)
            dve.wait_ge(s2_exp, 1)
            link(nc.vector.reciprocal(rr[0:S, 0:B], rs[0:S, 0:B]))
            for b in range(B):
                i = ts(Dm[:, b, :], Dm[:, b, :], rr[0:S, b:b + 1], None, ALU.mult)
            i.then_inc(s2_d, 1)
            dve.wait_ge(s2_dps, 1)
            nc.vector.tensor_copy(DT.rearrange("p a b -> p (a b)"), bank[:, 5, 0:4 * S])
            for b in range(B):
                i = ts(DTc[:, b, :], bank[0:B, 5, 4 * S:5 * S], cst[0:B, CST["eye2"][0] + b:CST["eye2"][0] + b + 1],
                       None, ALU.mult)
            i.then_inc(s2_dt, 1)
            dve.wait_ge(s2_yps, 1)
            for par in range(2):
                r = slice(64 * par, 64 * par + 64)
                for i8 in range(PAIRS // 4):
                    i = nc.vector.tensor_copy(
                        YM[r, 4 * i8:4 * i8 + 4, :, 4 * i8 + 2 * par:4 * i8 + 2 * par + 2],
                        bank[r, 6, 0:3 * B * PAIRS].rearrange("p (j b s) -> p s j b", j=3, b=B)[:, 4 * i8:4 * i8 + 4])
            link(i)
            def stage(g):
                nc.vector.tensor_copy(YMg.rearrange("p a j n -> p (a j n)"),
                                      YM[:, ds(RING * g, RING)].rearrange("p a j n -> p (a j n)")).then_inc(s2_yg, 1)
            stage(0)
            dve.wait_ge(s2_cps, 1)
            nc.vector.tensor_copy(lgc[:, 0:4, :], bank[:, 4, 0:4 * S].rearrange("p (t s) -> p t s", t=4))
            link(nc.vector.tensor_copy(lgc[0:B, 4, :], bank[0:B, 4, 4 * S:5 * S]))
            link(nc.vector.tensor_reduce(sm[:, 13, :], lgc, AX.X, ALU.max))
            tt(lgc, lgc, sm[:, 13, :].unsqueeze(2).to_broadcast([P, TILES, S]), ALU.subtract).then_inc(s2_csub, 1)
            dve.wait_ge(s2_cexp, 1)
            link(nc.vector.tensor_reduce(sm[:, 14, :], lgc, AX.X, ALU.add))
            link(nc.vector.reciprocal(sm[:, 15, :], sm[:, 14, :]))
            link(tt(lgc, lgc, sm[:, 15, :].unsqueeze(2).to_broadcast([P, TILES, S]), ALU.mult))

            def by_row(x, p, t, b):
                return x[0:p, t, :].rearrange("p (c i o b) -> p c i o b", c=4, o=2, b=B)[:, :, :, :, b]

            def by_slot(x, p, t):
                return x[0:p, t, :].rearrange("p (i c o) -> p c i o", c=4, o=2)
            for t in range(4):
                nc.vector.tensor_copy(by_row(lgx, P, t, t // 2), by_slot(lgc, P, t))
            for b in range(B):
                i = ts(by_row(lgx, B, 4, b), by_slot(lgc, B, 4), cst[0:B, CST["eye2"][0] + b:CST["eye2"][0] + b + 1],
                       None, ALU.mult)
            i.then_inc(s2_c, 1)
            with dve.Fori(1, PAIRS // RING) as g:
                dve.wait_ge(s_free[RING - 1], g)
                stage(g)
            dve.wait_ge(s2_ctps, 1)
            nc.vector.tensor_copy(CT[:, 0:4, :].rearrange("p a b -> p (a b)"), bank[:, 4, :])
            nc.vector.tensor_copy(CT[:, 4, 0:B], bank[:, 5, 0:B]).then_inc(s2_ct, 1)
            dve.wait_ge(s_free[RING - 1], PAIRS // RING)
            tt(hrow.rearrange("p (a n) -> p a n", a=2), bank[:, 0:2, 0:FF // 2], b1R.rearrange("p (a n) -> p a n", a=2),
               ALU.add).then_inc(s2_hb, 1)
            nc.vector.tensor_copy(Y2, b2R).then_inc(s2_y2, 1)
            with dve.Fori(0, PAIRS // RING) as g:
                dve.wait_ge(s2_y2, 4 * g + 1)
                nc.vector.tensor_copy(mcol, cst[:, ds(CST["m16"][0] + 4 * g, 4)]).then_inc(s2_mg, 1)
                dve.wait_ge(s2_mg, g + 1)
                for n in range(4):
                    if n % 2:
                        dve.wait_ge(s_free[2 * n + 1], g + PAIRS // RING + 1)
                    else:
                        dve.wait_ge(s2_f2, 2 * g + n // 2 + 1)
                    if n:
                        dve.wait_ge(s2_y2, 4 * g + n + 1)
                    stt(Y2, bank[:, 2 + n, 0:D], mcol[:, n:n + 1], Y2, ALU.mult, ALU.add).then_inc(s2_y2, 1)
            for t in range(TILES):
                dve.wait_ge(s2_ops, t + 1)
                tt(h[0:rows(t), t, :], bank[0:rows(t), t if t else 6, 0:D], h[0:rows(t), t, :], ALU.add).then_inc(s_final, 1)


def kernel(**inputs):
    import concourse.bacc as bacc
    from concourse.bass_utils import run_bass_kernel_spmd

    x = {k: np.asarray(v) for k, v in inputs.items()}
    patch = D // 3
    side = int(patch ** 0.5)
    xp = x["x"].reshape(B, 3, GRID, side, GRID, side).transpose(1, 3, 5, 0, 2, 4).reshape(D, B, NP)[:, :, ::-1]
    chunk = lambda m: m.reshape(KD, KP, -1).transpose(1, 0, 2)
    cst = np.zeros((P, CST_W), np.float32)

    def put(name, v):
        lo, hi = CST[name]
        cst[:v.shape[0], lo:hi] = v.reshape(v.shape[0], -1)

    p, p1 = np.arange(P), np.arange(KP)
    put("ident", np.eye(P))
    m = np.zeros((P, C0, B, NR))
    mo = np.zeros((P, C0, H))
    for c in range(C0):
        for b in range(B):
            m[p, c, b, b * H + 2 * c + p // HD0] = 1
        mo[p, c, 2 * c + p // HD0] = 1
    put("mq0", m)
    put("mo0", mo)
    m = np.zeros((KP, KD, B, NR))
    mo = np.zeros((KP, KD, H))
    for c in range(KD):
        for b in range(B):
            m[p1, c, b, b * H + HPC * c + p1 // HD1] = HD1 ** -0.5
        mo[p1, c, HPC * c + p1 // HD1] = 1
    put("mq1", m)
    put("mo1", mo)
    m = np.zeros((KP, HPC))
    m[p1, p1 // HD1] = HD1 ** -0.5
    put("mz1", m)
    put("nb", -(np.eye(NR) + np.kron(np.eye(B), np.ones((H, H))) / H))
    put("iota", np.tile(np.arange(E), (P, 1)))
    put("eye2", np.eye(B))
    quarter, i8, odd = p // 32, p % 32 // 4, p % 4 // 2
    slot_of_row = 8 * i8 + 2 * quarter + odd
    m = np.zeros((P, 16))
    m[p, 2 * i8 + odd] = 1
    put("m16", m)
    bf = mybir.dt.np(BF16)
    cstb = np.zeros((P, CSTB_W), np.float32)
    cstb[:, 0:P] = np.eye(P)
    cstb[p, CSTB["bigd"][0] + P + p] = -BIG
    cstb[:, CSTB["bigc"][0] + NP] = -BIG
    arrays = {
        "xp": chunk(xp.reshape(D, B * NP)), "wt": chunk(x["L0_tok_w"].reshape(D, D).T),
        "cst": cst, "cstb": cstb.astype(bf),
        "tok_b": x["L0_tok_b"], "b_out": x["L0_attn_b_out"], "b_proj": x["L1_attn_b_proj"],
        "norm_w": x["L1_ffn_norm_weight"], "scale0": x["L0_attn_scale"],
        "cls": x["cls_tok"].reshape(D), "wqkv0": x["L0_attn_w_qkv"], "wo0": x["L0_attn_w_out"],
        "wqkv1": chunk(x["L1_attn_w_qkv"].T), "wp1": chunk(x["L1_attn_w_proj"].T),
        "slots": x["L1_ffn_slots"], "slot_scale": x["L1_ffn_scale"].reshape(S, 1),
        "fc1": x["L1_ffn_fc1_weight"], "fc2": x["L1_ffn_fc2_weight"],
        "b1R": x["L1_ffn_fc1_bias"][slot_of_row], "b2R": x["L1_ffn_fc2_bias"][slot_of_row],
        "wr": chunk(x["L0_ffn_Wr"].T), "w1e": x["L0_ffn_W1"], "w2e": x["L0_ffn_W2"], "b2e": x["L0_ffn_b2"],
        "b1e": x["L0_ffn_b1"].reshape(E, MF, P).transpose(2, 1, 0),
    }
    nc = bacc.Bacc("TRN2", target_bir_lowering=False, num_devices=1)
    arrays = {k: np.ascontiguousarray(v) for k, v in arrays.items()}
    aps = {k: nc.dram_tensor(f"in_{k}", v.shape, mybir.dt.from_np(v.dtype), kind="ExternalInput").ap()
           for k, v in arrays.items()}
    aps["out"] = nc.dram_tensor("out", (B * NT, D), F32, kind="ExternalOutput").ap()
    vit_tower(nc, aps)
    r = run_bass_kernel_spmd(nc, [{f"in_{k}": v for k, v in arrays.items()}], core_ids=[0])
    got = r.results[0]["out"]
    patches = got[:B * NP].reshape(B, NP, D)[:, ::-1]
    return np.ascontiguousarray(np.concatenate([got[B * NP:].reshape(B, 1, D), patches], axis=1))
```

```python
import concourse.bass as bass
from concourse import mybir
from contextlib import ExitStack
import numpy as np

F32 = mybir.dt.float32
BF16 = mybir.dt.bfloat16
U32 = mybir.dt.uint32
ALU = mybir.AluOpType
ACT = mybir.ActivationFunctionType
AX = mybir.AxisListType
RMAX = bass.bass_isa.ReduceOp.max
ds = bass.ds

P = 128
B = 2
GRID = 16
NP = GRID * GRID
NT = NP + 1
D = 192
KP = 96
KD = D // KP
H = 12
HD0, HD1 = 64, 16
IN0 = H * HD0
C0 = IN0 // P
HPC = KP // HD1
NR = B * H
DROP = NT - int(NT * 0.75) - 1
ROUNDS = DROP // 8
E, FF = 16, 768
MF = FF // P
S = 64
PAIRS = S // 2
TILES = 5
BIG = 2.0 ** 126
THR = 1e30
MAGIC = 12582912.0
QMAX = 127.0
EPS = 1e-5
TOPK = 2
MT = (TOPK * B * NT + E * (P - 1)) // P
NB = 4
RING = 8
SLOT = 3 * FF

CST = {}
_at = 0
for _name, _w in (("ident", P), ("mq0", C0 * B * H * B), ("mo0", C0 * H), ("mz1", HPC), ("mq1", KD * B * NR),
                  ("mo1", KD * H), ("nb", NR), ("iota", E), ("eye2", B), ("m16", 16),
                  ("below", P), ("ones", P), ("fill", TILES), ("upto", E * E), ("tile", MT)):
    CST[_name] = (_at, _at + _w)
    _at += _w
CST_W = _at
CSTB = {"identb": (0, P), "bigd": (P, P + NP + P + 1), "bigc": (2 * P + NP + 1, 2 * P + NP + 1 + NT)}
CSTB_W = 2 * P + NP + 1 + NT


def rows(t):
    return P if t < TILES - 1 else B


def cols(t):
    if t == TILES - 1:
        return slice(NP, B * NT, NT)
    a = (t // 2) * NT + (t % 2) * P
    return slice(a, a + P)


def vit_tower(nc, a):
    out = a["out"]
    xs = nc.dram_tensor("expert_rows", (MT * P, D), F32).ap()
    ys = nc.dram_tensor("expert_out", (MT * P, D), F32).ap()
    with ExitStack() as ctx:
        def sb(name, shape, dt=F32):
            return ctx.enter_context(nc.sbuf_tensor(name, shape, dt))

        def sem(name):
            return ctx.enter_context(nc.semaphore(name))

        cst = sb("cst", [P, CST_W])
        cstb = sb("cstb", [P, CSTB_W], BF16)

        def const(name, p=P):
            lo, hi = CST[name]
            return cst[0:p, lo:hi]

        ident = const("ident")
        identb = cstb[:, 0:P]
        bigd = cstb[:, CSTB["bigd"][0]:CSTB["bigd"][1]]
        bigc = cstb[0:NR, CSTB["bigc"][0]:CSTB["bigc"][1]]

        h = sb("h", [P, TILES, D])
        hb = sb("hb", [P, TILES, D])
        xn = sb("xn", [P, TILES, D])
        xT = sb("xT", [KP, KD, B * NT])
        rowsb = sb("rowsb", [P, 4, D])
        stats = sb("stats", [P, TILES, 6])
        mv = sb("mv", [P, TILES, 2])
        sm = sb("sm", [P, 16, TILES])
        NEGB = RING * SLOT
        arena = sb("arena", [P, NEGB])

        class Cut:
            at = 0

        def take(p, *shape):
            n = 1
            for s_ in shape:
                n *= s_
            v = arena[0:p, Cut.at:Cut.at + n]
            Cut.at += n
            assert Cut.at <= NEGB
            if len(shape) == 1:
                return v
            names = "abc"[:len(shape)]
            return v.rearrange("p (%s) -> p %s" % (" ".join(names), " ".join(names)),
                               **{k: s_ for k, s_ in zip(names, shape)})

        wq0 = sb("wq0", [KP, KD, 3 * IN0])
        kT0 = take(P, C0, B * NT)
        qz0 = take(P, H, P)
        qf0 = take(P, C0, P)
        W = take(P, 2, NT)
        X = take(P, 2, NT)
        PR = take(P, 2, NT)
        PT = take(P, 2, P)
        PTr = take(1, P)
        O0 = take(P, IN0)
        seb = take(P, NT)
        negC = take(NR, NT)
        Oc = take(P, B * C0, H)
        L = sb("L", [P, H, NT])
        neg = sb("neg", [P, H, NT])
        OT0 = sb("OT0", [P, C0, B * NT])
        v0 = sb("v0", [P, 4, IN0])
        vc0 = sb("vc0", [1, B, IN0])
        wo0 = sb("wo0", [P, C0, D])
        QM0 = sb("QM0", [P, C0, B * NR])
        PCT = sb("PCT", [P, 2, NR])
        PCr = sb("PCr", [1, NR])
        m8 = sb("m8", [P, 2, 8])
        tick = sb("tick", [P, 8])
        nmx = sb("nmx", [P, 2])
        rs = sb("rs", [P, H])
        rr = sb("rr", [P, H])
        scb = sb("scb", [KP, H])
        junk = sb("junk", [S, D])

        wr = sb("wr", [KP, KD, E])
        lg = sb("lg", [P, TILES, E])
        gate = sb("gate", [P, TILES, E])
        gate2 = sb("gate2", [P, TILES, E])
        top = sb("top", [P, TILES, 8])
        topi = sb("topi", [P, TILES, 8], U32)
        topf = sb("topf", [P, TILES, 8])
        gT = sb("gT", [E, TILES, P])
        b2e = sb("b2e", [E, D])
        flat = lambda buf: buf[:, :, :].rearrange("p a b -> p (a b)")
        w1e = [flat(buf)[0:KP, n * KD * FF:(n + 1) * KD * FF].rearrange("p (k f) -> p k f", k=KD)
               for buf in (v0, L) for n in range(2)]
        w2a = [sb(f"w2e{n}", [P, MF, D]) for n in range(2)]
        w2e = [w2a[0][:, :, :], w2a[1][:, :, :]] + [
            flat(neg)[:, n * MF * D:(n + 1) * MF * D].rearrange("p (m d) -> p m d", m=MF) for n in range(2)]
        yt = [flat(neg)[:, 2 * MF * D + n * D:2 * MF * D + (n + 1) * D] for n in range(NB)]
        hT = [flat(OT0)[:, n * MF * P:(n + 1) * MF * P].rearrange("p (m n) -> p m n", m=MF) for n in range(2)]
        xg = [flat(OT0)[:, 2 * MF * P + n * D:2 * MF * P + (n + 1) * D] for n in range(NB)]
        xgT = [flat(OT0)[0:KP, 2 * MF * P + NB * D + n * KD * P:2 * MF * P + NB * D + (n + 1) * KD * P].rearrange(
            "p (k n) -> p k n", k=KD) for n in range(2)]
        b1c = sb("b1c", [P, NB, MF])
        yg = flat(L)[:, 0:TILES * TOPK * D].rearrange("p (t k d) -> p t k d", t=TILES, k=TOPK)
        oh = sb("oh", [P, TOPK, TILES, E])
        ohs = sb("ohs", [P, TILES, E])
        rank = sb("rank", [P, TILES, E])
        prod = sb("prod", [P, TOPK, TILES, E])
        filled = sb("filled", [P, E, TILES])
        ntile = sb("ntile", [P, E])
        upto = sb("upto", [P, E, E])
        ends = sb("ends", [P, E])
        base = sb("base", [P, E])
        posf = sb("posf", [P, TOPK, TILES])
        posi = sb("posi", [P, TOPK, TILES], U32)
        past = sb("past", [1, MT, E])
        eidf = sb("eidf", [1, MT])
        eid = sb("eid", [1, MT], U32)

        wq0f = wq0[:, :, :].rearrange("p a b -> p (a b)")
        wq1 = wq0f[:, 0:KD * 3 * D].rearrange("p (k n) -> p k n", k=KD)
        wp1 = wq0f[:, 1152:1152 + KD * D].rearrange("p (k n) -> p k n", k=KD)
        kT1 = wq0f[:, 1536:1536 + KD * B * NT].rearrange("p (k n) -> p k n", k=KD)
        OT1 = wq0f[:, 2564:2564 + KD * B * NT].rearrange("p (k n) -> p k n", k=KD)
        v1 = sb("v1", [P, 4, D])
        vc1 = sb("vc1", [P, B, D])
        QM1 = sb("QM1", [KP, KD, B * NR])
        qz1 = L[0:KP, :, 0:P]
        PR1 = neg
        v0f = v0[:, :, :].rearrange("p a b -> p (a b)")
        PT1 = v0f[:, 0:4 * 2 * P].rearrange("p (g h k n) -> p g h k n", g=2, h=2, k=2)
        O1 = v0f[:, 1024:1024 + D]
        OR1 = v0f[:, 1216:1216 + D]
        Oc1 = v0f[0:KP, 1408:1408 + B * KD * H]
        PC1 = v0f[0:NR, 1456:1456 + NT]
        xc1 = v0f[0:KP, 1714:1714 + KD * B * P].rearrange("p (k b n) -> p k b n", k=KD, b=B)
        nmx1 = v0f[:, 2226:2230].rearrange("p (g h) -> p g h", g=2)
        kTc = v0f[0:KP, 2230:2230 + KD * NT].rearrange("p (k n) -> p k n", k=KD)
        vC = w2a[0][:, 0:2, :]

        def carve(buf):
            flat, at = buf[:, :, :].rearrange("p a b -> p (a b)"), [0]

            def cut(p, *shape):
                n = int(np.prod(shape))
                v = flat[0:p, at[0]:at[0] + n]
                at[0] += n
                assert at[0] <= flat.shape[1]
                names = "abc"[:len(shape)]
                if len(shape) == 1:
                    return v
                return v.rearrange("p (%s) -> p %s" % (" ".join(names), " ".join(names)), **dict(zip(names, shape)))
            return cut

        cut = carve(neg)
        YM = cut(P, PAIRS, 3, 32)
        cut = carve(L)
        hrow = cut(P, FF)
        hT2 = cut(P, MF, P)
        lgc = cut(P, TILES, S)
        lgx = cut(P, TILES, P)
        Y2 = cut(P, D)
        cut = carve(OT0)
        slots = cut(S, D)
        slscale = cut(S, 1)
        b1R = cut(P, FF)
        b2R = cut(P, D)
        xr = cut(P, TILES, D)
        DT = cut(P, 4, S)
        DTc = cut(B, B, S)
        Dm = cut(S, B, NT)
        cut = carve(v0)
        CT = cut(P, TILES, P)
        slT = cut(KP, KD, S)
        YMg = cut(P, RING, 3, 32)
        mcol = cut(P, 4)
        zero = cut(P, 32)

        s_cst = sem("constants_landed")
        s_x = sem("patches_landed")
        s_wq0 = sem("attn0_weights_landed")
        s_wo0 = sem("attn0_out_weights_landed")
        s_hz = sem("residual_cleared")
        s_cls = sem("class_rows_landed")
        s_dve = sem("vector_chain")
        s_amax = sem("absmax_of_partitions")
        s_gmax = sem("absmax_of_all")
        s_xq = sem("quantized")
        s_tokps = sem("tokens_in_psum")
        s_var = sem("variances_ready")
        s_std = sem("deviations_ready")
        s_xn = sem("normalised_tiles")
        s_xtps = sem("transposed_tiles_in_psum")
        s_xt = sem("transposed_tiles")
        s_out = sem("stored")
        s_final = sem("result_ready")
        s_amz = sem("absmax_cleared")
        s_qzz = sem("spread_queries_cleared")

        xp = wq0[:, 0, 0:KD * B * NP].rearrange("p (k n) -> p k n", k=KD)
        wt = wq0[:, 1, 0:KD * D].rearrange("p (k n) -> p k n", k=KD)
        xqb = OT0[0:KP, 0:2, 0:NP].bitcast(BF16)
        wqb = OT0[0:KP, 2:4, 0:D // 2].bitcast(BF16)
        am = sb("am", [P, 2])
        gm = sb("gm", [P, 8])

        bank = ctx.enter_context(nc.psum_tensor("bank", [P, 8, 512], F32))

        block = ctx.enter_context(nc.Block())

        s_kps, s_kev = sem("keys0_in_psum"), sem("keys0_ready")
        s_vps, s_vev = sem("values0_in_psum"), sem("values0_ready")
        s_wqs = sem("query_weights_scaled")
        s_qcps, s_qm = sem("class_queries_in_psum"), sem("class_queries_spread")
        s_ncps, s_nc = sem("class_scores_in_psum"), sem("class_scores_ready")
        s_lc = sem("class_logits_in_psum")
        s_xc, s_pc, s_pcn = sem("class_masked"), sem("class_exp"), sem("class_probs")
        s_pctps, s_pct = sem("class_probsT_in_psum"), sem("class_probsT")
        s_ocps, s_oc = sem("class_out_in_psum"), sem("class_out_copied")
        s_qps, s_qev = sem("queries_in_psum"), sem("queries_ready")
        s_seps, s_se = sem("mean_scores_in_psum"), sem("mean_scores_ready")
        s_dps, s_neg = sem("scores_in_psum"), sem("scores_ready")
        s_L = sem("logits_ready")
        s_step = sem("topk_step")
        s_xm = sem("masked_logits_ready")
        s_exp = sem("exp_done_plus_two")
        s_rr = sem("row_reciprocals")
        s_ptps, s_pt = sem("probsT_in_psum"), sem("probsT_ready")
        s_av = sem("head_out_in_psum")
        s_o = sem("tile_out_ready")
        s_otps, s_ot = sem("tile_outT_in_psum"), sem("tile_outT_ready")
        s_otc = sem("class_outT_ready")
        s_prps = sem("projection0_in_psum")
        s_mw = sem("router_weights_landed")
        s_rps = sem("router_logits_in_psum")
        s_rsub, s_rexp = sem("router_logits_shifted"), sem("router_exp_ready")
        s_gate = sem("gates_ready")
        s_gtps, s_gt = sem("gatesT_in_psum"), sem("gatesT_ready")
        s_gbps = sem("gated_bias_in_psum")
        s_hzb, s_xz = sem("zero_tile_ready"), sem("expert_rows_cleared")
        s_msk, s_rkps = sem("expert_choices_ready"), sem("expert_ranks_in_psum")
        s_eid, s_pos = sem("tile_experts_ready"), sem("row_positions_ready")
        s_scat = sem("tokens_scattered")
        s_ew = [sem(f"expert_tile_landed_{n}") for n in range(NB)]
        s_gxps, s_gx = sem("tile_tokensT_in_psum"), sem("tile_tokensT_ready")
        s_h1ps, s_h1 = sem("hidden_in_psum"), sem("hidden_ready")
        s_yps, s_ye = sem("expert_out_in_psum"), sem("expert_out_ready_plus_two")
        s_yst = [sem(f"expert_out_stored_{n}") for n in range(NB)]
        s_gath, s_y = sem("expert_out_gathered"), sem("experts_added")
        s_aw = sem("attn1_weights_landed")
        s1_kps, s1_kev = sem("keys1_in_psum"), sem("keys1_ready")
        s1_vps, s1_vev = sem("values1_in_psum"), sem("values1_ready")
        s1_qcps, s1_qm = sem("class_queries1_in_psum"), sem("class_queries1_spread")
        s1_csc, s1_cmx, s1_cexp = sem("class_scores1_in_psum"), sem("class_max1"), sem("class_exp1")
        s1_cp, s1_ctps, s1_ct = sem("class_probs1"), sem("class_probsT1_in_psum"), sem("class_probsT1")
        s1_ocps = sem("class_out1_in_psum")
        s1_qps, s1_qz = sem("queries1_in_psum"), sem("queries1_spread")
        s1_dps, s1_mx, s1_exp = sem("scores1_in_psum"), sem("max1_ready"), sem("exp1_done")
        s1_ptps, s1_pt, s1_xc = sem("probsT1_in_psum"), sem("probsT1_ready"), sem("class_tokens_repeated")
        s1_ops, s1_o = sem("out1_in_psum"), sem("out1_normalised")
        s1_otps, s1_ot, s1_otc = sem("outT1_in_psum"), sem("outT1_ready"), sem("class_outT1_ready")
        s1_prps = sem("projection1_in_psum")
        s_sl = sem("slots_landed")
        s_slot = [sem(f"ring_quad_landed_{n}") for n in range(RING // 4)]
        s_free = [sem(f"ring_quad_free_{n}") for n in range(RING // 4)]
        s2_u, s2_sq, s2_ms, s2_rms = sem("layernorm_done"), sem("squares_summed"), sem("mean_squares"), sem("rms_ready")
        s2_xr, s2_nrm = sem("rmsnorm_done"), sem("norms_ready")
        s2_sln, s2_sl, s2_slps, s2_slT = sem("slot_norms_ready"), sem("slots_ready"), sem("slotsT_in_psum"), sem("slotsT_ready")
        s2_lps, s2_mx, s2_exp, s2_d = sem("logits2_in_psum"), sem("logits2_max"), sem("logits2_exp"), sem("dispatch_ready")
        s2_dps, s2_dt = sem("dispatchT_in_psum"), sem("dispatchT_ready")
        s2_yps = sem("slot_inputs_in_psum")
        s2_cps, s2_csub, s2_cexp, s2_c = sem("combine_in_psum"), sem("combine_shifted"), sem("combine_exp"), sem("combine_ready")
        s2_ctps, s2_ct = sem("combineT_in_psum"), sem("combineT_ready")
        s2_hb, s2_ge, s2_htps, s2_hs = sem("fc1_biased"), sem("gelu2_done"), sem("hiddenT_in_psum"), sem("hiddenT_ready")
        s2_z, s2_yg, s2_mg, s2_f2, s2_y2 = sem("zeros_ready"), sem("group_inputs_ready"), sem("group_masks_ready"), sem("fc2_even_in_psum"), sem("slot_out_added")
        s2_ops = sem("combined_in_psum")

        @block.sync
        def _(sp):
            sp.dma_start(xp, a["xp"]).then_inc(s_x, 16)
            sp.dma_start(wt, a["wt"]).then_inc(s_x, 16)
            sp.dma_start(cst[:, :], a["cst"]).then_inc(s_cst, 16)
            sp.dma_start(cstb[:, :], a["cstb"]).then_inc(s_cst, 16)
            for n, name in enumerate(("tok_b", "b_out", "b_proj", "norm_w")):
                sp.dma_start(rowsb[:, n, :], a[name].partition_broadcast(P)).then_inc(s_cst, 16)
            sp.dma_start(scb[:, :], a["scale0"].partition_broadcast(KP)).then_inc(s_cst, 16)
            sp.wait_ge(s_hz, 1)
            sp.dma_start(h[0:B, TILES - 1, :], a["cls"].partition_broadcast(B)).then_inc(s_cls, 16)
            sp.dma_start(wo0[:, :, :], a["wo0"].rearrange("(c p) n -> p c n", p=P)).then_inc(s_wo0, 16)
            sp.wait_ge(s_xq, 2)
            sp.dma_start(wq0[:, :, :], a["wqkv0"].rearrange("(k p) n -> p k n", p=KP)).then_inc(s_wq0, 16)
            sp.wait_ge(s_hzb, 1)
            sp.dma_start(xs.rearrange("(t p) d -> p t d", p=P),
                         hb[:, 0, :].unsqueeze(1).to_broadcast([P, MT, D])).then_inc(s_xz, 16)
            sp.wait_ge(s_av, 4 * H)
            sp.dma_start(wq1, a["wqkv1"]).then_inc(s_aw, 16)
            sp.dma_start(wp1, a["wp1"]).then_inc(s_aw, 16)
            sp.dma_start(wr[:, :, :], a["wr"]).then_inc(s_mw, 16)
            sp.dma_start(b2e[:, :], a["b2e"]).then_inc(s_mw, 16)
            f1 = a["fc1"].rearrange("(g s) (p j) f -> g s p (j f)", s=2, j=3)
            f2 = a["fc2"].rearrange("s (c p) d -> s p c d", p=P)
            sp.wait_ge(s_prps, TILES)
            for n in range(RING):
                sp.dma_start(arena[:, n * SLOT:(n + 1) * SLOT], f1[n].rearrange("s p f -> (s p) f")).then_inc(s_slot[n // 4], 16)
            w1d = a["w1e"].rearrange("e (k p) f -> e p k f", p=KP)
            w2d = a["w2e"].rearrange("e (c p) d -> e p c d", p=P)
            xsd, ysd = xs.rearrange("(t p) d -> t p d", p=P), ys.rearrange("(t p) d -> t p d", p=P)

            def weights(j, n):
                e = sp.value_load(eid[0:1, j:j + 1] if isinstance(j, int) else eid[0:1, ds(j, 1)],
                                  min_val=0, max_val=E - 1)
                sp.dma_start(w1e[n], w1d[ds(e, 1)].rearrange("e p k f -> p (e k) f")).then_inc(s_ew[n], 16)
                sp.dma_start(w2e[n], w2d[ds(e, 1)].rearrange("e p c d -> p (e c) d")).then_inc(s_ew[n], 16)
                sp.dma_start(b1c[:, n, :], a["b1e"][ds(e, 1)].rearrange("e p m -> p (e m)")).then_inc(s_ew[n], 16)

            def tokens(j, n):
                src = xsd[j] if isinstance(j, int) else xsd[ds(j, 1)].rearrange("t p d -> p (t d)")
                sp.dma_start(xg[n], src).then_inc(s_ew[n], 16)

            def store(j, n):
                sp.wait_ge(s_ye, j + 3)
                dst = ysd[j] if isinstance(j, int) else ysd[ds(j, 1)].rearrange("t p d -> p (t d)")
                sp.dma_start(dst, yt[n]).then_inc(s_yst[n], 16)

            sp.wait_ge(s_eid, 1)
            for n in range(NB):
                weights(n, n)
            sp.wait_ge(s_scat, 16 * TOPK * TILES)
            for n in range(NB):
                tokens(n, n)
            with sp.Fori(0, MT // NB - 1) as i:
                for n in range(NB):
                    store(NB * i + n, n)
                    weights(NB * i + n + NB, n)
                    tokens(NB * i + n + NB, n)
            for j in range(MT - NB - MT % NB, MT):
                store(j, j % NB)
                if j + NB < MT:
                    weights(j + NB, j % NB)
                    tokens(j + NB, j % NB)
            sp.wait_ge(s_y, 1)
            sp.dma_start(slots, a["slots"]).then_inc(s_sl, 16)
            sp.dma_start(slscale, a["slot_scale"]).then_inc(s_sl, 16)
            sp.dma_start(b1R, a["b1R"]).then_inc(s_sl, 16)
            sp.dma_start(b2R, a["b2R"]).then_inc(s_sl, 16)
            with sp.Fori(1, PAIRS // RING) as i:
                for n in range(RING):
                    if n % 4 == 0:
                        sp.wait_ge(s_free[n // 4], i)
                    sp.dma_start(arena[:, n * SLOT:(n + 1) * SLOT],
                                 f1[ds(RING * i + n, 1)].rearrange("g s p f -> (g s p) f")).then_inc(s_slot[n // 4], 16)
            with sp.Fori(0, PAIRS // RING) as i:
                for n in range(RING):
                    if n % 4 == 0:
                        sp.wait_ge(s_free[n // 4], i + PAIRS // RING)
                    sp.dma_start(arena[:, n * SLOT:(n + 1) * SLOT].rearrange("p (s c d) -> p s c d", s=2, c=MF),
                                 f2[ds(2 * (RING * i + n), 2)].rearrange("s p c d -> p s c d")).then_inc(s_slot[n // 4], 16)
            sp.wait_ge(s_final, TILES)
            sp.dma_start(out[0:4 * P, :].rearrange("(t p) d -> p t d", p=P), h[:, 0:4, :]).then_inc(s_out, 16)
            sp.dma_start(out[4 * P:4 * P + B, :], h[0:B, 4, :]).then_inc(s_out, 16)
            sp.wait_ge(s_out, 32)

        @block.gpsimd
        def _(pool):
            nc.gpsimd.memset(h[:, TILES - 1, :], 0.0).then_inc(s_hz, 1)
            nc.gpsimd.memset(hb[:, 0, :], 0.0).then_inc(s_hzb, 1)
            nc.gpsimd.memset(am[:, :], 0.0).then_inc(s_amz, 1)
            nc.gpsimd.memset(qz0[:, :, :], 0.0).then_inc(s_qzz, 1)
            pool.wait_ge(s_amax, 2)
            nc.gpsimd.partition_all_reduce(gm[:, 0:2], am[:, 0:2], P, RMAX).then_inc(s_gmax, 1)
            with pool.Fori(0, 4) as t:
                for hd in range(H):
                    n = t * H + hd
                    if hd == 0:
                        pool.wait_ge(s_se, t + 1)
                    pool.wait_ge(s_neg, n + 1)
                    nc.gpsimd.tensor_tensor(L[:, hd, :], seb, neg[:, hd, :], ALU.subtract).then_inc(s_L, 1)
            pool.wait_ge(s_xz, 16)
            pool.wait_ge(s_pos, 1)
            for t in range(TILES):
                for k in range(TOPK):
                    nc.gpsimd.indirect_dma_start(xs, bass.IndirectOffsetOnAxis(posi[0:rows(t), k, t:t + 1], 0),
                                                 xn[0:rows(t), t, :], None).then_inc(s_scat, 16)
            for n in range(NB):
                pool.wait_ge(s_yst[n], 16 * len(range(n, MT, NB)))
            for t in range(TILES):
                for k in range(TOPK):
                    nc.gpsimd.indirect_dma_start(yg[0:rows(t), t, k, :], None, ys,
                                                 bass.IndirectOffsetOnAxis(posi[0:rows(t), k, t:t + 1], 0)).then_inc(s_gath, 16)

        @block.tensor
        def _(pe):
            def mm(o, l, r, start=True, stop=True, **kw):
                return nc.tensor.matmul(o, l, r, start=start, stop=stop, **kw)

            def transpose_tiles(s_):
                for t in range(TILES):
                    pe.wait_ge(s_xn, s_ * TILES + t + 1)
                    for k in range(KD):
                        i = nc.tensor.transpose(bank[0:KP, t, k * P:k * P + rows(t)],
                                                xn[0:rows(t), t, k * KP:(k + 1) * KP], ident[0:rows(t), 0:rows(t)])
                    i.then_inc(s_xtps, 1)

            pe.wait_ge(s_cst, 16 * 7)
            pe.wait_ge(s_xq, 2)
            for t in range(4):
                b, q = t // 2, t % 2
                for k in range(KD):
                    i = mm(bank[:, t, 0:D], xqb[:, k, t * P:(t + 1) * P], wqb[:, k, :], k == 0, k == KD - 1)
                i.then_inc(s_tokps, 1)
            transpose_tiles(0)

            pe.wait_ge(s_wq0, 16)
            pe.wait_ge(s_xt, TILES)

            def keys(c):
                if c >= 2:
                    pe.wait_ge(s_kev, c - 1)
                for b in range(B):
                    for k in range(KD):
                        i = mm(bank[:, 2 * (c % 2) + b, 0:NT], wq0[:, k, IN0 + c * P:IN0 + (c + 1) * P],
                               xT[:, k, b * NT:(b + 1) * NT], k == 0, k == KD - 1)
                i.then_inc(s_kps, 1)

            def values(v):
                if v >= 2:
                    pe.wait_ge(s_vev, v - 1)
                m = P if v < 4 else 1
                cs = cols(v) if v < 4 else slice((v - 4) * NT + NP, (v - 3) * NT)
                for half in range(2):
                    for k in range(KD):
                        i = mm(bank[0:m, 4 + 2 * (v % 2) + half, 0:IN0 // 2], xT[:, k, cs],
                               wq0[:, k, 2 * IN0 + half * 384:2 * IN0 + half * 384 + 384], k == 0, k == KD - 1)
                i.then_inc(s_vps, 1)

            for c in range(6):
                keys(c)
                values(c)

            pe.wait_ge(s_wqs, 1)
            pe.wait_ge(s_kev, 6)
            for c in range(C0):
                for k in range(KD):
                    i = mm(bank[:, 0, c * B:(c + 1) * B], wq0[:, k, c * P:(c + 1) * P], xT[:, k, cols(4)],
                           k == 0, k == KD - 1)
            i.then_inc(s_qcps, 1)
            pe.wait_ge(s_qm, 1)
            for b in range(B):
                for c in range(C0):
                    mm(bank[0:NR, 1, 0:NT], QM0[:, c, b * NR:(b + 1) * NR], kT0[:, c, b * NT:(b + 1) * NT],
                       b == 0 and c == 0, False)
            mm(bank[0:NR, 1, 0:NT], identb[0:NR, 0:NR], bigc, False, True).then_inc(s_ncps, 1)
            pe.wait_ge(s_nc, 1)
            mm(bank[0:NR, 3, 0:NT], const("nb", NR), negC).then_inc(s_lc, 1)

            def prepare(t):
                b = t // 2
                col = t * P + b
                for c in range(C0):
                    for k in range(KD):
                        i = mm(bank[:, 4 + c // 3, (c % 3) * P:(c % 3 + 1) * P], wq0[:, k, c * P:(c + 1) * P],
                               xT[:, k, ds(col, P)], k == 0, k == KD - 1)
                i.then_inc(s_qps, 1)
                pe.wait_ge(s_qev, t + 1)
                for c in range(C0):
                    i = mm(bank[:, 2, 0:NT], qf0[:, c, :], kT0[:, c, ds(b * NT, NT)], c == 0, c == C0 - 1)
                i.then_inc(s_seps, 1)

            def scores(t, hd):
                b = t // 2
                mm(bank[:, hd % 2, 0:NT], qz0[:, hd, :], kT0[:, hd // 2, ds(b * NT, NT)], True, False)
                mm(bank[:, hd % 2, 0:NT], identb, bigd[:, ds((1 - t % 2) * P, NT)], False, True).then_inc(s_dps, 1)

            def attend(t, hd):
                b = t // 2
                pe.wait_ge(s_exp, t * H + hd + 3)
                for k in range(2):
                    nc.tensor.transpose(bank[:, 3, k * P:(k + 1) * P], PR[:, hd % 2, k * P:(k + 1) * P], ident)
                nc.tensor.transpose(bank[0:1, 3, 2 * P:3 * P], PR[:, hd % 2, NP:NT], ident).then_inc(s_ptps, 1)
                pe.wait_ge(s_pt, t * H + hd + 1)
                o = bank[:, 6 + hd % 2, 0:HD0]
                hs = slice(hd * HD0, (hd + 1) * HD0)
                for k in range(2):
                    mm(o, PT[:, k, :], v0[:, ds(2 * b + k, 1), hs], k == 0, False)
                mm(o, PTr, vc0[0:1, ds(b, 1), hs], False, True).then_inc(s_av, 1)

            def finish(t):
                pe.wait_ge(s_o, t + 1)
                for c in range(C0):
                    i = nc.tensor.transpose(bank[:, 4 + c // 3, (c % 3) * P:(c % 3 + 1) * P],
                                            O0[:, c * P:(c + 1) * P], ident)
                i.then_inc(s_otps, 1)
                pe.wait_ge(s_ot, t + 1)

            prepare(0)
            for hd in range(H):
                if hd >= 2:
                    pe.wait_ge(s_neg, hd - 1)
                scores(0, hd)
            pe.wait_ge(s_pcn, 1)
            for k in range(2):
                nc.tensor.transpose(bank[:, 3, k * NR:(k + 1) * NR], PR[0:NR, 0, k * P:(k + 1) * P], ident[0:NR, 0:NR])
            nc.tensor.transpose(bank[0:1, 3, 2 * NR:3 * NR], PR[0:NR, 0, NP:NT], ident[0:NR, 0:NR]).then_inc(s_pctps, 1)
            pe.wait_ge(s_pct, 1)
            for b in range(B):
                for c in range(C0):
                    o = bank[:, 6, (b * C0 + c) * H:(b * C0 + c + 1) * H]
                    for k in range(2):
                        mm(o, v0[:, 2 * b + k, c * P:(c + 1) * P], PCT[:, k, b * H:(b + 1) * H], k == 0, False)
                    i = mm(o, vc0[0:1, b, c * P:(c + 1) * P], PCr[0:1, b * H:(b + 1) * H], False, True)
            i.then_inc(s_ocps, 1)
            pe.wait_ge(s_oc, 1)

            with pe.Fori(0, 3) as t:
                for hd in range(H):
                    if hd == H // 2:
                        prepare(t + 1)
                    attend(t, hd)
                    if hd % 2 and hd >= H // 2:
                        for g in range(2 * hd - H - 2, 2 * hd - H + 2):
                            pe.wait_ge(s_neg, (t + 1) * H + g - 1)
                            scores(t + 1, g)
                finish(t)
            for hd in range(H):
                attend(3, hd)
            finish(3)

            pe.wait_ge(s_wo0, 16)
            for t in range(TILES):
                if t == TILES - 1:
                    pe.wait_ge(s_otc, 1)
                for c in range(C0):
                    i = mm(bank[0:rows(t), t, 0:D], OT0[:, c, cols(t)], wo0[:, c, :], c == 0, c == C0 - 1)
                i.then_inc(s_prps, 1)
            transpose_tiles(1)
            pe.wait_ge(s_xt, 2 * TILES)
            pe.wait_ge(s_mw, 32)
            for t in range(TILES):
                for k in range(KD):
                    i = mm(bank[0:rows(t), 5, t * E:(t + 1) * E], xT[:, k, cols(t)], wr[:, k, :], k == 0, k == KD - 1)
            i.then_inc(s_rps, 1)
            pe.wait_ge(s_msk, 1)
            for t in range(TILES):
                for q in range(t + 1):
                    mm(bank[:, 5, t * E:(t + 1) * E], const("below" if q == t else "ones", rows(q)), ohs[0:rows(q), q, :],
                       q == 0, q == t)
            for q in range(TILES):
                i = mm(bank[:, 5, TILES * E:(TILES + 1) * E], const("ones", rows(q)), ohs[0:rows(q), q, :], q == 0,
                       q == TILES - 1)
            i.then_inc(s_rkps, 1)
            pe.wait_ge(s_gate, 1)
            for t in range(TILES):
                i = nc.tensor.transpose(bank[0:E, 6 + t // 4, (t % 4) * P:(t % 4) * P + rows(t)], gate[0:rows(t), t, :],
                                        ident[0:rows(t), 0:rows(t)])
            i.then_inc(s_gtps, 1)
            pe.wait_ge(s_gt, 1)
            for t in range(TILES):
                i = mm(bank[0:rows(t), t, 0:D], gT[:, t, 0:rows(t)], b2e[:, :])
            i.then_inc(s_gbps, 1)
            pe.wait_ge(s_ye, 2)

            def fc1(j, n, turn):
                pe.wait_ge(s_ew[n], 64 * turn)
                for k in range(KD):
                    i = nc.tensor.transpose(bank[0:KP, 4 + n % 2, k * P:(k + 1) * P], xg[n][:, k * KP:(k + 1) * KP], ident)
                i.then_inc(s_gxps, 1)
                pe.wait_ge(s_gx, j + 1)
                for m in range(MF):
                    for k in range(KD):
                        i = mm(bank[:, 2 * (n % 2) + m // 3, (m % 3) * P:(m % 3 + 1) * P], w1e[n][:, k, m * P:(m + 1) * P],
                               xgT[n % 2][:, k, :], k == 0, k == KD - 1)
                    if m % 3 == 2:
                        i.then_inc(s_h1ps, 1)

            def fc2(j, n):
                pe.wait_ge(s_ye, j + 1)
                for m in range(MF):
                    pe.wait_ge(s_h1, j * MF + m + 1)
                    i = mm(bank[:, 6 + n % 2, 0:D], hT[n % 2][:, m, :], w2e[n][:, m, :], m == 0, m == MF - 1)
                i.then_inc(s_yps, 1)

            fc1(0, 0, 1)
            with pe.Fori(0, MT // NB) as i:
                for n in range(NB):
                    fc1(NB * i + n + 1, (n + 1) % NB, i + 1 + (n + 1) // NB)
                    fc2(NB * i + n, n)
            for j in range(MT - MT % NB, MT):
                if j + 1 < MT:
                    fc1(j + 1, (j + 1) % NB, (j + 1) // NB + 1)
                fc2(j, j % NB)
            transpose_tiles(2)
            pe.wait_ge(s_aw, 32)
            pe.wait_ge(s_xt, 3 * TILES)
            for c in range(KD):
                for b in range(B):
                    for k in range(KD):
                        i = mm(bank[0:KP, 2 * c + b, 0:NT], wq1[:, k, D + c * KP:D + (c + 1) * KP],
                               xT[:, k, b * NT:(b + 1) * NT], k == 0, k == KD - 1)
                i.then_inc(s1_kps, 1)
            for v in range(6):
                if v >= 2:
                    pe.wait_ge(s1_vev, v - 1)
                if v == 4:
                    pe.wait_ge(s1_xc, 1)
                for k in range(KD):
                    i = mm(bank[:, 4 + v % 2, 0:D], xT[:, k, cols(v)] if v < 4 else xc1[:, k, v - 4, :],
                           wq1[:, k, 2 * D:3 * D], k == 0, k == KD - 1)
                i.then_inc(s1_vps, 1)
            for c in range(KD):
                for k in range(KD):
                    i = mm(bank[0:KP, 6, c * B:(c + 1) * B], wq1[:, k, c * KP:(c + 1) * KP], xT[:, k, cols(4)],
                           k == 0, k == KD - 1)
            i.then_inc(s1_qcps, 1)
            pe.wait_ge(s1_qm, 1)
            pe.wait_ge(s1_kev, 2)
            for b in range(B):
                for c in range(KD):
                    i = mm(bank[0:NR, 7, 0:NT], QM1[:, c, b * NR:(b + 1) * NR], kT1[:, c, b * NT:(b + 1) * NT],
                           b == 0 and c == 0, b == 1 and c == KD - 1)
            i.then_inc(s1_csc, 1)
            pe.wait_ge(s1_cp, 1)
            for k in range(2):
                nc.tensor.transpose(bank[:, 3, k * NR:(k + 1) * NR], PC1[:, k * P:(k + 1) * P], ident[0:NR, 0:NR])
            nc.tensor.transpose(bank[0:1, 3, 2 * NR:3 * NR], PC1[:, NP:NT], ident[0:NR, 0:NR]).then_inc(s1_ctps, 1)
            pe.wait_ge(s1_ct, 1)
            pe.wait_ge(s1_vev, 6)
            for b in range(B):
                for c in range(KD):
                    o = bank[0:KP, 6, (b * KD + c) * H:(b * KD + c + 1) * H]
                    for k in range(2):
                        mm(o, v1[:, 2 * b + k, c * KP:(c + 1) * KP], PCT[:, k, b * H:(b + 1) * H], k == 0, False)
                    i = mm(o, vc1[0:1, b, c * KP:(c + 1) * KP], PCr[0:1, b * H:(b + 1) * H], False, True)
            i.then_inc(s1_ocps, 1)
            pe.wait_ge(s1_otc, 1)
            with pe.Fori(0, 4) as t:
                pe.wait_ge(s1_ot, t + 1)
                for c in range(KD):
                    for k in range(KD):
                        i = mm(bank[0:KP, 7, c * P:(c + 1) * P], wq1[:, k, c * KP:(c + 1) * KP],
                               xT[:, k, ds(t * P + t // 2, P)], k == 0, k == KD - 1)
                i.then_inc(s1_qps, 1)
                pe.wait_ge(s1_qz, t + 1)

                def scores(g):
                    if g >= 2:
                        pe.wait_ge(s1_exp, t * (H // 2) + g - 1)
                    for hd in (2 * g, 2 * g + 1):
                        i = mm(bank[:, hd % 4, 0:NT], qz1[:, hd, :], kTc[:, hd // HPC, :])
                    i.then_inc(s1_dps, 1)

                def attend(g):
                    pe.wait_ge(s1_pt, t * (H // 2) + g + 1)
                    for hd in (2 * g, 2 * g + 1):
                        for k in range(2):
                            i = mm(bank[:, 6, hd * HD1:(hd + 1) * HD1], PT1[:, g % 2, hd % 2, k, :],
                                   vC[:, k, hd * HD1:(hd + 1) * HD1], k == 0, k == 1)
                    return i

                scores(0)
                scores(1)
                for g in range(H // 2):
                    pe.wait_ge(s1_exp, t * (H // 2) + g + 1)
                    for hd in (2 * g, 2 * g + 1):
                        for k in range(2):
                            i = nc.tensor.transpose(bank[:, 4 + g % 2, (hd % 2 * 2 + k) * P:(hd % 2 * 2 + k + 1) * P],
                                                    PR1[:, hd, k * P:(k + 1) * P], ident)
                    i.then_inc(s1_ptps, 1)
                    if g + 2 < H // 2:
                        scores(g + 2)
                    if g:
                        attend(g - 1)
                attend(H // 2 - 1).then_inc(s1_ops, 1)
                pe.wait_ge(s1_o, t + 1)
                for c in range(KD):
                    i = nc.tensor.transpose(bank[0:KP, 7, (KD + c) * P:(KD + c + 1) * P],
                                            O1[:, c * KP:(c + 1) * KP], ident)
                i.then_inc(s1_otps, 1)
            pe.wait_ge(s1_ot, 5)
            for t in range(TILES):
                for k in range(KD):
                    i = mm(bank[0:rows(t), t, 0:D], OT1[:, k, cols(t)], wp1[:, k, :], k == 0, k == KD - 1)
                i.then_inc(s1_prps, 1)
            pe.wait_ge(s2_sl, 1)
            for k in range(KD):
                i = nc.tensor.transpose(bank[0:KP, 5, k * S:(k + 1) * S], slots[:, k * KP:(k + 1) * KP], ident[0:S, 0:S])
            i.then_inc(s2_slps, 1)
            transpose_tiles(3)
            pe.wait_ge(s2_slT, 1)
            pe.wait_ge(s_xt, 4 * TILES)
            for b in range(B):
                for k in range(KD):
                    i = mm(bank[0:S, 6 + b, 0:NT], slT[:, k, :], xT[:, k, b * NT:(b + 1) * NT], k == 0, k == KD - 1)
            i.then_inc(s2_lps, 1)
            for t in range(TILES):
                for k in range(KD):
                    i = mm(bank[0:rows(t), 4, t * S:(t + 1) * S], xT[:, k, cols(t)], slT[:, k, :], k == 0, k == KD - 1)
            i.then_inc(s2_cps, 1)
            pe.wait_ge(s2_d, 1)
            for t in range(4):
                nc.tensor.transpose(bank[:, 5, t * S:(t + 1) * S], Dm[:, t // 2, (t % 2) * P:(t % 2 + 1) * P], ident[0:S, 0:S])
            nc.tensor.transpose(bank[0:B, 5, 4 * S:5 * S], Dm[:, :, NP], ident[0:S, 0:S]).then_inc(s2_dps, 1)
            pe.wait_ge(s2_dt, 1)
            for par in range(2):
                for j in range(3):
                    for b in range(B):
                        o = bank[64 * par:64 * par + 64, 6, (j * B + b) * PAIRS:(j * B + b + 1) * PAIRS]
                        for q in range(2):
                            mm(o, xr[:, 2 * b + q, j:D:3], DT[:, 2 * b + q, par:S:2], q == 0, False)
                        i = mm(o, xr[0:B, 4, j:D:3], DTc[:, b, par:S:2], False, True)
            i.then_inc(s2_yps, 1)
            pe.wait_ge(s2_z, 1)
            for half in range(2):
                for c in range(4):
                    mm(bank[32 * c:32 * c + 32, half, 0:FF // 2], zero, cst[:, 0:FF // 2], True, False, skip_group_check=True)
            with pe.Fori(0, PAIRS // RING) as g:
                pe.wait_ge(s2_yg, g + 1)
                for quad in range(RING // 4):
                    pe.wait_ge(s_slot[quad], 64 * g + 64)
                    for j in range(3):
                        for half in range(2):
                            for c in range(4):
                                n = 4 * quad + c
                                i = mm(bank[32 * c:32 * c + 32, half, 0:FF // 2], YMg[:, n, j, :],
                                       arena[:, n * SLOT + j * FF + half * 384:n * SLOT + j * FF + half * 384 + 384],
                                       False, False, skip_group_check=True)
                    i.then_inc(s_free[quad], 1)
            pe.wait_ge(s2_c, 1)
            for t in range(TILES):
                i = nc.tensor.transpose(bank[:, 4 + t // 4, (t % 4) * P:(t % 4) * P + rows(t)], lgx[0:rows(t), t, :],
                                        ident[0:rows(t), 0:rows(t)])
            i.then_inc(s2_ctps, 1)
            pe.wait_ge(s2_ge, 1)
            for k in range(MF):
                i = nc.tensor.transpose(bank[:, 6 + k // 3, (k % 3) * P:(k % 3 + 1) * P], hrow[:, k * P:(k + 1) * P], ident)
            i.then_inc(s2_htps, 1)
            pe.wait_ge(s2_hs, 1)
            pe.wait_ge(s2_ct, 1)
            with pe.Fori(0, PAIRS // RING) as g:
                pe.wait_ge(s2_mg, g + 1)
                for quad in range(RING // 4):
                    pe.wait_ge(s_slot[quad], 64 * g + 64 * (PAIRS // RING + 1))
                    for odd in range(2):
                        for k in range(MF):
                            for c in range(4):
                                n = 4 * quad + c
                                at = n * SLOT + (odd * MF + k) * D
                                i = mm(bank[32 * c:32 * c + 32, 2 + 2 * quad + odd, 0:D], hT2[:, k, 32 * c:32 * c + 32],
                                       arena[:, at:at + D], k == 0, k == MF - 1)
                        i.then_inc(s_free[quad] if odd else s2_f2, 1)
            pe.wait_ge(s2_y2, 4 * (PAIRS // RING) + 1)
            for t in range(TILES):
                mm(bank[0:rows(t), t if t else 6, 0:D], CT[:, t, 0:rows(t)], Y2).then_inc(s2_ops, 1)

        @block.scalar
        def _(act):
            def copy(o, i, scale=1.0):
                return nc.scalar.activation(o, i, ACT.Copy, scale=scale)

            def deviations(s_):
                act.wait_ge(s_var, s_ + 1)
                nc.scalar.activation(sm[:, 1, :], sm[:, 0, :], ACT.Sqrt).then_inc(s_std, 1)

            def copy_tiles(s_):
                for t in range(TILES):
                    act.wait_ge(s_xtps, s_ * TILES + t + 1)
                    copy(xT[:, :, cols(t)],
                         bank[0:KP, t, 0:KD * P].rearrange("p (k n) -> p k n", k=KD)[:, :, 0:rows(t)]).then_inc(s_xt, 1)

            deviations(0)
            copy_tiles(0)
            for c in range(C0):
                act.wait_ge(s_kps, c + 1)
                copy(kT0[:, c, :].rearrange("p (b n) -> p b n", b=B), bank[:, 2 * (c % 2):2 * (c % 2) + 2, 0:NT]).then_inc(s_kev, 1)
            act.wait_ge(s_ncps, 1)
            copy(negC, bank[0:NR, 1, 0:NT]).then_inc(s_nc, 1)

            def prepare(t, first):
                qb = bank[:, 4:6, 0:3 * P].rearrange("p a (c n) -> p a c n", c=3)
                act.wait_ge(s_qps, t + 1)
                for par in range(2):
                    r = slice(64 * par, 64 * par + 64)
                    for half in range(2):
                        copy(qz0[r, 6 * half + par:6 * half + 6:2, :], bank[r, 4 + half, 0:3 * P].rearrange(
                            "p (c n) -> p c n", c=3))
                for half in range(2):
                    i = copy(qf0[:, 3 * half:3 * half + 3, :],
                             bank[:, 4 + half, 0:3 * P].rearrange("p (c n) -> p c n", c=3), -1.0 / H)
                i.then_inc(s_qev, 1)
                act.wait_ge(s_seps, t + 1)
                if not first:
                    act.wait_ge(s_L, t * H)
                copy(seb, bank[:, 2, 0:NT]).then_inc(s_se, 1)

            def keep(t, hd):
                act.wait_ge(s_dps, t * H + hd + 1)
                copy(neg[:, hd, :], bank[:, hd % 2, 0:NT]).then_inc(s_neg, 1)

            def attend(t, hd):
                n = t * H + hd
                for g in range(2):
                    act.wait_ge(s_xm, n + g + 1)
                    nc.scalar.activation(PR[:, g, :], X[:, g, :], ACT.Exp, bias=nmx[:, g:g + 1],
                                         accum_out=rs[:, hd + g:hd + g + 1]).then_inc(s_exp, 1)
                for g in range(2):
                    act.wait_ge(s_ptps, n + g + 1)
                    if g:
                        act.wait_ge(s_av, n + 1)
                    copy(PT, bank[:, 3, 0:2 * P].rearrange("p (k n) -> p k n", k=2))
                    copy(PTr, bank[0:1, 3, 2 * P:3 * P]).then_inc(s_pt, 1)
                act.wait_ge(s_av, n + 2)
                act.wait_ge(s_rr, t * (H // 2) + hd // 2 + 2)
                for g in range(2):
                    i = nc.scalar.activation(O0[:, (hd + g) * HD0:(hd + g + 1) * HD0], bank[:, 6 + g, 0:HD0], ACT.Copy,
                                             scale=rr[:, hd + g:hd + g + 1])
                if hd == H - 2:
                    i.then_inc(s_o, 1)

            def finish(t):
                act.wait_ge(s_otps, t + 1)
                for half in range(2):
                    i = copy(OT0[:, 3 * half:3 * half + 3, ds(t * P + t // 2, P)],
                             bank[:, 4 + half, 0:3 * P].rearrange("p (c n) -> p c n", c=3))
                i.then_inc(s_ot, 1)

            act.wait_ge(s_qzz, 1)
            prepare(0, True)
            for hd in range(H):
                keep(0, hd)
            act.wait_ge(s_xc, 1)
            nc.scalar.activation(PR[0:NR, 0, :], X[0:NR, 0, :], ACT.Exp, bias=nmx[0:NR, 0:1],
                                 accum_out=gm[0:NR, 6:7]).then_inc(s_pc, 1)
            act.wait_ge(s_pctps, 1)
            copy(PCT[:, :, :], bank[:, 3, 0:2 * NR].rearrange("p (k n) -> p k n", k=2))
            copy(PCr[:, :], bank[0:1, 3, 2 * NR:3 * NR]).then_inc(s_pct, 1)
            act.wait_ge(s_ocps, 1)
            copy(Oc.rearrange("p a b -> p (a b)"), bank[:, 6, 0:B * C0 * H]).then_inc(s_oc, 1)
            act.sem_inc(s_exp, 2)
            with act.Fori(0, 3) as t:
                for hd in range(0, H, 2):
                    if hd == H // 2:
                        prepare(t + 1, False)
                    attend(t, hd)
                    if hd >= H // 2:
                        for g in range(2 * hd - H, 2 * hd - H + 4):
                            keep(t + 1, g)
                finish(t)
            for hd in range(0, H, 2):
                attend(3, hd)
            finish(3)
            deviations(1)
            copy_tiles(1)
            act.wait_ge(s_rsub, 1)
            nc.scalar.activation(lg[:, :, :], lg[:, :, :], ACT.Exp).then_inc(s_rexp, 1)
            act.wait_ge(s_gtps, 1)
            copy(gT[:, 0:4, :].rearrange("p a b -> p (a b)"), bank[0:E, 6, :])
            copy(gT[:, 4, 0:B], bank[0:E, 7, 0:B]).then_inc(s_gt, 1)

            def gelu(j, n):
                for m in range(MF):
                    if m % 3 == 0:
                        act.wait_ge(s_h1ps, 2 * j + m // 3 + 1)
                    nc.scalar.activation(hT[n % 2][:, m, :], bank[:, 2 * (n % 2) + m // 3, (m % 3) * P:(m % 3 + 1) * P],
                                         ACT.Gelu, bias=b1c[:, n, m:m + 1]).then_inc(s_h1, 1)
            with act.Fori(0, MT // NB) as i:
                for n in range(NB):
                    gelu(NB * i + n, n)
            for j in range(MT - MT % NB, MT):
                gelu(j, j % NB)
            deviations(2)
            copy_tiles(2)
            for c in range(KD):
                act.wait_ge(s1_kps, c + 1)
                copy(kT1[:, c, :].rearrange("p (b n) -> p b n", b=B), bank[0:KP, 2 * c:2 * c + 2, 0:NT]).then_inc(s1_kev, 1)
            act.wait_ge(s1_cmx, 1)
            nc.scalar.activation(PC1, bank[0:NR, 7, 0:NT], ACT.Exp, bias=nmx[0:NR, 0:1],
                                 accum_out=gm[0:NR, 6:7]).then_inc(s1_cexp, 1)
            act.wait_ge(s1_ctps, 1)
            copy(PCT[:, :, :], bank[:, 3, 0:2 * NR].rearrange("p (k n) -> p k n", k=2))
            copy(PCr[:, :], bank[0:1, 3, 2 * NR:3 * NR]).then_inc(s1_ct, 1)
            act.sem_inc(s1_ot, 1)
            with act.Fori(0, 4) as t:
                for g in range(H // 2):
                    act.wait_ge(s1_mx, t * (H // 2) + g + 1)
                    for hd in (2 * g, 2 * g + 1):
                        i = nc.scalar.activation(PR1[:, hd, :], bank[:, hd % 4, 0:NT], ACT.Exp,
                                                 bias=nmx1[:, g % 2, hd % 2:hd % 2 + 1], accum_out=rs[:, hd:hd + 1])
                    i.then_inc(s1_exp, 1)
                act.wait_ge(s1_otps, t + 1)
                copy(OT1[:, :, ds(t * P + t // 2, P)],
                     bank[0:KP, 7, KD * P:2 * KD * P].rearrange("p (k n) -> p k n", k=KD)).then_inc(s1_ot, 1)
            def sum_squares(src, dst, squares):
                return nc.scalar.activation(squares, src, ACT.Square, accum_out=dst)

            act.wait_ge(s_sl, 64)
            sum_squares(slots, sm[0:S, 12, 0:1], junk[:, :]).then_inc(s2_sln, 1)
            act.wait_ge(s2_sln, 1)
            nc.scalar.activation(sm[0:S, 12, 1:2], sm[0:S, 12, 0:1], ACT.Sqrt).then_inc(s2_sln, 1)
            act.wait_ge(s2_slps, 1)
            copy(slT, bank[0:KP, 5, 0:KD * S].rearrange("p (k n) -> p k n", k=KD)).then_inc(s2_slT, 1)
            deviations(3)
            act.wait_ge(s2_u, 1)
            for t in range(TILES):
                i = sum_squares(xn[:, t, :], sm[:, 6, t:t + 1], xr[:, t, :])
            i.then_inc(s2_sq, 1)
            act.wait_ge(s2_ms, 1)
            nc.scalar.activation(sm[:, 7, :], sm[:, 7, :], ACT.Sqrt).then_inc(s2_rms, 1)
            act.wait_ge(s2_xr, 1)
            for t in range(TILES):
                i = sum_squares(xr[:, t, :], sm[:, 9, t:t + 1], hb[:, t, :])
            i.then_inc(s2_nrm, 1)
            act.wait_ge(s2_nrm, 1)
            nc.scalar.activation(sm[:, 10, :], sm[:, 9, :], ACT.Sqrt).then_inc(s2_nrm, 1)
            copy_tiles(3)
            act.wait_ge(s2_mx, 1)
            for b in range(B):
                i = nc.scalar.activation(Dm[:, b, :], bank[0:S, 6 + b, 0:NT], ACT.Exp, bias=nmx[0:S, b:b + 1],
                                         accum_out=rs[0:S, b:b + 1])
            i.then_inc(s2_exp, 1)
            act.wait_ge(s2_csub, 1)
            nc.scalar.activation(lgc, lgc, ACT.Exp).then_inc(s2_cexp, 1)
            act.wait_ge(s2_hb, 1)
            nc.scalar.activation(hrow, hrow, ACT.Gelu).then_inc(s2_ge, 1)
            act.wait_ge(s2_htps, 1)
            copy(hT2.rearrange("p (a c) n -> p a (c n)", a=2), bank[:, 6:8, 0:3 * P]).then_inc(s2_hs, 1)

        @block.vector
        def _(dve):
            ts, tt, stt = nc.vector.tensor_scalar, nc.vector.tensor_tensor, nc.vector.scalar_tensor_tensor
            chain = [0]

            def link(ins):
                chain[0] += 1
                ins.then_inc(s_dve, 1)
                dve.wait_ge(s_dve, chain[0])

            def normalise(s_, done=None):
                for t in range(TILES):
                    i = nc.vector.bn_stats(stats[:, t, :], h[:, t, :])
                link(i)
                for t in range(TILES):
                    i = nc.vector.bn_aggr(mv[:, t, :], stats[:, t, :])
                link(i)
                ts(sm[:, 0, :], mv[:, :, 1], EPS, None, ALU.add).then_inc(s_var, 1)
                dve.wait_ge(s_std, s_ + 1)
                link(nc.vector.reciprocal(sm[:, 2, :], sm[:, 1, :]))
                for t in range(TILES):
                    i = ts(xn[:, t, :], h[:, t, :], mv[:, t, 0:1], sm[:, 2, t:t + 1], ALU.subtract, ALU.mult)
                    if not done:
                        i.then_inc(s_xn, 1)
                if done:
                    i.then_inc(done, 1)
                    dve.wait_ge(done, 1)
                else:
                    dve.wait_ge(s_xn, (s_ + 1) * TILES)

            dve.wait_ge(s_amz, 1)
            dve.wait_ge(s_x, 32)
            nc.vector.tensor_reduce(am[0:KP, 0:1], xp.rearrange("p k n -> p (k n)"), AX.X, ALU.max,
                                    apply_absolute_value=True).then_inc(s_amax, 1)
            nc.vector.tensor_reduce(am[0:KP, 1:2], wt.rearrange("p k n -> p (k n)"), AX.X, ALU.max,
                                    apply_absolute_value=True).then_inc(s_amax, 1)
            dve.wait_ge(s_gmax, 1)
            link(ts(gm[:, 2:4], gm[:, 0:2], 1e-8, 1.0 / QMAX, ALU.max, ALU.mult))
            link(nc.vector.reciprocal(gm[:, 4:6], gm[:, 2:4]))
            link(tt(gm[:, 6:7], gm[:, 2:3], gm[:, 3:4], ALU.mult))
            for n, (src, tmp, dst) in enumerate((
                    (xp.rearrange("p k (a n) -> p k a n", a=2), neg[0:KP, 0:4, 0:NP].rearrange("p (k a) n -> p k a n", a=2),
                     xqb.rearrange("p k (a n) -> p k a n", a=2)),
                    (wt, neg[0:KP, 4:6, 0:D], wqb))):
                link(ts(tmp, src, gm[0:KP, 4 + n:5 + n], QMAX, ALU.mult, ALU.min))
                link(ts(tmp, tmp, -QMAX, MAGIC, ALU.max, ALU.add))
                ts(dst, tmp, MAGIC, None, ALU.subtract).then_inc(s_xq, 1)
            dve.wait_ge(s_cst, 16 * 7)
            for t in range(4):
                dve.wait_ge(s_tokps, t + 1)
                i = stt(h[:, t, :], bank[:, t, 0:D], gm[:, 6:7], rowsb[:, 0, :], ALU.mult, ALU.add)
            dve.wait_ge(s_cls, 16)
            link(i)
            normalise(0)

            dve.wait_ge(s_wq0, 16)
            for k in range(KD):
                i = stt(wq0[:, k, 0:IN0].rearrange("p (h e) -> p h e", h=H),
                        wq0[:, k, 0:IN0].rearrange("p (h e) -> p h e", h=H), -1.0,
                        scb[:, :].unsqueeze(2).to_broadcast([KP, H, HD0]), ALU.mult, ALU.mult)
            i.then_inc(s_wqs, 1)
            for v in range(6):
                dve.wait_ge(s_vps, v + 1)
                src = bank[:, 4 + 2 * (v % 2):6 + 2 * (v % 2), 0:384]
                dst = v0[:, v, :] if v < 4 else vc0[0:1, v - 4, :]
                nc.vector.tensor_copy(dst.rearrange("p (a n) -> p a n", a=2), src if v < 4 else src[0:1]).then_inc(s_vev, 1)
            dve.wait_ge(s_qcps, 1)
            for b in range(B):
                i = tt(QM0[:, :, b * NR:(b + 1) * NR],
                       const("mq0").rearrange("p (c b r) -> p c b r", c=C0, b=B)[:, :, b, :],
                       bank[:, 0, b:C0 * B:B].unsqueeze(2).to_broadcast([P, C0, NR]), ALU.mult)
            i.then_inc(s_qm, 1)

            def drop(p, srcs, early):
                step, lag = 0, len(srcs) - 1
                now = list(srcs)
                for r in range(ROUNDS):
                    for n in range(len(srcs)):
                        if step > lag:
                            dve.wait_ge(s_step, step - lag)
                        nc.vector.max(m8[0:p, n, :], now[n]).then_inc(s_step, 1)
                        step += 1
                    for n in range(len(srcs)):
                        dve.wait_ge(s_step, step - lag)
                        nc.vector.match_replace(W[0:p, n, :], m8[0:p, n, :], now[n], -BIG).then_inc(s_step, 1)
                        now[n] = W[0:p, n, :]
                        step += 1
                    if r == 1 and early:
                        early()
                return step

            def mask(p, logits, step, done):
                lag = len(logits) - 1
                for n, lgt in enumerate(logits):
                    dve.wait_ge(s_step, step - lag)
                    stt(X[0:p, n, :], W[0:p, n, :], THR, lgt, ALU.add, ALU.min).then_inc(s_step, 1)
                    step += 1
                dve.wait_ge(s_step, step)
                dve.sem_clear(s_step)
                for n in range(len(logits)):
                    nc.vector.tensor_reduce(nmx[0:p, n:n + 1], X[0:p, n, :], AX.X, ALU.max,
                                            negate=True).then_inc(done, 1)

            dve.wait_ge(s_nc, 1)
            step = drop(NR, [negC], None)
            dve.wait_ge(s_lc, 1)
            mask(NR, [bank[0:NR, 3, 0:NT]], step, s_xc)
            dve.wait_ge(s_pc, 1)
            link(nc.vector.reciprocal(gm[0:NR, 7:8], gm[0:NR, 6:7]))
            ts(PR[0:NR, 0, :], PR[0:NR, 0, :], gm[0:NR, 7:8], None, ALU.mult).then_inc(s_pcn, 1)
            link(nc.vector.memset(rs[:, H - 2:H], 1.0))

            with dve.Fori(0, 4) as t:
                for hd in range(0, H, 2):
                    n = t * H + hd
                    dve.wait_ge(s_L, n + 2)
                    nc.vector.memset(tick[:, 0:1], 0.0)

                    def reciprocals_before():
                        dve.wait_ge(s_exp, n + 2)
                        g = (hd - 2) % H
                        nc.vector.reciprocal(rr[:, g:g + 2], rs[:, g:g + 2]).then_inc(s_rr, 1)

                    step = drop(P, [neg[:, hd, :], neg[:, hd + 1, :]], reciprocals_before)
                    mask(P, [L[:, hd, :], L[:, hd + 1, :]], step, s_xm)
            dve.wait_ge(s_exp, 4 * H + 2)
            nc.vector.reciprocal(rr[:, H - 2:H], rs[:, H - 2:H]).then_inc(s_rr, 1)
            dve.wait_ge(s_oc, 1)
            link(tt(Oc.rearrange("p (b c) r -> p b c r", b=B)[:, 0], Oc.rearrange("p (b c) r -> p b c r", b=B)[:, 0],
                    const("mo0").rearrange("p (c r) -> p c r", c=C0), ALU.mult))
            link(tt(Oc.rearrange("p (b c) r -> p b c r", b=B)[:, 1], Oc.rearrange("p (b c) r -> p b c r", b=B)[:, 1],
                    const("mo0").rearrange("p (c r) -> p c r", c=C0), ALU.mult))
            for b in range(B):
                i = nc.vector.tensor_reduce(OT0[:, :, b * NT + NP:b * NT + NP + 1],
                                            Oc.rearrange("p (b c) r -> p b c r", b=B)[:, b], AX.X, ALU.add)
            i.then_inc(s_otc, 1)
            dve.wait_ge(s_xz, 16)
            for t in range(TILES):
                i = tt(hb[:, t, :], h[:, t, :], rowsb[:, 1, :], ALU.add)
            link(i)
            for t in range(TILES):
                dve.wait_ge(s_prps, t + 1)
                i = tt(h[0:rows(t), t, :], bank[0:rows(t), t, 0:D], hb[0:rows(t), t, :], ALU.add)
            link(i)
            normalise(1)
            link(nc.vector.memset(lg[:, TILES - 1, :], 0.0))
            dve.wait_ge(s_rps, 1)
            nc.vector.tensor_copy(lg[:, 0:4, :], bank[:, 5, 0:4 * E].rearrange("p (t e) -> p t e", e=E))
            link(nc.vector.tensor_copy(lg[0:B, 4, :], bank[0:B, 5, 4 * E:5 * E]))
            link(nc.vector.tensor_reduce(sm[:, 3, :], lg[:, :, :], AX.X, ALU.max))
            tt(lg[:, :, :], lg[:, :, :], sm[:, 3, :].unsqueeze(2).to_broadcast([P, TILES, E]),
               ALU.subtract).then_inc(s_rsub, 1)
            dve.wait_ge(s_rexp, 1)
            link(nc.vector.tensor_reduce(sm[:, 4, :], lg[:, :, :], AX.X, ALU.add))
            link(nc.vector.reciprocal(sm[:, 5, :], sm[:, 4, :]))
            link(tt(lg[:, :, :], lg[:, :, :], sm[:, 5, :].unsqueeze(2).to_broadcast([P, TILES, E]), ALU.mult))
            for t in range(TILES):
                i = nc.vector.max(top[:, t, :], lg[:, t, :])
            link(i)
            for t in range(TILES):
                i = nc.vector.max_index(topi[:, t, :], top[:, t, :], lg[:, t, :])
            link(i)
            link(nc.vector.tensor_copy(topf[:, :, :], topi[:, :, :]))
            for t in range(TILES):
                for k in range(TOPK):
                    i = ts(oh[:, k, t, :], const("iota"), topf[:, t, k:k + 1], None, ALU.is_equal)
            link(i)
            tt(ohs[:, :, :], oh[:, 0], oh[:, 1], ALU.add).then_inc(s_msk, 1)
            for t in range(TILES):
                ts(gate[:, t, :], oh[:, 0, t, :], top[:, t, 0:1], None, ALU.mult)
                i = ts(gate2[:, t, :], oh[:, 1, t, :], top[:, t, 1:2], None, ALU.mult)
            link(i)
            tt(gate[:, :, :], gate[:, :, :], gate2[:, :, :], ALU.add).then_inc(s_gate, 1)
            dve.wait_ge(s_rkps, 1)
            link(tt(filled[:, :, :], bank[:, 5, TILES * E:(TILES + 1) * E].unsqueeze(2).to_broadcast([P, E, TILES]),
                    const("fill").unsqueeze(1).to_broadcast([P, E, TILES]), ALU.is_gt))
            link(nc.vector.tensor_reduce(ntile[:, :], filled[:, :, :], AX.X, ALU.add))
            link(tt(upto[:, :, :], ntile[:, :].unsqueeze(1).to_broadcast([P, E, E]),
                    const("upto").rearrange("p (a b) -> p a b", a=E), ALU.mult))
            link(nc.vector.tensor_reduce(ends[:, :], upto[:, :, :], AX.X, ALU.add))
            link(tt(past[:, :, :], ends[0:1, :].unsqueeze(1).to_broadcast([1, MT, E]),
                    const("tile", 1).unsqueeze(2).to_broadcast([1, MT, E]), ALU.is_le))
            link(nc.vector.tensor_reduce(eidf[:, :], past[:, :, :], AX.X, ALU.add))
            ts(eid[:, :], eidf[:, :], E - 1.0, None, ALU.min).then_inc(s_eid, 1)
            link(tt(base[:, :], ends[:, :], ntile[:, :], ALU.subtract))
            link(stt(rank[:, :, :], base[:, :].unsqueeze(1).to_broadcast([P, TILES, E]), float(P),
                     bank[:, 5, 0:TILES * E].rearrange("p (t e) -> p t e", t=TILES), ALU.mult, ALU.add))
            for k in range(TOPK):
                i = tt(prod[:, k], oh[:, k], rank[:, :, :], ALU.mult)
            link(i)
            link(nc.vector.tensor_reduce(posf[:, :, :].rearrange("p k t -> p (k t)"),
                                         prod[:, :, :, :].rearrange("p k t e -> p (k t) e"), AX.X, ALU.add))
            nc.vector.tensor_copy(posi[:, :, :], posf[:, :, :]).then_inc(s_pos, 1)
            link(tt(h[:, :, :], h[:, :, :], xn[:, :, :], ALU.add))
            dve.wait_ge(s_gbps, 1)
            for t in range(TILES):
                i = tt(h[0:rows(t), t, :], bank[0:rows(t), t, 0:D], h[0:rows(t), t, :], ALU.add)
            i.then_inc(s_ye, 2)

            def turn_tokens(j, n):
                dve.wait_ge(s_gxps, j + 1)
                nc.vector.tensor_copy(xgT[n % 2], bank[0:KP, 4 + n % 2, 0:KD * P].rearrange(
                    "p (k n) -> p k n", k=KD)).then_inc(s_gx, 1)

            def expert_out(j, n, turn):
                dve.wait_ge(s_yps, j + 1)
                if turn is not None:
                    dve.wait_ge(s_yst[n], 16 * turn)
                nc.vector.tensor_copy(yt[n], bank[:, 6 + n % 2, 0:D]).then_inc(s_ye, 1)

            turn_tokens(0, 0)
            for j in range(NB):
                turn_tokens(j + 1, (j + 1) % NB)
                expert_out(j, j, None)
            with dve.Fori(1, MT // NB) as i:
                for n in range(NB):
                    turn_tokens(NB * i + n + 1, (n + 1) % NB)
                    expert_out(NB * i + n, n, i)
            for j in range(MT - MT % NB, MT):
                if j + 1 < MT:
                    turn_tokens(j + 1, (j + 1) % NB)
                expert_out(j, j % NB, j // NB)
            dve.wait_ge(s_scat, 16 * TOPK * TILES)
            dve.wait_ge(s_gath, 16 * TOPK * TILES)
            for k in range(TOPK):
                for t in range(TILES):
                    i = stt(h[0:rows(t), t, :], yg[0:rows(t), t, k, :], top[0:rows(t), t, k:k + 1], h[0:rows(t), t, :],
                            ALU.mult, ALU.add)
                link(i)
            dve.sem_inc(s_y, 1)
            normalise(2)
            dve.wait_ge(s_xt, 3 * TILES)
            nc.vector.tensor_copy(xc1, xT[:, :, NP:B * NT:NT].unsqueeze(3).to_broadcast([KP, KD, B, P])).then_inc(s1_xc, 1)
            for v in range(6):
                dve.wait_ge(s1_vps, v + 1)
                nc.vector.tensor_copy(v1[:, v, :] if v < 4 else vc1[:, v - 4, :], bank[:, 4 + v % 2, 0:D]).then_inc(s1_vev, 1)
            dve.wait_ge(s1_qcps, 1)
            for b in range(B):
                i = tt(QM1[:, :, b * NR:(b + 1) * NR],
                       const("mq1", KP).rearrange("p (c b r) -> p c b r", c=KD, b=B)[:, :, b, :],
                       bank[0:KP, 6, b:KD * B:B].unsqueeze(2).to_broadcast([KP, KD, NR]), ALU.mult)
            i.then_inc(s1_qm, 1)
            dve.wait_ge(s1_csc, 1)
            nc.vector.tensor_reduce(nmx[0:NR, 0:1], bank[0:NR, 7, 0:NT], AX.X, ALU.max, negate=True).then_inc(s1_cmx, 1)
            dve.wait_ge(s1_cexp, 1)
            link(nc.vector.reciprocal(gm[0:NR, 7:8], gm[0:NR, 6:7]))
            ts(PC1, PC1, gm[0:NR, 7:8], None, ALU.mult).then_inc(s1_cp, 1)
            dve.wait_ge(s1_ocps, 1)
            for b in range(B):
                i = tt(Oc1[:, b * KD * H:(b + 1) * KD * H], bank[0:KP, 6, b * KD * H:(b + 1) * KD * H],
                       const("mo1", KP), ALU.mult)
            link(i)
            for b in range(B):
                i = nc.vector.tensor_reduce(OT1[:, :, b * NT + NP:b * NT + NP + 1],
                                            Oc1[:, b * KD * H:(b + 1) * KD * H].rearrange("p (c r) -> p c r", c=KD),
                                            AX.X, ALU.add)
            i.then_inc(s1_otc, 1)
            dve.wait_ge(s1_kev, 2)
            with dve.Fori(0, 4) as t:
                dve.wait_ge(s1_qps, t + 1)
                nc.vector.tensor_copy(kTc, kT1[:, :, ds((t // 2) * NT, NT)])
                nc.vector.tensor_copy(vC, v1[:, ds((t // 2) * 2, 2), :])
                for c in range(KD):
                    i = tt(qz1[:, c * HPC:(c + 1) * HPC, :],
                           bank[0:KP, 7, c * P:(c + 1) * P].unsqueeze(1).to_broadcast([KP, HPC, P]),
                           const("mz1", KP).unsqueeze(2).to_broadcast([KP, HPC, P]), ALU.mult)
                i.then_inc(s1_qz, 1)

                def maximum(g):
                    dve.wait_ge(s1_dps, t * (H // 2) + g + 1)
                    nc.vector.tensor_reduce(nmx1[:, g % 2, :], bank[:, 2 * (g % 2):2 * (g % 2) + 2, 0:NT], AX.X, ALU.max,
                                            negate=True).then_inc(s1_mx, 1)
                maximum(0)
                maximum(1)
                for g in range(H // 2):
                    dve.wait_ge(s1_ptps, t * (H // 2) + g + 1)
                    nc.vector.tensor_copy(PT1[:, g % 2].rearrange("p h k n -> p (h k n)"), bank[:, 4 + g % 2, :]).then_inc(s1_pt, 1)
                    if g + 2 < H // 2:
                        maximum(g + 2)
                dve.wait_ge(s1_ops, t + 1)
                nc.vector.reciprocal(rr[:, :], rs[:, :])
                tt(OR1.rearrange("p (h e) -> p h e", h=H), PR1[:, :, NP:NT].to_broadcast([P, H, HD1]),
                   vc1[:, ds(t // 2, 1), :].rearrange("p a (h e) -> p (a h) e", h=H), ALU.mult).then_inc(s_rr, 1)
                dve.wait_ge(s_rr, 2 * t + 1 + 2 * H + 1)
                tt(OR1, OR1, bank[:, 6, 0:D], ALU.add).then_inc(s_rr, 1)
                dve.wait_ge(s_rr, 2 * t + 2 + 2 * H + 1)
                tt(O1.rearrange("p (h e) -> p h e", h=H), OR1.rearrange("p (h e) -> p h e", h=H),
                   rr[:, :].unsqueeze(2).to_broadcast([P, H, HD1]), ALU.mult).then_inc(s1_o, 1)
            for t in range(TILES):
                i = tt(hb[:, t, :], h[:, t, :], rowsb[:, 2, :], ALU.add)
            link(i)
            for t in range(TILES):
                dve.wait_ge(s1_prps, t + 1)
                i = tt(h[0:rows(t), t, :], bank[0:rows(t), t, 0:D], hb[0:rows(t), t, :], ALU.add)
            link(i)
            dve.wait_ge(s2_sln, 2)
            link(ts(sm[0:S, 12, 2:3], sm[0:S, 12, 1:2], EPS, None, ALU.max))
            link(nc.vector.reciprocal(sm[0:S, 12, 3:4], sm[0:S, 12, 2:3]))
            ts(slots, slots, sm[0:S, 12, 3:4], slscale, ALU.mult, ALU.mult).then_inc(s2_sl, 1)
            normalise(3, s2_u)
            dve.wait_ge(s2_sq, 1)
            ts(sm[:, 7, :], sm[:, 6, :], 1.0 / D, EPS, ALU.mult, ALU.add).then_inc(s2_ms, 1)
            dve.wait_ge(s2_rms, 1)
            link(nc.vector.reciprocal(sm[:, 8, :], sm[:, 7, :]))
            for t in range(TILES):
                i = stt(xr[:, t, :], xn[:, t, :], sm[:, 8, t:t + 1], rowsb[:, 3, :], ALU.mult, ALU.mult)
            i.then_inc(s2_xr, 1)
            dve.wait_ge(s2_xr, 1)
            dve.wait_ge(s2_nrm, 2)
            link(ts(sm[:, 10, :], sm[:, 10, :], EPS, None, ALU.max))
            link(nc.vector.reciprocal(sm[:, 11, :], sm[:, 10, :]))
            for t in range(TILES):
                ts(xn[:, t, :], xr[:, t, :], sm[:, 11, t:t + 1], None, ALU.mult).then_inc(s_xn, 1)
            link(nc.vector.memset(YM, 0.0))
            link(nc.vector.memset(lgc[:, TILES - 1, :], 0.0))
            link(nc.vector.memset(lgx, 0.0))
            nc.vector.memset(zero, 0.0).then_inc(s2_z, 1)
            dve.wait_ge(s2_lps, 1)
            nc.vector.tensor_reduce(nmx[0:S, 0:B], bank[0:S, 6:8, 0:NT], AX.X, ALU.max, negate=True).then_inc(s2_mx, 1)
            dve.wait_ge(s2_exp, 1)
            link(nc.vector.reciprocal(rr[0:S, 0:B], rs[0:S, 0:B]))
            for b in range(B):
                i = ts(Dm[:, b, :], Dm[:, b, :], rr[0:S, b:b + 1], None, ALU.mult)
            i.then_inc(s2_d, 1)
            dve.wait_ge(s2_dps, 1)
            nc.vector.tensor_copy(DT.rearrange("p a b -> p (a b)"), bank[:, 5, 0:4 * S])
            for b in range(B):
                i = ts(DTc[:, b, :], bank[0:B, 5, 4 * S:5 * S], cst[0:B, CST["eye2"][0] + b:CST["eye2"][0] + b + 1],
                       None, ALU.mult)
            i.then_inc(s2_dt, 1)
            dve.wait_ge(s2_yps, 1)
            for par in range(2):
                r = slice(64 * par, 64 * par + 64)
                for i8 in range(PAIRS // 4):
                    i = nc.vector.tensor_copy(
                        YM[r, 4 * i8:4 * i8 + 4, :, 4 * i8 + 2 * par:4 * i8 + 2 * par + 2],
                        bank[r, 6, 0:3 * B * PAIRS].rearrange("p (j b s) -> p s j b", j=3, b=B)[:, 4 * i8:4 * i8 + 4])
            link(i)
            def stage(g):
                nc.vector.tensor_copy(YMg.rearrange("p a j n -> p (a j n)"),
                                      YM[:, ds(RING * g, RING)].rearrange("p a j n -> p (a j n)")).then_inc(s2_yg, 1)
            stage(0)
            dve.wait_ge(s2_cps, 1)
            nc.vector.tensor_copy(lgc[:, 0:4, :], bank[:, 4, 0:4 * S].rearrange("p (t s) -> p t s", t=4))
            link(nc.vector.tensor_copy(lgc[0:B, 4, :], bank[0:B, 4, 4 * S:5 * S]))
            link(nc.vector.tensor_reduce(sm[:, 13, :], lgc, AX.X, ALU.max))
            tt(lgc, lgc, sm[:, 13, :].unsqueeze(2).to_broadcast([P, TILES, S]), ALU.subtract).then_inc(s2_csub, 1)
            dve.wait_ge(s2_cexp, 1)
            link(nc.vector.tensor_reduce(sm[:, 14, :], lgc, AX.X, ALU.add))
            link(nc.vector.reciprocal(sm[:, 15, :], sm[:, 14, :]))
            link(tt(lgc, lgc, sm[:, 15, :].unsqueeze(2).to_broadcast([P, TILES, S]), ALU.mult))

            def by_row(x, p, t, b):
                return x[0:p, t, :].rearrange("p (c i o b) -> p c i o b", c=4, o=2, b=B)[:, :, :, :, b]

            def by_slot(x, p, t):
                return x[0:p, t, :].rearrange("p (i c o) -> p c i o", c=4, o=2)
            for t in range(4):
                nc.vector.tensor_copy(by_row(lgx, P, t, t // 2), by_slot(lgc, P, t))
            for b in range(B):
                i = ts(by_row(lgx, B, 4, b), by_slot(lgc, B, 4), cst[0:B, CST["eye2"][0] + b:CST["eye2"][0] + b + 1],
                       None, ALU.mult)
            i.then_inc(s2_c, 1)
            with dve.Fori(1, PAIRS // RING) as g:
                dve.wait_ge(s_free[-1], g)
                stage(g)
            dve.wait_ge(s2_ctps, 1)
            nc.vector.tensor_copy(CT[:, 0:4, :].rearrange("p a b -> p (a b)"), bank[:, 4, :])
            nc.vector.tensor_copy(CT[:, 4, 0:B], bank[:, 5, 0:B]).then_inc(s2_ct, 1)
            dve.wait_ge(s_free[-1], PAIRS // RING)
            tt(hrow.rearrange("p (a n) -> p a n", a=2), bank[:, 0:2, 0:FF // 2], b1R.rearrange("p (a n) -> p a n", a=2),
               ALU.add).then_inc(s2_hb, 1)
            nc.vector.tensor_copy(Y2, b2R).then_inc(s2_y2, 1)
            with dve.Fori(0, PAIRS // RING) as g:
                dve.wait_ge(s2_y2, 4 * g + 1)
                nc.vector.tensor_copy(mcol, cst[:, ds(CST["m16"][0] + 4 * g, 4)]).then_inc(s2_mg, 1)
                dve.wait_ge(s2_mg, g + 1)
                for n in range(4):
                    if n % 2:
                        dve.wait_ge(s_free[n // 2], g + PAIRS // RING + 1)
                    else:
                        dve.wait_ge(s2_f2, 2 * g + n // 2 + 1)
                    if n:
                        dve.wait_ge(s2_y2, 4 * g + n + 1)
                    stt(Y2, bank[:, 2 + n, 0:D], mcol[:, n:n + 1], Y2, ALU.mult, ALU.add).then_inc(s2_y2, 1)
            for t in range(TILES):
                dve.wait_ge(s2_ops, t + 1)
                tt(h[0:rows(t), t, :], bank[0:rows(t), t if t else 6, 0:D], h[0:rows(t), t, :], ALU.add).then_inc(s_final, 1)


def kernel(**inputs):
    import concourse.bacc as bacc
    from concourse.bass_utils import run_bass_kernel_spmd

    x = {k: np.asarray(v) for k, v in inputs.items()}
    patch = D // 3
    side = int(patch ** 0.5)
    xp = x["x"].reshape(B, 3, GRID, side, GRID, side).transpose(1, 3, 5, 0, 2, 4).reshape(D, B, NP)[:, :, ::-1]
    chunk = lambda m: m.reshape(KD, KP, -1).transpose(1, 0, 2)
    cst = np.zeros((P, CST_W), np.float32)

    def put(name, v):
        lo, hi = CST[name]
        cst[:v.shape[0], lo:hi] = v.reshape(v.shape[0], -1)

    p, p1 = np.arange(P), np.arange(KP)
    put("ident", np.eye(P))
    m = np.zeros((P, C0, B, NR))
    mo = np.zeros((P, C0, H))
    for c in range(C0):
        for b in range(B):
            m[p, c, b, b * H + 2 * c + p // HD0] = 1
        mo[p, c, 2 * c + p // HD0] = 1
    put("mq0", m)
    put("mo0", mo)
    m = np.zeros((KP, KD, B, NR))
    mo = np.zeros((KP, KD, H))
    for c in range(KD):
        for b in range(B):
            m[p1, c, b, b * H + HPC * c + p1 // HD1] = HD1 ** -0.5
        mo[p1, c, HPC * c + p1 // HD1] = 1
    put("mq1", m)
    put("mo1", mo)
    m = np.zeros((KP, HPC))
    m[p1, p1 // HD1] = HD1 ** -0.5
    put("mz1", m)
    put("nb", -(np.eye(NR) + np.kron(np.eye(B), np.ones((H, H))) / H))
    put("iota", np.tile(np.arange(E), (P, 1)))
    put("eye2", np.eye(B))
    quarter, i8, odd = p // 32, p % 32 // 4, p % 4 // 2
    slot_of_row = 8 * i8 + 2 * quarter + odd
    m = np.zeros((P, 16))
    m[p, 2 * i8 + odd] = 1
    put("m16", m)
    put("below", p[:, None] < p[None, :])
    put("ones", np.ones((P, P)))
    put("fill", np.tile(P * np.arange(TILES), (P, 1)))
    put("upto", np.tile((np.arange(E)[None, :] <= np.arange(E)[:, None]).reshape(-1), (P, 1)))
    put("tile", np.tile(np.arange(MT), (P, 1)))
    bf = mybir.dt.np(BF16)
    cstb = np.zeros((P, CSTB_W), np.float32)
    cstb[:, 0:P] = np.eye(P)
    cstb[p, CSTB["bigd"][0] + P + p] = -BIG
    cstb[:, CSTB["bigc"][0] + NP] = -BIG
    arrays = {
        "xp": chunk(xp.reshape(D, B * NP)), "wt": chunk(x["L0_tok_w"].reshape(D, D).T),
        "cst": cst, "cstb": cstb.astype(bf),
        "tok_b": x["L0_tok_b"], "b_out": x["L0_attn_b_out"], "b_proj": x["L1_attn_b_proj"],
        "norm_w": x["L1_ffn_norm_weight"], "scale0": x["L0_attn_scale"],
        "cls": x["cls_tok"].reshape(D), "wqkv0": x["L0_attn_w_qkv"], "wo0": x["L0_attn_w_out"],
        "wqkv1": chunk(x["L1_attn_w_qkv"].T), "wp1": chunk(x["L1_attn_w_proj"].T),
        "slots": x["L1_ffn_slots"], "slot_scale": x["L1_ffn_scale"].reshape(S, 1),
        "fc1": x["L1_ffn_fc1_weight"], "fc2": x["L1_ffn_fc2_weight"],
        "b1R": x["L1_ffn_fc1_bias"][slot_of_row], "b2R": x["L1_ffn_fc2_bias"][slot_of_row],
        "wr": chunk(x["L0_ffn_Wr"].T), "w1e": x["L0_ffn_W1"], "w2e": x["L0_ffn_W2"], "b2e": x["L0_ffn_b2"],
        "b1e": x["L0_ffn_b1"].reshape(E, MF, P).transpose(0, 2, 1),
    }
    nc = bacc.Bacc("TRN2", target_bir_lowering=False, num_devices=1)
    arrays = {k: np.ascontiguousarray(v) for k, v in arrays.items()}
    aps = {k: nc.dram_tensor(f"in_{k}", v.shape, mybir.dt.from_np(v.dtype), kind="ExternalInput").ap()
           for k, v in arrays.items()}
    aps["out"] = nc.dram_tensor("out", (B * NT, D), F32, kind="ExternalOutput").ap()
    vit_tower(nc, aps)
    r = run_bass_kernel_spmd(nc, [{f"in_{k}": v for k, v in arrays.items()}], core_ids=[0])
    got = r.results[0]["out"]
    patches = got[:B * NP].reshape(B, NP, D)[:, ::-1]
    return np.ascontiguousarray(np.concatenate([got[B * NP:].reshape(B, 1, D), patches], axis=1))
```
